# Optimizing a Trainium2 kernel written in Bass

```python
import numpy as np
import jax
import jax.numpy as jnp

def _softmax(x, axis=-1):
    return jax.nn.softmax(x, axis=axis)

def _gelu(x):
    return jax.nn.gelu(x, approximate=True)

def _silu(x):
    return jax.nn.silu(x)

def _sigmoid(x):
    return jax.nn.sigmoid(x)

def _layernorm(x, axis=-1, eps=1e-05):
    m = jnp.mean(x, axis=axis, keepdims=True)
    v = jnp.var(x, axis=axis, keepdims=True)
    return (x - m) / jnp.sqrt(v + eps)

def _scatter_add(tgt, idx, src, axis=0):
    return tgt.at[idx].add(src)

def _segment_sum(src, seg, n):
    return jax.ops.segment_sum(src, seg, n)
kernel_name = 'mk_decoder_preln_d2_seqx_r8_780c8b'

def setup_inputs(seed: int=0):
    np.random.seed(seed)
    _w = jnp.asarray

    def _rec_inputs():
        import jax
        import jax.numpy as jnp
        _rk = jax.random.key(seed)
        x = 7.22e-05 + 1 * jax.random.normal(jax.random.fold_in(_rk, 1), (64, 64, 128), jnp.float32)
        _lenS = 64 - jax.random.randint(jax.random.fold_in(_rk, 7), (64,), 0, max(1, 64 // 4) + 1, jnp.int32)
        _lenS2 = 64 - jax.random.randint(jax.random.fold_in(_rk, 8), (64,), 0, max(1, 64 // 4) + 1, jnp.int32)
        _ctx_1024P = jax.random.normal(jax.random.fold_in(_rk, 11), (64, 16, 128), jnp.float32)
        _ctx_1024c = jax.random.dirichlet(jax.random.fold_in(_rk, 511), 0.3 * jnp.ones((16,), jnp.float32), (64, 64))
        _ctx_1024t = jnp.einsum('bsk,bkd->bsd', _ctx_1024c, _ctx_1024P)
        _ctx_1024t = _ctx_1024t * jax.lax.rsqrt(jnp.mean(jnp.square(_ctx_1024t)) + 1e-12) * 0.953939
        ctx_1024 = 4.13588e-05 + 0.999923 * (_ctx_1024t + 0.3 * jax.random.normal(jax.random.fold_in(_rk, 611), (64, 64, 128), jnp.float32))
        _validS = jnp.arange(64)[None, :] < _lenS[:, None]
        _validS2 = jnp.arange(64)[None, :] < _lenS2[:, None]
        _causal = jnp.tril(jnp.ones((64, 64), dtype=bool))
        mask_Bx1x1xS2_ff0 = jnp.where(jnp.ones((64, 1, 1, 64), dtype=bool), 0.0, -1000000000.0).astype(jnp.float32)
        return (x, ctx_1024, mask_Bx1x1xS2_ff0)
    x, ctx_1024, mask_Bx1x1xS2_ff0 = _rec_inputs()

    def _L0_attn_setup():
        import jax, jax.numpy as jnp
        import numpy as np
        B, T, C, H = (4, 128, 128, 16)
        D = C // H

        def _expmap0_split(u):
            mink = -u[..., :1] ** 2 + jnp.sum(u[..., 1:] ** 2, axis=-1, keepdims=True)
            nomin = jnp.sqrt(jnp.maximum(mink, 1e-08))
            time = jnp.cosh(nomin)
            space = jnp.sinh(nomin) * u[..., 1:] / nomin
            return (time, space)
        key = jax.random.key(seed)
        ks = jax.random.split(key, 6)
        s = 1.0 / np.sqrt(C)
        return {'x': jax.random.normal(ks[0], (B, T, C), jnp.float32), 'W_qkv': jax.random.normal(ks[1], (C, 3 * C), jnp.float32) * s, 'b_qkv': jnp.zeros((3 * C,), jnp.float32), 'W_out': jax.random.normal(ks[2], (C, C), jnp.float32) * s, 'b_out': jnp.zeros((C,), jnp.float32), 'w_sur': jax.random.normal(ks[3], (C,), jnp.float32) * s, 'b_sur': jnp.zeros((), jnp.float32), 'threshold': jnp.float32(0.5)}
    _L0_attn_all = _L0_attn_setup()
    _L0_attn_in = {k: v for k, v in _L0_attn_all.items() if k in ('W_qkv', 'b_qkv', 'W_out', 'b_out', 'w_sur', 'b_sur', 'threshold')}
    del _L0_attn_all

    def _L0_xattn_setup():
        import jax, jax.numpy as jnp
        import numpy as np
        B, T, S, H, NH, F = (16, 64, 64, 128, 16, 512)
        HD = H // NH

        def _mha(x, bias, mem, wq, bq, wk, bk, wv, bv, wo, bo):
            b, t, h = x.shape
            q = (x @ wq + bq) * HD ** (-0.5)
            k = mem @ wk + bk
            v = mem @ wv + bv
            split = lambda z: z.reshape(z.shape[0], z.shape[1], NH, HD).transpose(0, 2, 1, 3)
            logits = jnp.einsum('bhqd,bhkd->bhqk', split(q), split(k)) + bias
            w = jax.nn.softmax(logits, axis=-1)
            o = jnp.einsum('bhqk,bhkd->bhqd', w, split(v))
            o = o.transpose(0, 2, 1, 3).reshape(b, t, h)
            return o @ wo + bo

        def _lstm(inp, w, b):
            bsz = inp.shape[0]

            def step(carry, xt):
                c, hdd = carry
                g = jnp.concatenate([xt, hdd], axis=-1) @ w + b
                i, j, f, o = jnp.split(g, 4, axis=-1)
                new_c = jax.nn.sigmoid(f) * c + jax.nn.sigmoid(i) * jnp.tanh(j)
                new_h = jax.nn.sigmoid(o) * jnp.tanh(new_c)
                return ((new_c, new_h), new_h)
            init = (jnp.zeros((bsz, H), inp.dtype), jnp.zeros((bsz, H), inp.dtype))
            _, hs = jax.lax.scan(step, init, inp.transpose(1, 0, 2))
            return hs.transpose(1, 0, 2)
        key = jax.random.key(seed)
        ks = jax.random.split(key, 16)
        d = {}
        d['x'] = jax.random.normal(ks[0], (B, T, H), jnp.float32)
        d['memory'] = jax.random.normal(ks[1], (B, S, H), jnp.float32)
        d['src_bias'] = jnp.zeros((B, 1, 1, S), jnp.float32)
        causal = jnp.triu(jnp.full((T, T), -1000000000.0, jnp.float32), k=1)
        d['tgt_bias'] = causal[None, None]
        sc = 0.02
        names = ['src_wq', 'src_wk', 'src_wv', 'src_wo', 'tgt_wq', 'tgt_wk', 'tgt_wv', 'tgt_wo']
        for i, n in enumerate(names):
            d[n] = jax.random.normal(ks[2 + i], (H, H), jnp.float32) * sc
            d[n.replace('w', 'b')] = jnp.zeros((H,), jnp.float32)
        d['lstm_w'] = jax.random.normal(ks[10], (3 * H, 4 * H), jnp.float32) * sc
        d['lstm_b'] = jnp.zeros((4 * H,), jnp.float32)
        d['ffn_w1'] = jax.random.normal(ks[11], (H, F), jnp.float32) * sc
        d['ffn_b1'] = jnp.zeros((F,), jnp.float32)
        d['ffn_w2'] = jax.random.normal(ks[12], (F, H), jnp.float32) * sc
        d['ffn_b2'] = jnp.zeros((H,), jnp.float32)
        return d
    _L0_xattn_all = _L0_xattn_setup()
    _L0_xattn_in = {k: v for k, v in _L0_xattn_all.items() if k in ('tgt_bias', 'src_wq', 'src_bq', 'src_wk', 'src_bk', 'src_wv', 'src_bv', 'src_wo', 'src_bo', 'tgt_wq', 'tgt_bq', 'tgt_wk', 'tgt_bk', 'tgt_wv', 'tgt_bv', 'tgt_wo', 'tgt_bo', 'lstm_w', 'lstm_b', 'ffn_w1', 'ffn_b1', 'ffn_w2', 'ffn_b2')}
    del _L0_xattn_all

    def _L0_ffn_setup():
        import jax, jax.numpy as jnp
        import numpy as np
        B, T, E, C, H, G = (2, 256, 8, 128, 256, 16)
        key = jax.random.key(seed)
        ks = jax.random.split(key, 7)
        return {'hidden_states': jax.random.normal(ks[0], (B, T, C), jnp.float32), 'w_red': jax.random.normal(ks[1], (C, G), jnp.float32) * 0.02, 'wg': jax.random.normal(ks[2], (E, G), jnp.float32), 'W1': jax.random.normal(ks[3], (E, C, H), jnp.float32) * 0.02, 'b1': jax.random.normal(ks[4], (E, H), jnp.float32) * 0.02, 'W2': jax.random.normal(ks[5], (E, H, C), jnp.float32) * 0.02, 'b2': jax.random.normal(ks[6], (E, C), jnp.float32) * 0.02}
    _L0_ffn_all = _L0_ffn_setup()
    _L0_ffn_in = {k: v for k, v in _L0_ffn_all.items() if k in ('w_red', 'wg', 'W1', 'b1', 'W2', 'b2')}
    del _L0_ffn_all

    def _L1_attn_setup():
        import jax, jax.numpy as jnp
        import numpy as np
        B, L, DM, H, HD, K = (4, 256, 128, 16, 64, 64)
        BASE_LR = 1.0
        EPS = 1e-06

        def _ttt_forward(hidden_states, wq, wk, wv, wo, W1, b1, theta, theta_bias, alpha, gamma, beta):
            Bs, Ls, _ = hidden_states.shape
            n_chunks = Ls // K

            def proj(w):
                return (hidden_states @ w).reshape(Bs, Ls, H, HD).transpose(0, 2, 1, 3)
            xq, xk, xv = (proj(wq), proj(wk), proj(wv))

            def to_chunks(x):
                return x.reshape(Bs, H, n_chunks, K, HD).transpose(2, 0, 1, 3, 4)
            cq, ck, cv = (to_chunks(xq), to_chunks(xk), to_chunks(xv))
            token_eta = jnp.clip(1.0 / jnp.arange(1, K + 1, dtype=jnp.float32) + alpha, 0.0)[None, None, :, None]
            g = gamma[None]
            be = beta[None]
            tb = theta_bias.reshape(1, H, 1, 1)
            W0 = jnp.broadcast_to(W1[None], (Bs, H, HD, HD))
            b0 = jnp.broadcast_to(b1[None], (Bs, H, 1, HD))

            def step(carry, inp):
                W, bb = carry
                xq_c, xk_c, xv_c = inp
                lr = jax.nn.sigmoid(jnp.einsum('bhkc,hcd->bhkd', xk_c, theta) + tb)
                eta = token_eta * (BASE_LR * lr / HD)
                Z1 = xk_c @ W + bb
                mu = Z1.mean(-1, keepdims=True)
                std = jnp.sqrt(Z1.var(-1, keepdims=True) + EPS)
                x_hat = (Z1 - mu) / std
                y = g * x_hat + be
                grad_output = y - (xv_c - xk_c)
                gxh = grad_output * g
                grad_x = (HD * gxh - gxh.sum(-1, keepdims=True) - x_hat * (gxh * x_hat).sum(-1, keepdims=True)) / (HD * std)
                dW = jnp.einsum('bhkc,bhkd->bhcd', eta * xk_c, grad_x)
                db = (eta * grad_x).sum(-2, keepdims=True)
                Wn, bn = (W - dW, bb - db)
                Zq = xq_c @ Wn + bn
                mu2 = Zq.mean(-1, keepdims=True)
                std2 = jnp.sqrt(Zq.var(-1, keepdims=True) + EPS)
                out = xq_c + g * ((Zq - mu2) / std2) + be
                return ((Wn, bn), out)
            _, outs = jax.lax.scan(step, (W0, b0), (cq, ck, cv))
            out = outs.transpose(1, 2, 0, 3, 4).reshape(Bs, H, Ls, HD)
            out = out.transpose(0, 2, 1, 3).reshape(Bs, Ls, H * HD)
            return out @ wo
        key = jax.random.key(seed)
        ks = jax.random.split(key, 8)
        s = 0.02
        return {'hidden_states': jax.random.normal(ks[0], (B, L, DM), jnp.float32), 'wq': jax.random.normal(ks[1], (DM, H * HD), jnp.float32) * s, 'wk': jax.random.normal(ks[2], (DM, H * HD), jnp.float32) * s, 'wv': jax.random.normal(ks[3], (DM, H * HD), jnp.float32) * s, 'wo': jax.random.normal(ks[4], (H * HD, DM), jnp.float32) * s, 'W1': jax.random.normal(ks[5], (H, HD, HD), jnp.float32) * s, 'b1': jnp.zeros((H, 1, HD), jnp.float32), 'theta': jax.random.normal(ks[6], (H, HD, 1), jnp.float32) * s, 'theta_bias': jnp.zeros((H, 1, 1), jnp.float32), 'alpha': jnp.zeros((K,), jnp.float32), 'gamma': jnp.ones((H, 1, HD), jnp.float32), 'beta': jnp.zeros((H, 1, HD), jnp.float32)}
    _L1_attn_all = _L1_attn_setup()
    _L1_attn_in = {k: v for k, v in _L1_attn_all.items() if k in ('wq', 'wk', 'wv', 'wo', 'W1', 'b1', 'theta', 'theta_bias', 'alpha', 'gamma', 'beta')}
    del _L1_attn_all

    def _L1_xattn_setup():
        import jax, jax.numpy as jnp
        import numpy as np
        B, S, D, DFF = (4, 256, 128, 512)
        EPS = 1e-05

        def layernorm(x, gamma, beta):
            mu = jnp.mean(x, axis=-1, keepdims=True)
            var = jnp.var(x, axis=-1, keepdims=True)
            return (x - mu) * jax.lax.rsqrt(var + EPS) * gamma + beta

        def attention(Q, K, V, causal):
            d_k = Q.shape[-1]
            scores = jnp.einsum('bqd,bkd->bqk', Q, K) / jnp.sqrt(jnp.asarray(d_k, Q.dtype))
            if causal:
                q_len, k_len = (scores.shape[-2], scores.shape[-1])
                mask = jnp.tril(jnp.ones((q_len, k_len), dtype=bool))
                scores = jnp.where(mask[None], scores, jnp.asarray(-jnp.inf, scores.dtype))
            w = jax.nn.softmax(scores, axis=-1)
            return jnp.einsum('bqk,bkd->bqd', w, V)
        key = jax.random.key(seed)
        ks = jax.random.split(key, 12)
        sd = 0.02
        return {'y': jax.random.normal(ks[0], (B, S, D), jnp.float32), 'Z': jax.random.normal(ks[1], (B, S, D), jnp.float32), 'w1': jax.random.normal(ks[2], (D, DFF), jnp.float32) * sd, 'b1': jnp.zeros((DFF,), jnp.float32), 'w2': jax.random.normal(ks[3], (DFF, D), jnp.float32) * sd, 'b2': jnp.zeros((D,), jnp.float32), 'g1': jnp.ones((D,), jnp.float32), 'beta1': jnp.zeros((D,), jnp.float32), 'g2': jnp.ones((D,), jnp.float32), 'beta2': jnp.zeros((D,), jnp.float32), 'g3': jnp.ones((D,), jnp.float32), 'beta3': jnp.zeros((D,), jnp.float32)}
    _L1_xattn_all = _L1_xattn_setup()
    _L1_xattn_in = {k: v for k, v in _L1_xattn_all.items() if k in ('w1', 'b1', 'w2', 'b2', 'g1', 'beta1', 'g2', 'beta2', 'g3', 'beta3')}
    del _L1_xattn_all

    def _L1_ffn_setup():
        import jax, jax.numpy as jnp
        import numpy as np
        TOP_K = 2
        N_EXPERTS = 8
        key = jax.random.key(seed)
        k_x, k_g, k_w1, k_w2 = jax.random.split(key, 4)
        B, S, d_in, d_hid, d_out, E = (8, 256, 128, 256, 128, N_EXPERTS)
        s_gate = float(np.sqrt(6.0 / (d_in + E)))
        s_w1 = float(np.sqrt(6.0 / (d_in + d_hid)))
        s_w2 = float(np.sqrt(6.0 / (d_hid + d_out)))
        x = jax.random.normal(k_x, (B, S, d_in), dtype=jnp.float32)
        gate_W = jax.random.uniform(k_g, (d_in, E), jnp.float32, -s_gate, s_gate)
        W1 = jax.random.uniform(k_w1, (E, d_in, d_hid), jnp.float32, -s_w1, s_w1)
        b1 = jnp.zeros((E, d_hid), jnp.float32)
        W2 = jax.random.uniform(k_w2, (E, d_hid, d_out), jnp.float32, -s_w2, s_w2)
        b2 = jnp.zeros((E, d_out), jnp.float32)
        return {'x': x, 'gate_W': gate_W, 'W1': W1, 'b1': b1, 'W2': W2, 'b2': b2}
    _L1_ffn_all = _L1_ffn_setup()
    _L1_ffn_in = {k: v for k, v in _L1_ffn_all.items() if k in ('gate_W', 'W1', 'b1', 'W2', 'b2')}
    del _L1_ffn_all
    return {'x': x, 'ctx_1024': ctx_1024, 'mask_Bx1x1xS2_ff0': mask_Bx1x1xS2_ff0, 'L0_attn_W_qkv': _L0_attn_in['W_qkv'], 'L0_attn_b_qkv': _L0_attn_in['b_qkv'], 'L0_attn_W_out': _L0_attn_in['W_out'], 'L0_attn_b_out': _L0_attn_in['b_out'], 'L0_attn_w_sur': _L0_attn_in['w_sur'], 'L0_attn_b_sur': _L0_attn_in['b_sur'], 'L0_attn_threshold': _L0_attn_in['threshold'], 'L0_xattn_tgt_bias': _L0_xattn_in['tgt_bias'], 'L0_xattn_src_wq': _L0_xattn_in['src_wq'], 'L0_xattn_src_bq': _L0_xattn_in['src_bq'], 'L0_xattn_src_wk': _L0_xattn_in['src_wk'], 'L0_xattn_src_bk': _L0_xattn_in['src_bk'], 'L0_xattn_src_wv': _L0_xattn_in['src_wv'], 'L0_xattn_src_bv': _L0_xattn_in['src_bv'], 'L0_xattn_src_wo': _L0_xattn_in['src_wo'], 'L0_xattn_src_bo': _L0_xattn_in['src_bo'], 'L0_xattn_tgt_wq': _L0_xattn_in['tgt_wq'], 'L0_xattn_tgt_bq': _L0_xattn_in['tgt_bq'], 'L0_xattn_tgt_wk': _L0_xattn_in['tgt_wk'], 'L0_xattn_tgt_bk': _L0_xattn_in['tgt_bk'], 'L0_xattn_tgt_wv': _L0_xattn_in['tgt_wv'], 'L0_xattn_tgt_bv': _L0_xattn_in['tgt_bv'], 'L0_xattn_tgt_wo': _L0_xattn_in['tgt_wo'], 'L0_xattn_tgt_bo': _L0_xattn_in['tgt_bo'], 'L0_xattn_lstm_w': _L0_xattn_in['lstm_w'], 'L0_xattn_lstm_b': _L0_xattn_in['lstm_b'], 'L0_xattn_ffn_w1': _L0_xattn_in['ffn_w1'], 'L0_xattn_ffn_b1': _L0_xattn_in['ffn_b1'], 'L0_xattn_ffn_w2': _L0_xattn_in['ffn_w2'], 'L0_xattn_ffn_b2': _L0_xattn_in['ffn_b2'], 'L0_ffn_w_red': _L0_ffn_in['w_red'], 'L0_ffn_wg': _L0_ffn_in['wg'], 'L0_ffn_W1': _L0_ffn_in['W1'], 'L0_ffn_b1': _L0_ffn_in['b1'], 'L0_ffn_W2': _L0_ffn_in['W2'], 'L0_ffn_b2': _L0_ffn_in['b2'], 'L1_attn_wq': _L1_attn_in['wq'], 'L1_attn_wk': _L1_attn_in['wk'], 'L1_attn_wv': _L1_attn_in['wv'], 'L1_attn_wo': _L1_attn_in['wo'], 'L1_attn_W1': _L1_attn_in['W1'], 'L1_attn_b1': _L1_attn_in['b1'], 'L1_attn_theta': _L1_attn_in['theta'], 'L1_attn_theta_bias': _L1_attn_in['theta_bias'], 'L1_attn_alpha': _L1_attn_in['alpha'], 'L1_attn_gamma': _L1_attn_in['gamma'], 'L1_attn_beta': _L1_attn_in['beta'], 'L1_xattn_w1': _L1_xattn_in['w1'], 'L1_xattn_b1': _L1_xattn_in['b1'], 'L1_xattn_w2': _L1_xattn_in['w2'], 'L1_xattn_b2': _L1_xattn_in['b2'], 'L1_xattn_g1': _L1_xattn_in['g1'], 'L1_xattn_beta1': _L1_xattn_in['beta1'], 'L1_xattn_g2': _L1_xattn_in['g2'], 'L1_xattn_beta2': _L1_xattn_in['beta2'], 'L1_xattn_g3': _L1_xattn_in['g3'], 'L1_xattn_beta3': _L1_xattn_in['beta3'], 'L1_ffn_gate_W': _L1_ffn_in['gate_W'], 'L1_ffn_W1': _L1_ffn_in['W1'], 'L1_ffn_b1': _L1_ffn_in['b1'], 'L1_ffn_W2': _L1_ffn_in['W2'], 'L1_ffn_b2': _L1_ffn_in['b2']}

def reference(x, ctx_1024, mask_Bx1x1xS2_ff0, L0_attn_W_qkv, L0_attn_b_qkv, L0_attn_W_out, L0_attn_b_out, L0_attn_w_sur, L0_attn_b_sur, L0_attn_threshold, L0_xattn_tgt_bias, L0_xattn_src_wq, L0_xattn_src_bq, L0_xattn_src_wk, L0_xattn_src_bk, L0_xattn_src_wv, L0_xattn_src_bv, L0_xattn_src_wo, L0_xattn_src_bo, L0_xattn_tgt_wq, L0_xattn_tgt_bq, L0_xattn_tgt_wk, L0_xattn_tgt_bk, L0_xattn_tgt_wv, L0_xattn_tgt_bv, L0_xattn_tgt_wo, L0_xattn_tgt_bo, L0_xattn_lstm_w, L0_xattn_lstm_b, L0_xattn_ffn_w1, L0_xattn_ffn_b1, L0_xattn_ffn_w2, L0_xattn_ffn_b2, L0_ffn_w_red, L0_ffn_wg, L0_ffn_W1, L0_ffn_b1, L0_ffn_W2, L0_ffn_b2, L1_attn_wq, L1_attn_wk, L1_attn_wv, L1_attn_wo, L1_attn_W1, L1_attn_b1, L1_attn_theta, L1_attn_theta_bias, L1_attn_alpha, L1_attn_gamma, L1_attn_beta, L1_xattn_w1, L1_xattn_b1, L1_xattn_w2, L1_xattn_b2, L1_xattn_g1, L1_xattn_beta1, L1_xattn_g2, L1_xattn_beta2, L1_xattn_g3, L1_xattn_beta3, L1_ffn_gate_W, L1_ffn_W1, L1_ffn_b1, L1_ffn_W2, L1_ffn_b2):
    import jax
    import jax.numpy as jnp

    def _L0_attn_ref(x, W_qkv, b_qkv, W_out, b_out, w_sur, b_sur, threshold):
        import jax, jax.numpy as jnp
        import numpy as np
        B, T, C, H = (4, 128, 128, 16)
        D = C // H

        def _expmap0_split(u):
            mink = -u[..., :1] ** 2 + jnp.sum(u[..., 1:] ** 2, axis=-1, keepdims=True)
            nomin = jnp.sqrt(jnp.maximum(mink, 1e-08))
            time = jnp.cosh(nomin)
            space = jnp.sinh(nomin) * u[..., 1:] / nomin
            return (time, space)
        Bx, Tx, Cx = x.shape
        importance = jax.nn.sigmoid(jnp.einsum('btc,c->bt', x, w_sur) + b_sur)
        spikes = (importance > threshold).astype(x.dtype)
        spike_mask = spikes[:, None, :, None]
        qkv = x @ W_qkv + b_qkv
        qkv = qkv.reshape(Bx, Tx, 3, H, D).transpose(2, 0, 3, 1, 4)
        q, k, v = (qkv[0], qkv[1], qkv[2])
        tq, sq = _expmap0_split(q)
        tk, sk = _expmap0_split(k)
        neg_inner = jnp.einsum('bhie,bhje->bhij', tq, tk) - jnp.einsum('bhid,bhjd->bhij', sq, sk)
        dist = jnp.arccosh(jnp.maximum(neg_inner, 1.0 + 1e-07))
        scores = -dist ** 2 / np.sqrt(D)
        causal = jnp.tril(jnp.ones((Tx, Tx), dtype=bool))
        scores = jnp.where(causal[None, None], scores, -jnp.inf)
        attn = jax.nn.softmax(scores, axis=-1) * spike_mask
        y = jnp.einsum('bhij,bhjd->bhid', attn, v)
        y = y.transpose(0, 2, 1, 3).reshape(Bx, Tx, Cx)
        return y @ W_out + b_out

    def _L0_xattn_ref(x, memory, src_bias, tgt_bias, src_wq, src_bq, src_wk, src_bk, src_wv, src_bv, src_wo, src_bo, tgt_wq, tgt_bq, tgt_wk, tgt_bk, tgt_wv, tgt_bv, tgt_wo, tgt_bo, lstm_w, lstm_b, ffn_w1, ffn_b1, ffn_w2, ffn_b2):
        import jax, jax.numpy as jnp
        import numpy as np
        B, T, S, H, NH, F = (16, 64, 64, 128, 16, 512)
        HD = H // NH

        def _mha(x, bias, mem, wq, bq, wk, bk, wv, bv, wo, bo):
            b, t, h = x.shape
            q = (x @ wq + bq) * HD ** (-0.5)
            k = mem @ wk + bk
            v = mem @ wv + bv
            split = lambda z: z.reshape(z.shape[0], z.shape[1], NH, HD).transpose(0, 2, 1, 3)
            logits = jnp.einsum('bhqd,bhkd->bhqk', split(q), split(k)) + bias
            w = jax.nn.softmax(logits, axis=-1)
            o = jnp.einsum('bhqk,bhkd->bhqd', w, split(v))
            o = o.transpose(0, 2, 1, 3).reshape(b, t, h)
            return o @ wo + bo

        def _lstm(inp, w, b):
            bsz = inp.shape[0]

            def step(carry, xt):
                c, hdd = carry
                g = jnp.concatenate([xt, hdd], axis=-1) @ w + b
                i, j, f, o = jnp.split(g, 4, axis=-1)
                new_c = jax.nn.sigmoid(f) * c + jax.nn.sigmoid(i) * jnp.tanh(j)
                new_h = jax.nn.sigmoid(o) * jnp.tanh(new_c)
                return ((new_c, new_h), new_h)
            init = (jnp.zeros((bsz, H), inp.dtype), jnp.zeros((bsz, H), inp.dtype))
            _, hs = jax.lax.scan(step, init, inp.transpose(1, 0, 2))
            return hs.transpose(1, 0, 2)
        c_src = _mha(x, src_bias, memory, src_wq, src_bq, src_wk, src_bk, src_wv, src_bv, src_wo, src_bo)
        c_tgt = _mha(x, tgt_bias, x, tgt_wq, tgt_bq, tgt_wk, tgt_bk, tgt_wv, tgt_bv, tgt_wo, tgt_bo)
        c = c_src + c_tgt
        hiddens = _lstm(jnp.concatenate([x, c], axis=-1), lstm_w, lstm_b)
        hiddens = jax.nn.relu(hiddens @ ffn_w1 + ffn_b1) @ ffn_w2 + ffn_b2
        return hiddens

    def _L0_ffn_ref(hidden_states, w_red, wg, W1, b1, W2, b2):
        import jax, jax.numpy as jnp
        import numpy as np
        B, T, E, C, H, G = (2, 256, 8, 128, 256, 16)
        b, t, c = hidden_states.shape
        x = hidden_states.reshape(-1, c)
        x_red = x @ w_red
        wg_n = wg / jnp.maximum(jnp.linalg.norm(wg, axis=1, keepdims=True), 0.0001)
        logits = x_red @ wg_n.T
        gates = jax.nn.softmax(logits, axis=1)
        scores = jnp.max(gates, axis=1)
        idx = jnp.argmax(gates, axis=1)
        h = jnp.einsum('nc,ech->neh', x, W1) + b1[None]
        h = jnp.take_along_axis(h, idx[:, None, None], axis=1)[:, 0, :]
        h = jax.nn.gelu(h, approximate=False)
        o = jnp.einsum('nh,ehc->nec', h, W2) + b2[None]
        o = jnp.take_along_axis(o, idx[:, None, None], axis=1)[:, 0, :]
        o = o * scores[:, None]
        return o.reshape(b, t, c)

    def _L1_attn_ref(hidden_states, wq, wk, wv, wo, W1, b1, theta, theta_bias, alpha, gamma, beta):
        import jax, jax.numpy as jnp
        import numpy as np
        B, L, DM, H, HD, K = (4, 256, 128, 16, 64, 64)
        BASE_LR = 1.0
        EPS = 1e-06

        def _ttt_forward(hidden_states, wq, wk, wv, wo, W1, b1, theta, theta_bias, alpha, gamma, beta):
            Bs, Ls, _ = hidden_states.shape
            n_chunks = Ls // K

            def proj(w):
                return (hidden_states @ w).reshape(Bs, Ls, H, HD).transpose(0, 2, 1, 3)
            xq, xk, xv = (proj(wq), proj(wk), proj(wv))

            def to_chunks(x):
                return x.reshape(Bs, H, n_chunks, K, HD).transpose(2, 0, 1, 3, 4)
            cq, ck, cv = (to_chunks(xq), to_chunks(xk), to_chunks(xv))
            token_eta = jnp.clip(1.0 / jnp.arange(1, K + 1, dtype=jnp.float32) + alpha, 0.0)[None, None, :, None]
            g = gamma[None]
            be = beta[None]
            tb = theta_bias.reshape(1, H, 1, 1)
            W0 = jnp.broadcast_to(W1[None], (Bs, H, HD, HD))
            b0 = jnp.broadcast_to(b1[None], (Bs, H, 1, HD))

            def step(carry, inp):
                W, bb = carry
                xq_c, xk_c, xv_c = inp
                lr = jax.nn.sigmoid(jnp.einsum('bhkc,hcd->bhkd', xk_c, theta) + tb)
                eta = token_eta * (BASE_LR * lr / HD)
                Z1 = xk_c @ W + bb
                mu = Z1.mean(-1, keepdims=True)
                std = jnp.sqrt(Z1.var(-1, keepdims=True) + EPS)
                x_hat = (Z1 - mu) / std
                y = g * x_hat + be
                grad_output = y - (xv_c - xk_c)
                gxh = grad_output * g
                grad_x = (HD * gxh - gxh.sum(-1, keepdims=True) - x_hat * (gxh * x_hat).sum(-1, keepdims=True)) / (HD * std)
                dW = jnp.einsum('bhkc,bhkd->bhcd', eta * xk_c, grad_x)
                db = (eta * grad_x).sum(-2, keepdims=True)
                Wn, bn = (W - dW, bb - db)
                Zq = xq_c @ Wn + bn
                mu2 = Zq.mean(-1, keepdims=True)
                std2 = jnp.sqrt(Zq.var(-1, keepdims=True) + EPS)
                out = xq_c + g * ((Zq - mu2) / std2) + be
                return ((Wn, bn), out)
            _, outs = jax.lax.scan(step, (W0, b0), (cq, ck, cv))
            out = outs.transpose(1, 2, 0, 3, 4).reshape(Bs, H, Ls, HD)
            out = out.transpose(0, 2, 1, 3).reshape(Bs, Ls, H * HD)
            return out @ wo
        return _ttt_forward(hidden_states, wq, wk, wv, wo, W1, b1, theta, theta_bias, alpha, gamma, beta)

    def _L1_xattn_ref(y, Z, w1, b1, w2, b2, g1, beta1, g2, beta2, g3, beta3):
        import jax, jax.numpy as jnp
        import numpy as np
        B, S, D, DFF = (4, 256, 128, 512)
        EPS = 1e-05

        def layernorm(x, gamma, beta):
            mu = jnp.mean(x, axis=-1, keepdims=True)
            var = jnp.var(x, axis=-1, keepdims=True)
            return (x - mu) * jax.lax.rsqrt(var + EPS) * gamma + beta

        def attention(Q, K, V, causal):
            d_k = Q.shape[-1]
            scores = jnp.einsum('bqd,bkd->bqk', Q, K) / jnp.sqrt(jnp.asarray(d_k, Q.dtype))
            if causal:
                q_len, k_len = (scores.shape[-2], scores.shape[-1])
                mask = jnp.tril(jnp.ones((q_len, k_len), dtype=bool))
                scores = jnp.where(mask[None], scores, jnp.asarray(-jnp.inf, scores.dtype))
            w = jax.nn.softmax(scores, axis=-1)
            return jnp.einsum('bqk,bkd->bqd', w, V)
        sa = attention(y, y, y, causal=True)
        y = layernorm(y + sa, g1, beta1)
        ca = attention(y, Z, Z, causal=False)
        y = layernorm(y + ca, g2, beta2)
        h = jax.nn.relu(jnp.einsum('bsd,df->bsf', y, w1) + b1)
        ff = jnp.einsum('bsf,fd->bsd', h, w2) + b2
        y = layernorm(y + ff, g3, beta3)
        return y

    def _L1_ffn_ref(x, gate_W, W1, b1, W2, b2):
        import jax, jax.numpy as jnp
        import numpy as np
        TOP_K = 2
        N_EXPERTS = 8
        E = W1.shape[0]
        d_in = x.shape[-1]
        d_out = W2.shape[-1]
        x_flat = x.reshape(-1, d_in)
        logits = x_flat @ gate_W
        gates = jax.nn.softmax(logits, axis=-1)
        tk_g, tk_i = jax.lax.top_k(gates, TOP_K)
        tk_g = tk_g / (jnp.sum(tk_g, axis=-1, keepdims=True) + 1e-08)
        cw = jnp.sum(jax.nn.one_hot(tk_i, E, dtype=x.dtype) * tk_g[..., None], axis=1)
        out = x_flat
        for e in range(E):
            h = jax.nn.relu(x_flat @ W1[e] + b1[e])
            out = out + cw[:, e:e + 1] * (h @ W2[e] + b2[e])
        return out.reshape(x.shape[:-1] + (d_out,))
    x = x + _L0_attn_ref(_layernorm(x, axis=-1), L0_attn_W_qkv, L0_attn_b_qkv, L0_attn_W_out, L0_attn_b_out, L0_attn_w_sur, L0_attn_b_sur, L0_attn_threshold)
    x = x + _L0_xattn_ref(_layernorm(x, axis=-1), ctx_1024, mask_Bx1x1xS2_ff0, L0_xattn_tgt_bias, L0_xattn_src_wq, L0_xattn_src_bq, L0_xattn_src_wk, L0_xattn_src_bk, L0_xattn_src_wv, L0_xattn_src_bv, L0_xattn_src_wo, L0_xattn_src_bo, L0_xattn_tgt_wq, L0_xattn_tgt_bq, L0_xattn_tgt_wk, L0_xattn_tgt_bk, L0_xattn_tgt_wv, L0_xattn_tgt_bv, L0_xattn_tgt_wo, L0_xattn_tgt_bo, L0_xattn_lstm_w, L0_xattn_lstm_b, L0_xattn_ffn_w1, L0_xattn_ffn_b1, L0_xattn_ffn_w2, L0_xattn_ffn_b2)
    x = x + _L0_ffn_ref(_layernorm(x, axis=-1), L0_ffn_w_red, L0_ffn_wg, L0_ffn_W1, L0_ffn_b1, L0_ffn_W2, L0_ffn_b2)
    x = x + _L1_attn_ref(_layernorm(x, axis=-1), L1_attn_wq, L1_attn_wk, L1_attn_wv, L1_attn_wo, L1_attn_W1, L1_attn_b1, L1_attn_theta, L1_attn_theta_bias, L1_attn_alpha, L1_attn_gamma, L1_attn_beta)
    x = x + _L1_xattn_ref(_layernorm(x, axis=-1), ctx_1024, L1_xattn_w1, L1_xattn_b1, L1_xattn_w2, L1_xattn_b2, L1_xattn_g1, L1_xattn_beta1, L1_xattn_g2, L1_xattn_beta2, L1_xattn_g3, L1_xattn_beta3)
    x = x + _L1_ffn_ref(_layernorm(x, axis=-1), L1_ffn_gate_W, L1_ffn_W1, L1_ffn_b1, L1_ffn_W2, L1_ffn_b2)
    return x

_drawn_inputs = setup_inputs


def setup_inputs(seed=0):
    import zlib

    import numpy as np

    out = dict(_drawn_inputs(seed))
    spreads = {'L0_attn_b_qkv': (0.0, 0.1),
     'L0_attn_b_out': (0.0, 0.1),
     'L0_xattn_src_bq': (0.0, 0.8),
     'L0_xattn_src_bk': (0.0, 2.0),
     'L0_xattn_src_bv': (0.0, 0.8),
     'L0_xattn_src_bo': (0.0, 0.8),
     'L0_xattn_tgt_bq': (0.0, 0.8),
     'L0_xattn_tgt_bk': (0.0, 2.0),
     'L0_xattn_tgt_bv': (0.0, 0.8),
     'L0_xattn_tgt_bo': (0.0, 0.8),
     'L0_xattn_lstm_b': (0.0, 0.8),
     'L0_xattn_ffn_b1': (0.0, 0.1),
     'L0_xattn_ffn_b2': (0.0, 0.1),
     'L1_attn_b1': (0.0, 0.1),
     'L1_attn_theta_bias': (0.0, 0.493),
     'L1_attn_alpha': (0.0, 0.1),
     'L1_attn_gamma': (1.0, 0.2),
     'L1_attn_beta': (0.0, 0.1),
     'L1_xattn_b1': (0.0, 0.52),
     'L1_xattn_b2': (0.0, 0.1),
     'L1_xattn_g1': (1.0, 0.2),
     'L1_xattn_beta1': (0.0, 0.1),
     'L1_xattn_g2': (1.0, 0.2),
     'L1_xattn_beta2': (0.0, 0.1),
     'L1_xattn_g3': (1.0, 0.2),
     'L1_xattn_beta3': (0.0, 0.1),
     'L1_ffn_b1': (0.0, 0.421),
     'L1_ffn_b2': (0.0, 0.334)}
    factors = {'L0_xattn_tgt_bias': 8.0,
     'L0_xattn_src_wq': 8.0,
     'L0_xattn_src_wk': 8.0,
     'L0_xattn_src_wv': 8.0,
     'L0_xattn_src_wo': 8.0,
     'L0_xattn_tgt_wq': 8.0,
     'L0_xattn_tgt_wk': 8.0,
     'L0_xattn_tgt_wv': 8.0,
     'L0_xattn_tgt_wo': 8.0,
     'L0_xattn_lstm_w': 8.0,
     'L0_xattn_ffn_w1': 8.0,
     'L0_ffn_w_red': 7.76,
     'L0_ffn_wg': 7.402,
     'L0_ffn_W1': 8.0,
     'L0_ffn_b1': 8.0,
     'L0_ffn_W2': 7.674,
     'L0_ffn_b2': 8.0,
     'L1_attn_theta': 28.434}
    for name, (base, spread) in spreads.items():
        noise = np.random.default_rng([zlib.crc32(name.encode()), seed]).standard_normal(out[name].shape)
        drawn = base * np.exp(spread * noise) if base else spread * noise
        out[name] = jnp.asarray(drawn.astype(out[name].dtype))
    for name, factor in factors.items():
        out[name] = (out[name] * factor).astype(out[name].dtype)
    return out
```

```python
from contextlib import ExitStack

import numpy as np

import concourse.bass as bass
from concourse import mybir

F32 = mybir.dt.float32
ACT = mybir.ActivationFunctionType
ALU = mybir.AluOpType
AX_X = mybir.AxisListType.X

P = 128
C = 128
SEQ = 64
BATCH = 64
TOKENS = SEQ * BATCH
TILES = TOKENS // P
GT = 4
GB = 2 * GT
GN = GT * P
GROUPS = TILES // GT
H = 16
D = C // H
STRIPS = 4
HG = H // STRIPS
PAIRS = H // 2
PW = 2 * D + 2
GATES = 4
GATE_ORDER = (1, 0, 2, 3)
HID = 512
HC = HID // P
E = 8
EH = 256
EC = EH // P
RED = 16
TD = 64
TW = H * TD
LN_TURN = {"ln1": 0, "ln2": 1, "ln3": 0, "ln4": 1, "ln5": 0, "g1": 1, "g2": 2, "g3": 3, "ln6": 4}
NEG = -1e30
INV_SQRT_D = float(1.0 / np.sqrt(D))
INV_SQRT_C = float(1.0 / np.sqrt(C))


class Signals:

    def __init__(self, nc, stack):
        self.nc, self.stack, self.made = nc, stack, {}

    def __getitem__(self, name):
        if name not in self.made:
            self.made[name] = self.stack.enter_context(self.nc.semaphore(name))
        return self.made[name]

    def runs(self):
        nums = sorted(s.num for s in self.made.values())
        starts = [n for n in nums if n - 1 not in nums]
        ends = [n + 1 for n in nums if n + 1 not in nums]
        return [range(a, b) for a, b in zip(starts, ends)]


class Shared:

    def __init__(self, four_banks, nc, I, out, sb, tiles, pair, bank, x_all, gate0, gates123, arena, ident, eps5, eps6, one, x_cur,
                 ctx_cur, x_norm, lstm_wh, ln_vector, ln_scalar, transpose_tiles):
        self.nc, self.I, self.out, self.sb, self.tiles, self.pair, self.bank = nc, I, out, sb, tiles, pair, bank
        self.x_all, self.gate0, self.gates123, self.arena, self.ident = x_all, gate0, gates123, arena, ident
        self.eps5, self.eps6, self.one, self.x_cur, self.ctx_cur, self.x_norm = eps5, eps6, one, x_cur, ctx_cur, x_norm
        self.lstm_wh, self.ln_vector, self.ln_scalar = lstm_wh, ln_vector, ln_scalar
        self.transpose_tiles, self.four_banks = transpose_tiles, four_banks


def bcast(ap, axis, count):
    a = ap.unsqueeze(axis)
    shape = list(a.shape)
    shape[axis] = count
    return a.broadcast_to(shape)


def finish_phase(nc, signals):
    for run in signals.runs():
        nc.multi_engine_barrier(list(nc.engines), sems_to_clear=run)


def build(nc, I, out):
    with ExitStack() as whole, nc.allow_non_contiguous_dma(reason="bias columns and padded heads, once"):
        _build(nc, I, out, whole)


def _build(nc, I, out, whole):
    def sb(name, shape, stack=whole):
        return stack.enter_context(nc.sbuf_tensor(name, shape, F32))

    tiles = lambda ap: ap.rearrange("b s d -> (b s) d").rearrange("(t p) d -> p t d", p=P)

    lower = whole.enter_context(nc.psum_tensor("lower_banks", [P, 4, 512], F32))
    upper = whole.enter_context(nc.psum_tensor("upper_banks", [P, 4, 512], F32))
    pair = [half[:, 2 * i:2 * i + 2, :].rearrange("p k n -> p (k n)") for half in (lower, upper) for i in range(2)]

    def bank(i):
        return pair[i // 2][:, (i % 2) * 512:(i % 2) * 512 + 512]

    x_all = sb("x_all", [P, TILES, C])
    gate0 = sb("gate0", [P, TOKENS])
    ident = sb("ident", [P, P])
    eps5 = sb("eps5", [P, 1])
    eps6 = sb("eps6", [P, 1])
    x_cur = sb("x_cur", [P, GT, C])
    ctx_cur = sb("ctx_cur", [P, GT, C])
    x_norm = sb("x_norm", [P, GT, C])
    ln_stats = sb("ln_stats", [P, GT, 6])
    ln_moments = sb("ln_moments", [P, GT, 2])
    ln_logvar = sb("ln_logvar", [P, GT])
    ln_rstd = sb("ln_rstd", [P, GT])
    lstm_wh = sb("lstm_wh", [P, GATES * C])
    one = sb("one", [P, 1])
    arena = sb("arena", [P, (GATES - 1) * TOKENS])

    def ln_vector(e, S, tag, src, dst, affine=None):
        n = LN_TURN[tag]
        for t in range(GT):
            nc.vector.bn_stats(ln_stats[:, t, :], src[:, t, :]).then_inc(S["ln_stats"], 1)
        for t in range(GT):
            e.wait_ge(S["ln_stats"], GT * n + t + 1)
            nc.vector.bn_aggr(ln_moments[:, t, :], ln_stats[:, t, :]).then_inc(S["ln_moments"], 1)
        e.wait_ge(S["ln_rstd"], n + 1)
        for t in range(GT):
            nc.vector.tensor_scalar(dst[:, t, :], src[:, t, :], ln_moments[:, t, 0:1], ln_rstd[:, t:t + 1],
                                    ALU.subtract, ALU.mult).then_inc(S["ln_unit"], 1)
        if affine is not None:
            gain, shift = affine
            e.wait_ge(S["ln_unit"], GT * (n + 1))
            nc.vector.tensor_tensor(dst, dst, bcast(gain, 1, GT), ALU.mult).then_inc(S[f"{tag}_gained"], 1)
            e.wait_ge(S[f"{tag}_gained"], 1)
            nc.vector.tensor_tensor(dst, dst, bcast(shift, 1, GT), ALU.add).then_inc(S[f"{tag}_done"], 1)

    def ln_scalar(e, S, tag):
        n = LN_TURN[tag]
        e.wait_ge(S["ln_moments"], GT * (n + 1))
        nc.scalar.activation(ln_logvar[:, :], ln_moments[:, :, 1], ACT.Ln, bias=eps5[:, 0:1])\
            .then_inc(S["ln_logvar"], 1)
        e.wait_ge(S["ln_logvar"], n + 1)
        nc.scalar.activation(ln_rstd[:, :], ln_logvar[:, :], ACT.Exp, scale=-0.5).then_inc(S["ln_rstd"], 1)

    def transpose_tiles(e, S, ready, ready_count, src, dst_bank, done):
        for t in range(GT):
            e.wait_ge(S[ready], ready_count(t))
            nc.tensor.transpose(dst_bank[:, t * P:(t + 1) * P], src[:, t, :], ident[:, :]).then_inc(S[done], 1)

    gates123 = arena[:, :].rearrange("p (j n) -> p j n", j=GATES - 1)
    m = Shared(lower, nc, I, out, sb, tiles, pair, bank, x_all, gate0, gates123, arena, ident, eps5, eps6, one, x_cur, ctx_cur,
               x_norm, lstm_wh, ln_vector, ln_scalar, transpose_tiles)
    with ExitStack() as mem_a:
        phase_a(m, mem_a)
    with ExitStack() as mem_c:
        m.stack_c = mem_c
        w = phase_b(m, mem_c)
        prepare_c(m, w)
        phase_c(m, w)


def row(ap):
    n = len(ap.shape)
    flat = ap if n == 1 else ap.rearrange({2: "a b -> (a b)", 3: "a b c -> (a b c)"}[n])
    return flat.partition_broadcast(P)


def phase_a(m, stack):
    four_banks = m.four_banks
    nc, I, tiles, pair, bank, ident = m.nc, m.I, m.tiles, m.pair, m.bank, m.ident
    x_all, gate0, gates123, x_cur, ctx_cur, x_norm = m.x_all, m.gate0, m.gates123, m.x_cur, m.ctx_cur, m.x_norm
    eps5, eps6, one, lstm_wh = m.eps5, m.eps6, m.one, m.lstm_wh
    ln_vector, ln_scalar, transpose_tiles = m.ln_vector, m.ln_scalar, m.transpose_tiles

    def sb(name, shape):
        return m.sb(name, shape, stack)

    w_qk = sb("w_qk", [P, 2 * C + 1])
    b_qk = sb("b_qk", [P, 2 * C + 1])
    w_v = {k: sb(f"w_v_{k}", [P, C]) for k in ("lor", "src", "tgt")}
    b_v = {k: sb(f"b_v_{k}", [P, C]) for k in ("lor", "src", "tgt")}
    w_o = {k: sb(f"w_o_{k}", [P, C]) for k in ("lor", "src", "tgt")}
    b_o_lor = sb("b_o_lor", [P, C])
    w_strip = {k + s: sb(f"w_strip_{k}_{s}", [P, HG, STRIPS, 32]) for k in ("src", "tgt") for s in "qk"}
    b_strip = {k + s: sb(f"b_strip_{k}_{s}", [P, HG]) for k in ("src", "tgt") for s in "qk"}
    b_o_col = sb("b_o_col", [P, 2])
    b_o_sum = sb("b_o_sum", [P, 1])
    lstm_wx = sb("lstm_wx", [P, 2, GATES * C])
    lstm_b = sb("lstm_b", [P, GATES])
    threshold = sb("threshold", [P, 1])
    tgt_bias = sb("tgt_bias", [P, SEQ])
    causal = sb("causal", [P, SEQ])

    xT = sb("xT", [P, GB, 2, SEQ])
    ctxT = sb("ctxT", [P, GB, 2, SEQ])
    x_once = sb("x_once", [P, GN])
    qk = sb("qk", [P, GT, 2 * C + 1])
    n_h = GT * 2 * H
    m_mink, m_log, m_norm, m_ep, m_en, m_cosh2, m_sinh2, m_rn, m_s, m_p, m_small, m_x = (
        sb(f"map_{n}", [P, n_h]) for n in ("mink", "log", "norm", "ep", "en", "cosh2", "sinh2", "rn", "s", "p",
                                            "small", "x"))
    spike_e = sb("spike_e", [P, GT])
    spike_s = sb("spike_s", [P, GT])
    spike = sb("spike", [P, GT])
    padded = sb("padded", [P, 2, 2, HG, STRIPS, 32])
    heads = {k: (sb(f"qT_{k}", [P, HG, GN]), sb(f"kT_{k}", [P, HG, GN])) for k in ("tgt", "src")}
    heads["lor"] = heads["tgt"]
    V = {k: sb(f"V_{k}", [P, GB, PAIRS, PW]) for k in ("src", "tgt")}
    V["lor"] = V["tgt"]
    score = sb("score", [P, 2, H, SEQ])
    aux = heads["src"][0][:, :, :].rearrange("p g n -> p (g n)").rearrange("p (u h k) -> p u h k", u=2, h=H)
    sq = heads["src"][1][:, 0:2, :].rearrange("p g n -> p (g n)").rearrange("p (t c) -> p t c", t=GT)
    row_max = sb("row_max", [P, 2, H])
    PT = sb("PT", [P, PAIRS, P])
    row_rec = sb("row_rec", [P, PAIRS, 2])
    o_tm = {k: sb(f"o_tm_{k}", [P, GT, C]) for k in ("lor", "src")}
    o_tm["tgt"] = o_tm["lor"]
    oT = {k: sb(f"oT_{k}", [P, GN]) for k in ("src", "tgt")}
    cT = sb("cT", [P, GN])

    with ExitStack() as sems:
        S = Signals(nc, sems)
        loads = [
            (x_all[:, :, :], tiles(I["x"])),
            (w_qk[:, 0:2 * C], I["L0_attn_W_qkv"][:, 0:2 * C]),
            (w_qk[:, 2 * C:], I["L0_attn_w_sur"].unsqueeze(1)),
            (b_qk[:, 0:2 * C], row(I["L0_attn_b_qkv"][0:2 * C])),
            (b_qk[:, 2 * C:], row(I["L0_attn_b_sur"])),
            (threshold[:, :], row(I["L0_attn_threshold"])),
            (w_v["lor"][:, :], I["L0_attn_W_qkv"][:, 2 * C:]),
            (b_v["lor"][:, :], row(I["L0_attn_b_qkv"][2 * C:])),
            (w_o["lor"][:, :], I["L0_attn_W_out"]),
            (b_o_lor[:, :], row(I["L0_attn_b_out"])),
            (lstm_wx[:, :, :], I["L0_xattn_lstm_w"][0:2 * C, :].rearrange("(k p) n -> p k n", p=P)),
            (lstm_wh[:, :], I["L0_xattn_lstm_w"][2 * C:, :]),
            (lstm_b[:, :], I["L0_xattn_lstm_b"].rearrange("(c p) -> p c", p=P)),
        ]
        for n, k in enumerate(("src", "tgt")):
            loads += [(w_v[k][:, :], I[f"L0_xattn_{k}_wv"]), (b_v[k][:, :], row(I[f"L0_xattn_{k}_bv"])),
                      (w_o[k][:, :], I[f"L0_xattn_{k}_wo"]),
                      (b_o_col[:, n:n + 1], I[f"L0_xattn_{k}_bo"].unsqueeze(1))]
        for half in range(2):
            rows = slice(half * SEQ, half * SEQ + SEQ)
            loads += [(tgt_bias[rows, :], I["L0_xattn_tgt_bias"])]
        padded_loads = []
        for k in ("src", "tgt"):
            for s in "qk":
                for g in range(HG):
                    padded_loads.append((w_strip[k + s][:, g, :, 0:D], I[f"L0_xattn_{k}_w{s}"].rearrange(
                        "k (s g d) -> g k s d", s=STRIPS, d=D)[g]))
                for strip in range(STRIPS):
                    padded_loads.append((b_strip[k + s][32 * strip:32 * strip + D, :], I[f"L0_xattn_{k}_b{s}"].rearrange(
                        "(s g d) -> s d g", s=STRIPS, d=D)[strip]))
        with nc.Block() as block:
            @block.sync
            def _(sp):
                for dst, src in loads:
                    sp.dma_start(dst, src).then_inc(S["inputs_loaded"], 16)
                sp.wait_ge(S["strips_cleared"], 8)
                for dst, src in padded_loads:
                    sp.dma_start(dst, src).then_inc(S["inputs_loaded"], 16)
                sp.wait_ge(S["inputs_loaded"], 16 * (len(loads) + len(padded_loads)))

            @block.vector
            def _(dve):
                for k in w_strip:
                    nc.vector.memset(w_strip[k][:, :, :, :], 0.0).then_inc(S["strips_cleared"], 1)
                    nc.vector.memset(b_strip[k][:, :], 0.0).then_inc(S["strips_cleared"], 1)
                nc.vector.memset(padded[:, :, :, :, :, :], 0.0)
                nc.vector.memset(eps5[:, :], 1e-5)
                nc.vector.memset(eps6[:, :], 1e-6)
                nc.vector.memset(one[:, :], 1.0)
                for k in ("src", "tgt"):
                    nc.vector.memset(V[k][:, :, :, :], 0.0).then_inc(S["V_cleared"], 1)
                dve.wait_ge(S["V_cleared"], 2)
                for k in ("src", "tgt"):
                    for half in range(2):
                        rows = slice(half * SEQ, half * SEQ + SEQ)
                        col = 2 * D + half
                        nc.vector.memset(V[k][rows, :, :, col:col + 1], 1.0)
                dve.wait_ge(S["inputs_loaded"], 16 * (len(loads) + len(padded_loads)))
                nc.vector.tensor_tensor(b_o_sum[:, :], b_o_col[:, 0:1], b_o_col[:, 1:2], ALU.add)
                for k in ("srcq", "tgtq"):
                    nc.vector.tensor_scalar(b_strip[k][:, :], b_strip[k][:, :], INV_SQRT_D, None, ALU.mult)

            @block.gpsimd
            def _(pool):
                nc.gpsimd.memset(ident[:, :], 0.0).then_inc(S["ident_cleared"], 1)
                nc.gpsimd.memset(causal[:, :], 0.0).then_inc(S["causal_cleared"], 1)
                pool.wait_ge(S["ident_cleared"], 1)
                nc.gpsimd.affine_select(out=ident[:, :], in_=ident[:, :], compare_op=ALU.not_equal, fill=1.0,
                                        base=0, pattern=[[-1, P]], channel_multiplier=1)\
                    .then_inc(S["ident_made"], 1)
                pool.wait_ge(S["causal_cleared"], 1)
                for half in range(2):
                    rows = slice(half * SEQ, half * SEQ + SEQ)
                    pool.wait_ge(S["ident_made"], half + 1)
                    nc.gpsimd.affine_select(out=causal[rows, :], in_=causal[rows, :], compare_op=ALU.is_ge, fill=NEG,
                                            base=0, pattern=[[-1, SEQ]], channel_multiplier=1)\
                        .then_inc(S["ident_made"], 1)
        finish_phase(nc, S)

    def scores_tensor(e, S, tag, u, kind, t):
        qT, kT = heads[kind]
        if u >= 1:
            e.wait_ge(S[f"{tag}_score_read"], u)
        for b in range(2):
            for h in range(H):
                s, g = divmod(h, HG)
                rows, cols = slice(32 * s, 32 * s + D), slice((2 * t + b) * SEQ, (2 * t + b + 1) * SEQ)
                mm = nc.tensor.matmul(bank(s)[b * SEQ:(b + 1) * SEQ, g * SEQ:(g + 1) * SEQ],
                                      qT[rows, g, cols], kT[rows, g, cols], start=True, stop=True)
        mm.then_inc(S[f"{tag}_score"], 1)

    def values_tensor(e, S, tag, u, kind, t):
        e.wait_ge(S[f"{tag}_prob"], u + 1)
        for half in range(2):
            if u >= 1:
                e.wait_ge(S[f"{tag}_PT_act" if half == 0 else f"{tag}_PT_dve"], u)
            for p in range(4 * half, 4 * half + 4):
                tr = nc.tensor.transpose(pair[2][:, p * P:(p + 1) * P], score[:, u % 2, 2 * p:2 * p + 2, :],
                                         ident[:, :])
            tr.then_inc(S[f"{tag}_turned"], 1)
        e.wait_ge(S[f"{tag}_PT_act"], u + 1)
        e.wait_ge(S[f"{tag}_PT_dve"], u + 1)
        if u >= 1:
            e.wait_ge(S[f"{tag}_normed"], u)
        for b in range(2):
            for p in range(PAIRS):
                mm = nc.tensor.matmul(bank(6)[b * SEQ:(b + 1) * SEQ, p * PW:(p + 1) * PW],
                                      PT[:, p, b * SEQ:(b + 1) * SEQ], V[kind][:, 2 * t + b, p, :],
                                      start=True, stop=True)
        mm.then_inc(S[f"{tag}_summed"], 1)

    def front_vector(e, S, tag, u, kind, t):
        ps = four_banks[:, :, 0:HG * SEQ]
        wide = score[:, u % 2, :, :].rearrange("q (s g) k -> q s (g k)", s=STRIPS)
        sc, ax = score[:, u % 2, :, :], aux[:, u % 2, :, :]
        e.wait_ge(S[f"{tag}_score"], u + 1)
        if u >= 2:
            e.wait_ge(S[f"{tag}_turned"], 2 * (u - 1))
        if kind == "lor":
            nc.vector.tensor_scalar(wide, ps, float(np.float32(1.0 + 1e-7)), -1.0, ALU.max, ALU.add)\
                .then_inc(S[f"{tag}_score_read"], 1)
            e.wait_ge(S[f"{tag}_score_read"], u + 1)
            nc.vector.scalar_tensor_tensor(out=ax, in0=sc, scalar=2.0, in1=sc, op0=ALU.add, op1=ALU.mult)\
                .then_inc(S[f"{tag}_w"], 1)
        else:
            bias = src_cur[:, t, :] if kind == "src" else tgt_bias[:, :]
            nc.vector.tensor_tensor(score[:, u % 2, :, :].rearrange("q (s g) k -> q s g k", s=STRIPS),
                                    ps.rearrange("q s (g k) -> q s g k", g=HG), bcast(bcast(bias, 1, HG), 1, STRIPS),
                                    ALU.add).then_inc(S[f"{tag}_score_read"], 1)
            e.wait_ge(S[f"{tag}_score_read"], u + 1)
            nc.vector.tensor_reduce(row_max[:, u % 2, :], sc, AX_X, ALU.max).then_inc(S[f"{tag}_max"], 1)

    def lorentz_scores_vector(e, S, tag, u):
        sc, ax = score[:, u % 2, :, :], aux[:, u % 2, :, :]
        e.wait_ge(S[f"{tag}_dist2"], u + 1)
        nc.vector.scalar_tensor_tensor(out=sc, in0=ax, scalar=-INV_SQRT_D, in1=bcast(causal[:, :], 1, H),
                                       op0=ALU.mult, op1=ALU.add).then_inc(S[f"{tag}_masked"], 1)
        e.wait_ge(S[f"{tag}_masked"], u + 1)
        nc.vector.tensor_reduce(row_max[:, u % 2, :], sc, AX_X, ALU.max).then_inc(S[f"{tag}_max"], 1)

    def back_vector(e, S, tag, u, kind, t):
        e.wait_ge(S[f"{tag}_turned"], 2 * u + 2)
        if u >= 1:
            e.wait_ge(S[f"{tag}_summed"], u)
        nc.vector.tensor_copy(PT[:, 4:8, :], pair[2][:, 512:1024].rearrange("k (p q) -> k p q", p=4))\
            .then_inc(S[f"{tag}_PT_dve"], 1)
        e.wait_ge(S[f"{tag}_summed"], u + 1)
        O = bank(6)[:, 0:PAIRS * PW].rearrange("q (p w) -> q p w", w=PW)
        nc.vector.reciprocal(row_rec[:, :, :], O[:, :, 2 * D:]).then_inc(S[f"{tag}_rec"], 1)
        e.wait_ge(S[f"{tag}_rec"], u + 1)
        if kind == "lor":
            nc.vector.tensor_scalar(row_rec[:, :, :], row_rec[:, :, :], spike[:, t:t + 1], None, ALU.mult)\
                .then_inc(S[f"{tag}_spiked"], 1)
            e.wait_ge(S[f"{tag}_spiked"], u + 1)
        nc.vector.tensor_tensor(o_tm[kind][:, t, :].rearrange("q (p two d) -> q p two d", two=2, d=D),
                                O[:, :, 0:2 * D].rearrange("q p (two d) -> q p two d", two=2),
                                bcast(row_rec[:, :, :], 3, D), ALU.mult).then_inc(S[f"{tag}_normed"], 1)

    def shift_gpsimd(e, S, tag, u):
        e.wait_ge(S[f"{tag}_max"], u + 1)
        nc.gpsimd.tensor_tensor(score[:, u % 2, :, :], score[:, u % 2, :, :], bcast(row_max[:, u % 2, :], 2, SEQ),
                                ALU.subtract).then_inc(S[f"{tag}_shifted"], 1)

    def exp_scalar(e, S, tag, u):
        e.wait_ge(S[f"{tag}_shifted"], u + 1)
        nc.scalar.activation(score[:, u % 2, :, :], score[:, u % 2, :, :], ACT.Exp).then_inc(S[f"{tag}_prob"], 1)

    def turned_scalar(e, S, tag, u):
        e.wait_ge(S[f"{tag}_turned"], 2 * u + 1)
        if u >= 1:
            e.wait_ge(S[f"{tag}_summed"], u)
        nc.scalar.activation(PT[:, 0:4, :], pair[2][:, 0:512].rearrange("k (p q) -> k p q", p=4), ACT.Copy)\
            .then_inc(S[f"{tag}_PT_act"], 1)

    def fill_V_vector(e, S, kind, b0):
        src = pair[2].rearrange("k (b p two d) -> k b p two d", b=GB, p=PAIRS, two=2)
        for half in range(2):
            rows = slice(half * SEQ, half * SEQ + SEQ)
            bias = b_v[kind][rows, :].rearrange("k (p two d) -> k p two d", p=PAIRS, two=2)[:, :, half, :]
            nc.vector.tensor_tensor(V[kind][rows, :, :, half * D:half * D + D], src[rows, :, :, half, :],
                                    bcast(bias, 1, GB), ALU.add).then_inc(S[f"{kind}_V"], 1)

    src_cur = sb("src_cur", [P, GT, SEQ])
    masks = I["mask_Bx1x1xS2_ff0"].rearrange("(t two) a b s -> two t (a b s)", two=2)
    lor_units = [("lor", t) for t in range(GT)]
    mha_units = [(k, t) for k in ("src", "tgt") for t in range(GT)]
    n_l, n_m = len(lor_units), len(mha_units)

    with ExitStack() as sems:
        S = Signals(nc, sems)
        with nc.Fori(0, GROUPS) as g:
            with nc.Block() as block:
                @block.tensor
                def _(pe):
                    transpose_tiles(pe, S, "ln_unit", lambda t: GT * LN_TURN["ln1"] + t + 1, x_norm, bank(7), "ln1_turned")
                    pe.wait_ge(S["ctx_loaded"], 16)
                    for t in range(GT):
                        nc.tensor.transpose(bank(6)[:, t * P:(t + 1) * P], ctx_cur[:, t, :], ident[:, :])\
                            .then_inc(S["ctx_turned"], 1)
                    pe.wait_ge(S["ln1_T"], 2)
                    for t in range(GT):
                        nc.tensor.matmul(bank(t)[:, 0:2 * C + 1], x_once[:, t * P:(t + 1) * P], w_qk[:, :],
                                         start=True, stop=True).then_inc(S["lor_qk"], 1)
                    for b in range(GB):
                        mm = nc.tensor.matmul(pair[2][:, b * C:(b + 1) * C], xT[:, b, :, :], w_v["lor"][:, :],
                                              start=True, stop=True)
                    mm.then_inc(S["lor_v"], 1)
                    for j in range(2 * GT):
                        t, side = divmod(j, 2)
                        pe.wait_ge(S["padded"], 2 * t + 2)
                        if j < 4:
                            pe.wait_ge(S["lor_qk_sb"], j + 1)
                        else:
                            pe.wait_ge(S["strips_act"], j // 2 - 1)
                            pe.wait_ge(S["strips_dve"], j // 2 - 1)
                        for hg in range(HG):
                            tr = nc.tensor.transpose(bank(j % 4)[:, hg * P:(hg + 1) * P],
                                                     padded[:, t % 2, side, hg, :, :],
                                                     ident[:, :])
                        tr.then_inc(S["strips_turned"], 1)
                    pe.wait_ge(S["strips_act"], GT)
                    pe.wait_ge(S["strips_dve"], GT)
                    pe.wait_ge(S["lor_V"], 2)
                    pe.wait_ge(S["ctx_T"], 1)
                    for u in range(n_l + 1):
                        if u < n_l:
                            scores_tensor(pe, S, "lor", u, *lor_units[u])
                        if u >= 1:
                            values_tensor(pe, S, "lor", u - 1, *lor_units[u - 1])
                    pe.wait_ge(S["lor_normed"], n_l)
                    for t in range(GT):
                        tr = nc.tensor.transpose(bank(7)[:, t * P:(t + 1) * P], o_tm["lor"][:, t, :], ident[:, :])
                    tr.then_inc(S["lor_o_turned"], 1)
                    pe.wait_ge(S["lor_oT"], 1)
                    for t in range(GT):
                        mm = nc.tensor.matmul(bank(6)[:, t * P:(t + 1) * P], oT["src"][:, t * P:(t + 1) * P],
                                              w_o["lor"][:, :], start=True, stop=True)
                    mm.then_inc(S["lor_y"], 1)

                    transpose_tiles(pe, S, "ln_unit", lambda t: GT * LN_TURN["ln2"] + t + 1, x_norm, bank(7), "ln2_turned")
                    pe.wait_ge(S["ln2_T"], 1)
                    for k, src in (("src", ctxT), ("tgt", xT)):
                        if k == "tgt":
                            pe.wait_ge(S["src_V"], 2)
                        for b in range(GB):
                            mm = nc.tensor.matmul(pair[2][:, b * C:(b + 1) * C], src[:, b, :, :], w_v[k][:, :],
                                                  start=True, stop=True)
                        mm.then_inc(S[f"{k}_v"], 1)
                    j = 0
                    for k in ("src", "tgt"):
                        for s in "qk":
                            for hg in range(HG):
                                if j >= 4:
                                    pe.wait_ge(S["proj_sb"], j - 3)
                                src = ctxT if (k, s) == ("src", "k") else xT
                                nc.tensor.matmul(bank(j % 4), w_strip[k + s][:, hg, :, :], src[:, :, 0, :],
                                                 start=True, stop=True).then_inc(S["proj"], 1)
                                j += 1
                    pe.wait_ge(S["tgt_V"], 2)
                    pe.wait_ge(S["proj_sb"], 16)
                    for u in range(n_m + 1):
                        if u < n_m:
                            scores_tensor(pe, S, "mha", u, *mha_units[u])
                        if u >= 1:
                            values_tensor(pe, S, "mha", u - 1, *mha_units[u - 1])
                    for n, k in enumerate(("src", "tgt")):
                        pe.wait_ge(S["mha_normed"], GT * (n + 1))
                        for t in range(GT):
                            tr = nc.tensor.transpose(bank(n)[:, t * P:(t + 1) * P], o_tm[k][:, t, :], ident[:, :])
                        tr.then_inc(S["mha_o_turned"], 1)
                    pe.wait_ge(S["mha_oT"], 2)
                    nc.tensor.matmul(bank(7), w_o["src"][:, :], oT["src"][:, :], start=True, stop=False)
                    nc.tensor.matmul(bank(7), w_o["tgt"][:, :], oT["tgt"][:, :], start=False, stop=True)\
                        .then_inc(S["c"], 1)
                    for n, j in enumerate(GATE_ORDER):
                        nc.tensor.matmul(bank(2 + n), lstm_wx[:, 0, j * C:(j + 1) * C], xT[:, :, 0, :],
                                         start=True, stop=False)
                        if n == 0:
                            pe.wait_ge(S["cT"], 1)
                        nc.tensor.matmul(bank(2 + n), lstm_wx[:, 1, j * C:(j + 1) * C], cT[:, :],
                                         start=False, stop=True).then_inc(S["gate_x"], 1)

                @block.scalar
                def _(act):
                    ln_scalar(act, S, "ln1")
                    act.wait_ge(S["ln1_turned"], GT)
                    nc.scalar.activation(x_once[:, :], bank(7), ACT.Copy).then_inc(S["ln1_T"], 1)
                    nc.scalar.activation(xT[:, :, :, :], bcast(bank(7).rearrange("c (b s) -> c b s", b=GB), 2, 2),
                                         ACT.Copy).then_inc(S["ln1_T"], 1)
                    act.wait_ge(S["ctx_turned"], GT)
                    nc.scalar.activation(ctxT[:, :, :, :], bcast(bank(6).rearrange("c (b s) -> c b s", b=GB), 2, 2),
                                         ACT.Copy).then_inc(S["ctx_T"], 1)
                    act.wait_ge(S["mink"], 1)
                    nc.scalar.activation(m_log[:, :], m_mink[:, :], ACT.Ln).then_inc(S["norm_log"], 1)
                    act.wait_ge(S["norm_log"], 1)
                    nc.scalar.activation(m_norm[:, :], m_log[:, :], ACT.Exp, scale=0.5).then_inc(S["norm"], 1)
                    act.wait_ge(S["norm"], 1)
                    nc.scalar.activation(m_ep[:, :], m_norm[:, :], ACT.Exp).then_inc(S["exps"], 1)
                    nc.scalar.activation(m_en[:, :], m_norm[:, :], ACT.Exp, scale=-1.0).then_inc(S["exps"], 1)
                    act.wait_ge(S["lor_qk_sb"], GT)
                    nc.scalar.activation(spike_e[:, :], qk[:, :, 2 * C], ACT.Exp, scale=-1.0).then_inc(S["spike_e"], 1)
                    for t in range(GT):
                        act.wait_ge(S["strips_turned"], 2 * t + 1)
                        nc.scalar.activation(heads["lor"][0][:, :, t * P:(t + 1) * P],
                                             bank((2 * t) % 4).rearrange("r (g q) -> r g q", g=HG), ACT.Copy)\
                            .then_inc(S["strips_act"], 1)

                    def lorentz_scalar(u):
                        sc, ax = score[:, u % 2, :, :], aux[:, u % 2, :, :]
                        act.wait_ge(S["lor_w"], u + 1)
                        nc.scalar.activation(ax, ax, ACT.Ln).then_inc(S["lor_logw"], 1)
                        act.wait_ge(S["lor_logw"], u + 1)
                        nc.scalar.activation(ax, ax, ACT.Exp, scale=0.5).then_inc(S["lor_root"], 1)

                    def arccosh_scalar(u):
                        ax = aux[:, u % 2, :, :]
                        act.wait_ge(S["lor_arg"], u + 1)
                        nc.scalar.activation(ax, ax, ACT.Ln, bias=one[:, 0:1]).then_inc(S["lor_dist"], 1)

                    for u in range(n_l + 1):
                        if u < n_l:
                            lorentz_scalar(u)
                            arccosh_scalar(u)
                            exp_scalar(act, S, "lor", u)
                        if u >= 1:
                            turned_scalar(act, S, "lor", u - 1)
                    act.wait_ge(S["lor_o_turned"], 1)
                    nc.scalar.activation(oT["src"][:, :], bank(7), ACT.Copy).then_inc(S["lor_oT"], 1)

                    ln_scalar(act, S, "ln2")
                    act.wait_ge(S["ln2_turned"], GT)
                    nc.scalar.activation(xT[:, :, :, :], bcast(bank(7).rearrange("c (b s) -> c b s", b=GB), 2, 2),
                                         ACT.Copy).then_inc(S["ln2_T"], 1)
                    j = 0
                    for k in ("src", "tgt"):
                        for i, s in enumerate("qk"):
                            for hg in range(HG):
                                act.wait_ge(S["proj"], j + 1)
                                nc.scalar.activation(heads[k][i][:, hg, :], bank(j % 4), ACT.Identity,
                                                     bias=b_strip[k + s][:, hg:hg + 1],
                                                     scale=INV_SQRT_D if s == "q" else 1.0).then_inc(S["proj_sb"], 1)
                                j += 1
                    for u in range(n_m + 1):
                        if u < n_m:
                            exp_scalar(act, S, "mha", u)
                        if u >= 1:
                            turned_scalar(act, S, "mha", u - 1)
                    for n, k in enumerate(("src", "tgt")):
                        act.wait_ge(S["mha_o_turned"], n + 1)
                        nc.scalar.activation(oT[k][:, :], bank(n), ACT.Copy).then_inc(S["mha_oT"], 1)
                    act.wait_ge(S["c"], 1)
                    nc.scalar.activation(cT[:, :], bank(7), ACT.Identity, bias=b_o_sum[:, 0:1]).then_inc(S["cT"], 1)
                    for n, j in enumerate(GATE_ORDER):
                        act.wait_ge(S["gate_x"], n + 1)
                        dst = gate0[:, bass.ds(g * GN, GN)] if n == 0 else gates123[:, n - 1, bass.ds(g * GN, GN)]
                        nc.scalar.activation(dst, bank(2 + n), ACT.Identity, bias=lstm_b[:, j:j + 1])\
                            .then_inc(S["gates_stored"], 1)

                @block.vector
                def _(dve):
                    nc.vector.tensor_copy(x_cur[:, :, :], x_all[:, bass.ds(g * GT, GT), :]).then_inc(S["x_cur"], 1)
                    dve.wait_ge(S["x_cur"], 1)
                    ln_vector(dve, S, "ln1", x_cur, x_norm)
                    for t in range(GT):
                        dve.wait_ge(S["lor_qk"], t + 1)
                        nc.vector.tensor_tensor(qk[:, t, :], bank(t)[:, 0:2 * C + 1], b_qk[:, :], ALU.add)\
                            .then_inc(S["lor_qk_sb"], 1)
                    dve.wait_ge(S["lor_v"], 1)
                    fill_V_vector(dve, S, "lor", 0)
                    dve.wait_ge(S["sq"], 1)
                    sq4 = sq[:, :, :].rearrange("q t (h d) -> q (t h) d", d=D)
                    nc.vector.tensor_reduce(m_x[:, :], sq4[:, :, 1:D], AX_X, ALU.add).then_inc(S["map_v"], 1)
                    dve.wait_ge(S["map_v"], 1)
                    nc.vector.tensor_tensor(m_x[:, :], m_x[:, :], sq4[:, :, 0], ALU.subtract).then_inc(S["map_v"], 1)
                    dve.wait_ge(S["map_v"], 2)
                    nc.vector.tensor_scalar(m_mink[:, :], m_x[:, :], 1e-8, None, ALU.max).then_inc(S["mink"], 1)
                    dve.wait_ge(S["mink"], 1)
                    nc.vector.tensor_scalar(m_x[:, :], m_mink[:, :], 1.0, None, ALU.min).then_inc(S["map_v"], 1)
                    nc.vector.tensor_scalar(m_small[:, :], m_mink[:, :], 1.0, None, ALU.is_lt).then_inc(S["map_small"], 1)
                    dve.wait_ge(S["map_v"], 3)
                    nc.vector.tensor_scalar(m_p[:, :], m_x[:, :], 1.0 / 362880, None, ALU.mult).then_inc(S["map_v"], 1)
                    for n, coeff in enumerate((1.0 / 5040, 1.0 / 120, 1.0 / 6)):
                        dve.wait_ge(S["map_v"], 4 + n)
                        nc.vector.scalar_tensor_tensor(out=m_p[:, :], in0=m_p[:, :], scalar=coeff, in1=m_x[:, :],
                                                       op0=ALU.add, op1=ALU.mult).then_inc(S["map_v"], 1)
                    dve.wait_ge(S["map_v"], 7)
                    dve.wait_ge(S["exps"], 2)
                    nc.vector.tensor_tensor(m_cosh2[:, :], m_ep[:, :], m_en[:, :], ALU.add).then_inc(S["cosh2"], 1)
                    nc.vector.tensor_tensor(m_sinh2[:, :], m_ep[:, :], m_en[:, :], ALU.subtract).then_inc(S["map_e"], 1)
                    nc.vector.reciprocal(m_rn[:, :], m_norm[:, :]).then_inc(S["map_e"], 1)
                    dve.wait_ge(S["map_e"], 2)
                    nc.vector.scalar_tensor_tensor(out=m_s[:, :], in0=m_sinh2[:, :], scalar=0.5, in1=m_rn[:, :],
                                                   op0=ALU.mult, op1=ALU.mult).then_inc(S["map_e"], 1)
                    dve.wait_ge(S["map_e"], 3)
                    nc.vector.scalar_tensor_tensor(out=m_p[:, :], in0=m_p[:, :], scalar=1.0, in1=m_s[:, :],
                                                   op0=ALU.add, op1=ALU.subtract).then_inc(S["map_e"], 1)
                    dve.wait_ge(S["map_e"], 4)
                    dve.wait_ge(S["map_small"], 1)
                    nc.vector.tensor_tensor(m_p[:, :], m_p[:, :], m_small[:, :], ALU.mult).then_inc(S["map_e"], 1)
                    dve.wait_ge(S["map_e"], 5)
                    nc.vector.tensor_tensor(m_s[:, :], m_s[:, :], m_p[:, :], ALU.add).then_inc(S["map_s"], 1)
                    dve.wait_ge(S["map_s"], 1)
                    dve.wait_ge(S["cosh2"], 1)
                    dve.wait_ge(S["spike_e"], 1)
                    nc.vector.tensor_scalar(spike_s[:, :], spike_e[:, :], 1.0, None, ALU.add).then_inc(S["spike_v"], 1)
                    dve.wait_ge(S["spike_v"], 1)
                    nc.vector.reciprocal(spike_s[:, :], spike_s[:, :]).then_inc(S["spike_v"], 1)
                    dve.wait_ge(S["spike_v"], 2)
                    nc.vector.tensor_scalar(spike[:, :], spike_s[:, :], threshold[:, 0:1], None, ALU.is_gt)\
                        .then_inc(S["spike_v"], 1)
                    dve.wait_ge(S["spike_v"], 3)
                    s4 = m_s[:, :].rearrange("q (t side h) -> q t side h", t=GT, side=2)
                    nc.vector.tensor_scalar(s4[:, :, 0, :], s4[:, :, 0, :], -1.0, None, ALU.mult).then_inc(S["map_s"], 1)
                    dve.wait_ge(S["map_s"], 2)
                    c4 = m_cosh2[:, :].rearrange("q (t side h) -> q t side h", t=GT, side=2)
                    q5 = qk[:, :, 0:2 * C].rearrange("q t (side h d) -> q t side h d", side=2, d=D)
                    pad_sg = padded[:, :, :, :, :, :].rearrange("q u side g s d -> q u side s g d")
                    for t in range(GT):
                        if t >= 2:
                            dve.wait_ge(S["strips_turned"], 2 * (t - 1))
                        by_strip = lambda ap: ap.rearrange("q (s g) d -> q s g d", s=STRIPS)
                        for side in range(2):
                            nc.vector.tensor_scalar(pad_sg[:, t % 2, side, :, :, 0],
                                                    c4[:, t, side, :].rearrange("q (s g) -> q s g", s=STRIPS), 0.5,
                                                    None, ALU.mult)
                        nc.vector.tensor_tensor(pad_sg[:, t % 2, 0, :, :, 1:D], by_strip(q5[:, t, 0, :, 1:D]),
                                                by_strip(bcast(s4[:, t, 0, :], 2, D - 1)), ALU.mult).then_inc(S["padded"], 1)
                        nc.vector.tensor_tensor(pad_sg[:, t % 2, 1, :, :, 1:D], by_strip(q5[:, t, 1, :, 1:D]),
                                                by_strip(bcast(s4[:, t, 1, :], 2, D - 1)), ALU.mult).then_inc(S["padded"], 1)
                        if t >= 1:
                            dve.wait_ge(S["strips_turned"], 2 * t)
                            nc.vector.tensor_copy(heads["lor"][1][:, :, (t - 1) * P:t * P],
                                                  bank((2 * t - 1) % 4).rearrange("r (g q) -> r g q", g=HG))\
                                .then_inc(S["strips_dve"], 1)
                    dve.wait_ge(S["strips_turned"], 2 * GT)
                    nc.vector.tensor_copy(heads["lor"][1][:, :, (GT - 1) * P:],
                                          bank((2 * GT - 1) % 4).rearrange("r (g q) -> r g q", g=HG))\
                        .then_inc(S["strips_dve"], 1)
                    for u in range(n_l + 1):
                        if u < n_l:
                            front_vector(dve, S, "lor", u, *lor_units[u])
                            lorentz_scores_vector(dve, S, "lor", u)
                        if u >= 1:
                            back_vector(dve, S, "lor", u - 1, *lor_units[u - 1])
                    dve.wait_ge(S["lor_y"], 1)
                    x_flat = x_cur[:, :, :].rearrange("q t c -> q (t c)")
                    nc.vector.tensor_tensor(x_flat, x_flat, bank(6), ALU.add).then_inc(S["lor_added"], 1)
                    dve.wait_ge(S["lor_added"], 1)
                    nc.vector.tensor_tensor(x_cur[:, :, :], x_cur[:, :, :], bcast(b_o_lor[:, :], 1, GT), ALU.add)\
                        .then_inc(S["lor_added"], 1)
                    dve.wait_ge(S["lor_added"], 2)
                    dve.wait_ge(S["ln1_turned"], GT)
                    nc.vector.tensor_copy(x_all[:, bass.ds(g * GT, GT), :], x_cur[:, :, :])
                    ln_vector(dve, S, "ln2", x_cur, x_norm)
                    for k in ("src", "tgt"):
                        dve.wait_ge(S[f"{k}_v"], 1)
                        fill_V_vector(dve, S, k, 0)
                    dve.wait_ge(S["mask_loaded"], 32)
                    for u in range(n_m + 1):
                        if u < n_m:
                            front_vector(dve, S, "mha", u, *mha_units[u])
                        if u >= 1:
                            back_vector(dve, S, "mha", u - 1, *mha_units[u - 1])

                @block.sync
                def _(sp):
                    sp.dma_start(ctx_cur[:, :, :], tiles(I["ctx_1024"])[:, bass.ds(g * GT, GT), :])\
                        .then_inc(S["ctx_loaded"], 16)
                    for half in range(2):
                        sp.dma_start(src_cur[half * SEQ:(half + 1) * SEQ, :, :],
                                     masks[half][bass.ds(g * GT, GT), :].partition_broadcast(SEQ))\
                            .then_inc(S["mask_loaded"], 16)

                @block.gpsimd
                def _(pool):
                    pool.wait_ge(S["lor_qk_sb"], GT)
                    nc.gpsimd.tensor_tensor(sq[:, :, :], qk[:, :, 0:2 * C], qk[:, :, 0:2 * C], ALU.mult)\
                        .then_inc(S["sq"], 1)
                    for u in range(n_l):
                        sc, ax = score[:, u % 2, :, :], aux[:, u % 2, :, :]
                        pool.wait_ge(S["lor_root"], u + 1)
                        nc.gpsimd.tensor_tensor(ax, ax, sc, ALU.add).then_inc(S["lor_arg"], 1)
                        pool.wait_ge(S["lor_dist"], u + 1)
                        nc.gpsimd.tensor_tensor(ax, ax, ax, ALU.mult).then_inc(S["lor_dist2"], 1)
                        shift_gpsimd(pool, S, "lor", u)
                    for u in range(n_m):
                        shift_gpsimd(pool, S, "mha", u)
            finish_phase(nc, S)


LSTM_UNROLL = 8


def phase_b(m, stack):
    nc, I, bank, gate0, gates123, lstm_wh = m.nc, m.I, m.bank, m.gate0, m.gates123, m.lstm_wh

    def sb(name, shape, where=None):
        return m.sb(name, shape, where or stack)

    w = {}
    loads = []

    def load(name, shape, *parts):
        w[name] = sb(name, shape)
        for index, src in parts:
            loads.append((w[name][index], src))

    all2, all3 = np.s_[:, :], np.s_[:, :, :]
    for tag, w1, b1, w2, b2 in (("hid0", "L0_xattn_ffn_w1", "L0_xattn_ffn_b1", "L0_xattn_ffn_w2", "L0_xattn_ffn_b2"),
                                ("hid1", "L1_xattn_w1", "L1_xattn_b1", "L1_xattn_w2", "L1_xattn_b2")):
        load(tag + "_w1", [P, HID], (all2, I[w1]))
        load(tag + "_b1", [P, HC], (all2, I[b1].rearrange("(c p) -> p c", p=P)))
        load(tag + "_w2", [P, HC, C], (all3, I[w2].rearrange("(c p) n -> p c n", p=P)))
        load(tag + "_b2", [P, 1], (all2, I[b2].unsqueeze(1)))
    for tag, name in (("moe0", "L0_ffn"), ("moe1", "L1_ffn")):
        load(tag + "_w1", [P, E, EH], (all3, I[name + "_W1"].rearrange("e c h -> c e h")))
        load(tag + "_b1", [P, E, EC], (all3, I[name + "_b1"].rearrange("e (k p) -> p e k", p=P)))
        load(tag + "_w2", [P, E * EC, C], (all3, I[name + "_W2"].rearrange("e (k p) c -> p (e k) c", p=P)))
        load(tag + "_b2", [E, C], (all2, I[name + "_b2"]))
    load("w_red", [P, RED], (all2, I["L0_ffn_w_red"]))
    load("wg", [E, RED], (all2, I["L0_ffn_wg"]))
    load("gate_w", [P, E], (all2, I["L1_ffn_gate_W"]))
    load("fw_q", [P, TW], (all2, I["L1_attn_wq"]))
    load("fw_k", [P, TW], (all2, I["L1_attn_wk"]))
    load("fw_t", [P, TW], (all2, I["L1_attn_wv"]))
    load("fw_o", [P, PAIRS, C], (all3, I["L1_attn_wo"].rearrange("(p r) c -> r p c", r=P)))
    load("fw_theta", [P, PAIRS], (all2, I["L1_attn_theta"].rearrange("(p two) c one -> (two c) (p one)", two=2)))
    load("fw_theta_b", [P, H], (all2, row(I["L1_attn_theta_bias"])))
    load("fw_b", [P, TW], (all2, row(I["L1_attn_b1"])))
    load("fw_g2", [P, TW], (all2, row(I["L1_attn_gamma"])))
    load("fw_gbe", [P, TW], (all2, row(I["L1_attn_beta"])))
    load("fw_g_col", [P, PAIRS], (all2, I["L1_attn_gamma"].rearrange("(p two) one d -> (two d) (p one)", two=2)))
    load("fw_be_col", [P, PAIRS], (all2, I["L1_attn_beta"].rearrange("(p two) one d -> (two d) (p one)", two=2)))
    load("fw_alpha", [P, 1], *[(np.s_[half * TD:half * TD + TD, :], I["L1_attn_alpha"].unsqueeze(1))
                               for half in range(2)])
    for n in (1, 2, 3):
        load(f"ln_g{n}", [P, C], (all2, row(I[f"L1_xattn_g{n}"])))
        load(f"ln_b{n}", [P, C], (all2, row(I[f"L1_xattn_beta{n}"])))
    w["fw_w1"] = m.x_norm[:, :, :].rearrange("q t c -> q (t c)").rearrange("q (p d) -> q p d", p=PAIRS)
    loads.append((w["fw_w1"], I["L1_attn_W1"].rearrange("(p two) c d -> (two c) p d", two=2)))

    with ExitStack() as mem:
        h = sb("lstm_h", [P, BATCH], mem)
        c = sb("lstm_c", [P, BATCH], mem)
        pre = sb("lstm_pre", [P, GATES, BATCH], mem)
        cand = sb("lstm_cand", [P, BATCH], mem)
        sig = sb("lstm_sig", [P, GATES - 1, BATCH], mem)
        kept = sb("lstm_kept", [P, BATCH], mem)
        new = sb("lstm_new", [P, BATCH], mem)
        c_tanh = sb("lstm_c_tanh", [P, BATCH], mem)
        with ExitStack() as sems:
            S = Signals(nc, sems)
            with nc.Block() as block:
                @block.sync
                def _(sp):
                    for dst, src in loads:
                        sp.dma_start(dst, src).then_inc(S["weights_loaded"], 16)
                    sp.wait_ge(S["weights_loaded"], 16 * len(loads))

                @block.vector
                def _(dve):
                    nc.vector.memset(h[:, :], 0.0)
                    nc.vector.memset(c[:, :], 0.0)
            finish_phase(nc, S)

        at0 = gate0[:, :].rearrange("c (b s) -> c b s", s=SEQ)
        at123 = gates123.rearrange("c j (b s) -> c j b s", s=SEQ)
        with ExitStack() as sems:
            S = Signals(nc, sems)
            with nc.Fori(0, SEQ // LSTM_UNROLL) as i:
                with nc.Block() as block:
                    @block.tensor
                    def _(pe):
                        for k in range(LSTM_UNROLL):
                            if k >= 1:
                                pe.wait_ge(S["h"], k)
                            for n, j in enumerate(GATE_ORDER):
                                nc.tensor.matmul(bank(2 * (k % 2) + (n > 0))[:, n * BATCH:(n + 1) * BATCH],
                                                 lstm_wh[:, j * C:(j + 1) * C], h[:, :],
                                                 start=True, stop=True).then_inc(S["gate_h"], 1)

                    @block.vector
                    def _(dve):
                        for k in range(LSTM_UNROLL):
                            step = i * LSTM_UNROLL + k
                            dve.wait_ge(S["gate_h"], GATES * k + 1)
                            nc.vector.tensor_tensor(pre[:, 0, :], bank(2 * (k % 2))[:, 0:BATCH],
                                                    at0[:, :, bass.ds(step, 1)].rearrange("c b s -> c (b s)"),
                                                    ALU.add).then_inc(S["pre_cand"], 1)
                            dve.wait_ge(S["gate_h"], GATES * k + 4)
                            nc.vector.tensor_tensor(pre[:, 1:, :], bank(2 * (k % 2) + 1)[:, BATCH:GATES * BATCH].rearrange(
                                                        "c (j b) -> c j b", b=BATCH),
                                                    at123[:, :, :, bass.ds(step, 1)].rearrange("c j b s -> c j (b s)"),
                                                    ALU.add).then_inc(S["pre_gates"], 1)
                            dve.wait_ge(S["cand"], k + 1)
                            dve.wait_ge(S["gates"], k + 1)
                            nc.vector.tensor_tensor(kept[:, :], sig[:, 1, :], c[:, :], ALU.mult)\
                                .then_inc(S["kept"], 1)
                            nc.vector.tensor_tensor(new[:, :], sig[:, 0, :], cand[:, :], ALU.mult)\
                                .then_inc(S["new"], 1)
                            dve.wait_ge(S["kept"], k + 1)
                            dve.wait_ge(S["new"], k + 1)
                            nc.vector.tensor_tensor(c[:, :], kept[:, :], new[:, :], ALU.add).then_inc(S["c"], 1)
                            dve.wait_ge(S["c_tanh"], k + 1)
                            if k >= 1:
                                dve.wait_ge(S["h_stored"], k)
                            nc.vector.tensor_tensor(h[:, :], sig[:, 2, :], c_tanh[:, :], ALU.mult)\
                                .then_inc(S["h"], 1)

                    @block.scalar
                    def _(act):
                        for k in range(LSTM_UNROLL):
                            act.wait_ge(S["pre_cand"], k + 1)
                            nc.scalar.activation(cand[:, :], pre[:, 0, :], ACT.Tanh).then_inc(S["cand"], 1)
                            act.wait_ge(S["pre_gates"], k + 1)
                            nc.scalar.activation(sig[:, :, :], pre[:, 1:, :], ACT.Sigmoid).then_inc(S["gates"], 1)
                            act.wait_ge(S["c"], k + 1)
                            nc.scalar.activation(c_tanh[:, :], c[:, :], ACT.Tanh).then_inc(S["c_tanh"], 1)

                    @block.gpsimd
                    def _(pool):
                        for k in range(LSTM_UNROLL):
                            step = i * LSTM_UNROLL + k
                            pool.wait_ge(S["h"], k + 1)
                            nc.gpsimd.tensor_copy(at0[:, :, bass.ds(step, 1)].rearrange("c b s -> c (b s)"), h[:, :])\
                                .then_inc(S["h_stored"], 1)
                finish_phase(nc, S)

    for name, shape in (("wg_nT", [RED, E]), ("sel", [E, E, P]), ("rank", [P, E]), ("block_mask", [P, P]),
                        ("causal_mask", [P, P]), ("fw_z", [P, TW]), ("fw_zq", [P, TW]), ("fw_go", [P, PAIRS, C]),
                        ("fw_qo", [P, C]), ("fw_beo", [P, C]), ("fw_lr", [P, H]), ("token_eta", [P, 1]),
                        ("ones_row", [1, P])):
        w[name] = sb(name, shape)
    return w


def prepare_c(m, w):
    nc, pair, bank, ident = m.nc, m.pair, m.bank, m.ident
    with ExitStack() as mem, ExitStack() as sems:
        S = Signals(nc, sems)

        def sb(name, shape):
            return m.sb(name, shape, mem)

        arena = m.arena
        wkT = arena[:, 0:1024].rearrange("r (p c) -> r p c", p=PAIRS)
        wqT = arena[:, 1024:2048].rearrange("r (p c) -> r p c", p=PAIRS)
        be_mat = arena[:, 2048:3072].rearrange("r (p q) -> r p q", p=PAIRS)
        mean = arena[:, 3072:3120].rearrange("q (n h) -> q n h", n=3)
        wg_sq = arena[0:E, 3200:3216]
        wg_v = arena[0:E, 3216:3224]
        by_bank = lambda ap: ap.rearrange("q (two p d) -> q p two d", two=2, p=PAIRS)
        pos_i = sb("pos_i", [P, 1])
        pos = sb("pos", [P, 1])
        by_head = lambda ap: ap.rearrange("q (h d) -> q h d", h=H)

        with nc.Block() as block:
            @block.tensor
            def _(pe):
                for p in range(PAIRS):
                    tr = nc.tensor.transpose(pair[0][:, p * P:(p + 1) * P], w["fw_k"][:, p * P:(p + 1) * P], ident[:, :])
                tr.then_inc(S["wk_turned"], 1)
                for p in range(PAIRS):
                    tr = nc.tensor.transpose(pair[1][:, p * P:(p + 1) * P], w["fw_q"][:, p * P:(p + 1) * P], ident[:, :])
                tr.then_inc(S["wq_turned"], 1)
                pe.wait_ge(S["wkT"], 1)
                pe.wait_ge(S["wqT"], 1)
                for dst, src, done in ((2, wkT, "wk_w1"), (3, wqT, "wq_w1")):
                    for h in range(H):
                        rows = slice(TD * (h % 2), TD * (h % 2) + TD)
                        mm = nc.tensor.matmul(bank(2 * dst + h % 2)[:, (h // 2) * TD:(h // 2 + 1) * TD], src[rows, h // 2, :],
                                              w["fw_w1"][rows, h // 2, :], start=True, stop=True)
                    mm.then_inc(S[done], 1)
                for h in range(H):
                    rows = slice(TD * (h % 2), TD * (h % 2) + TD)
                    mm = nc.tensor.matmul(bank(h % 2)[:, h // 2:h // 2 + 1], wkT[rows, h // 2, :],
                                          w["fw_theta"][rows, h // 2:h // 2 + 1], start=True, stop=True)
                mm.then_inc(S["wk_theta"], 1)
                for p in range(PAIRS):
                    mm = nc.tensor.matmul(bank(2)[:, 0:C], wqT[:, p, :], w["fw_o"][:, p, :],
                                          start=(p == 0), stop=(p == PAIRS - 1))
                mm.then_inc(S["wq_wo"], 1)
                pe.wait_ge(S["be_mat"], 1)
                for p in range(PAIRS):
                    mm = nc.tensor.matmul(bank(3)[:, 0:C], be_mat[:, p, :], w["fw_o"][:, p, :],
                                          start=(p == 0), stop=(p == PAIRS - 1))
                mm.then_inc(S["be_wo"], 1)
                pe.wait_ge(S["wg_n"], 1)
                pe.wait_ge(S["wk_theta_sb"], 1)
                nc.tensor.transpose(bank(0)[0:RED, 128:128 + E], w["wg"][:, :], ident[0:E, 0:E])\
                    .then_inc(S["wg_turned"], 1)

            @block.scalar
            def _(act):
                act.wait_ge(S["wk_turned"], 1)
                nc.scalar.activation(wkT, pair[0].rearrange("r (p c) -> r p c", p=PAIRS), ACT.Copy)\
                    .then_inc(S["wkT"], 1)
                act.wait_ge(S["wq_turned"], 1)
                nc.scalar.activation(wqT, pair[1].rearrange("r (p c) -> r p c", p=PAIRS), ACT.Copy)\
                    .then_inc(S["wqT"], 1)
                act.wait_ge(S["wg_norm2"], 1)
                nc.scalar.activation(wg_v[:, 1:2], wg_v[:, 0:1], ACT.Ln).then_inc(S["wg_log"], 1)
                act.wait_ge(S["wg_log"], 1)
                nc.scalar.activation(wg_v[:, 2:3], wg_v[:, 1:2], ACT.Exp, scale=0.5).then_inc(S["wg_norm"], 1)
                act.wait_ge(S["wk_theta"], 1)
                nc.scalar.activation(w["fw_lr"][:, :].rearrange("q (p two) -> q two p", two=2),
                                     m.four_banks[:, 0:2, 0:PAIRS], ACT.Copy).then_inc(S["wk_theta_sb"], 1)
                act.wait_ge(S["wq_wo"], 1)
                nc.scalar.activation(w["fw_qo"][:, :], bank(2)[:, 0:C], ACT.Copy)
                act.wait_ge(S["be_wo"], 1)
                nc.scalar.activation(w["fw_beo"][:, :], bank(3)[:, 0:C], ACT.Copy)
                act.wait_ge(S["wg_turned"], 1)
                nc.scalar.activation(w["wg_nT"][:, :], bank(0)[0:RED, 128:128 + E], ACT.Copy)

            @block.vector
            def _(dve):
                nc.vector.tensor_copy(be_mat, bcast(w["fw_be_col"][:, :], 2, P)).then_inc(S["be_mat"], 1)
                nc.vector.tensor_tensor(wg_sq, w["wg"][:, :], w["wg"][:, :], ALU.mult).then_inc(S["wg_v"], 1)
                dve.wait_ge(S["wg_v"], 1)
                nc.vector.tensor_reduce(wg_v[:, 3:4], wg_sq, AX_X, ALU.add).then_inc(S["wg_v"], 1)
                dve.wait_ge(S["wg_v"], 2)
                nc.vector.tensor_scalar(wg_v[:, 0:1], wg_v[:, 3:4], 1e-18, None, ALU.max).then_inc(S["wg_norm2"], 1)
                dve.wait_ge(S["wg_norm"], 1)
                nc.vector.tensor_scalar(wg_v[:, 4:5], wg_v[:, 2:3], 1e-4, None, ALU.max).then_inc(S["wg_v"], 1)
                dve.wait_ge(S["wg_v"], 3)
                nc.vector.reciprocal(wg_v[:, 5:6], wg_v[:, 4:5]).then_inc(S["wg_v"], 1)
                dve.wait_ge(S["wg_v"], 4)
                nc.vector.tensor_scalar(w["wg"][:, :], w["wg"][:, :], wg_v[:, 5:6], None, ALU.mult)\
                    .then_inc(S["wg_n"], 1)
                nc.vector.tensor_tensor(w["fw_t"][:, :], w["fw_k"][:, :], w["fw_t"][:, :], ALU.subtract)\
                    .then_inc(S["fold"], 1)
                nc.vector.tensor_tensor(w["fw_gbe"][:, :], w["fw_gbe"][:, :], w["fw_g2"][:, :], ALU.mult)
                dve.wait_ge(S["fold"], 1)
                nc.vector.tensor_tensor(w["fw_t"][:, :], w["fw_t"][:, :], w["fw_g2"][:, :], ALU.mult)\
                    .then_inc(S["fold"], 1)
                dve.wait_ge(S["fold"], 2)
                nc.vector.tensor_tensor(w["fw_g2"][:, :], w["fw_g2"][:, :], w["fw_g2"][:, :], ALU.mult)
                nc.vector.tensor_tensor(w["fw_go"][:, :, :], w["fw_o"][:, :, :], bcast(w["fw_g_col"][:, :], 2, C), ALU.mult)
                nc.vector.tensor_reduce(mean[:, 0, :], by_head(w["fw_b"][:, :]), AX_X, ALU.add).then_inc(S["mean"], 1)
                dve.wait_ge(S["wk_w1"], 1)
                nc.vector.tensor_reduce(mean[:, 1, :].rearrange("q (p two) -> q p two", two=2), by_bank(pair[2]), AX_X, ALU.add).then_inc(S["mean"], 1)
                dve.wait_ge(S["wq_w1"], 1)
                nc.vector.tensor_reduce(mean[:, 2, :].rearrange("q (p two) -> q p two", two=2), by_bank(pair[3]), AX_X, ALU.add).then_inc(S["mean"], 1)
                dve.wait_ge(S["mean"], 3)
                nc.vector.tensor_scalar(mean, mean, 1.0 / TD, None, ALU.mult).then_inc(S["mean"], 1)
                dve.wait_ge(S["mean"], 4)
                nc.vector.tensor_tensor(by_head(w["fw_b"][:, :]), by_head(w["fw_b"][:, :]), bcast(mean[:, 0, :], 2, TD),
                                        ALU.subtract)
                for n, (dst, src) in enumerate(((w["fw_z"], pair[2]), (w["fw_zq"], pair[3])), start=1):
                    in_pairs = lambda ap: ap.rearrange("q (p two) d -> q p two d", two=2)
                    nc.vector.tensor_tensor(in_pairs(by_head(dst[:, :])), by_bank(src),
                                            in_pairs(bcast(mean[:, n, :], 2, TD)), ALU.subtract)
                dve.wait_ge(S["pos"], 2)
                nc.vector.tensor_copy(pos[:, :], pos_i[:, :].bitcast(mybir.dt.int32)).then_inc(S["pos_v"], 1)
                dve.wait_ge(S["pos_v"], 1)
                nc.vector.reciprocal(pos[:, :], pos[:, :]).then_inc(S["pos_v"], 1)
                dve.wait_ge(S["pos_v"], 2)
                nc.vector.tensor_scalar(w["token_eta"][:, :], pos[:, :], w["fw_alpha"][:, 0:1], 0.0, ALU.add, ALU.max)\
                    .then_inc(S["pos_v"], 1)
                dve.wait_ge(S["pos_v"], 3)
                nc.vector.tensor_scalar(w["token_eta"][:, :], w["token_eta"][:, :], -1.0 / TD, None, ALU.mult)

            @block.gpsimd
            def _(pool):
                for half in range(2):
                    if half == 1:
                        pool.wait_ge(S["pos"], 1)
                    nc.gpsimd.iota(pos_i[half * SEQ:(half + 1) * SEQ, :].bitcast(mybir.dt.int32), pattern=[[0, 1]],
                                   base=1, channel_multiplier=1).then_inc(S["pos"], 1)
                pool.wait_ge(S["pos"], 2)
                nc.gpsimd.memset(w["ones_row"][:, :], 1.0)
                for e in range(E):
                    nc.gpsimd.memset(w["rank"][:, e:e + 1], float(E - e))
                nc.gpsimd.memset(w["sel"][:, :, :], 0.0).then_inc(S["cleared"], 1)
                nc.gpsimd.memset(w["block_mask"][:, :], NEG).then_inc(S["cleared"], 1)
                pool.wait_ge(S["cleared"], 2)
                nc.gpsimd.affine_select(out=w["sel"][:, :, :], in_=w["sel"][:, :, :], compare_op=ALU.not_equal,
                                        fill=1.0, base=0, pattern=[[-1, E], [0, P]], channel_multiplier=1)\
                    .then_inc(S["sel_made"], 1)
                pool.wait_ge(S["sel_made"], 1)
                for half in range(2):
                    if half == 1:
                        pool.wait_ge(S["cleared"], 3)
                    rows = slice(half * SEQ, (half + 1) * SEQ)
                    nc.gpsimd.memset(w["block_mask"][rows, rows], 0.0).then_inc(S["cleared"], 1)
                pool.wait_ge(S["cleared"], 4)
                nc.gpsimd.affine_select(out=w["causal_mask"][:, :], in_=w["block_mask"][:, :], compare_op=ALU.is_ge,
                                        fill=NEG, base=0, pattern=[[-1, P]], channel_multiplier=1)
        finish_phase(nc, S)


def phase_c(m, w):
    nc, I, tiles, pair, bank, ident, arena = m.nc, m.I, m.tiles, m.pair, m.bank, m.ident, m.arena
    x_all, gate0, x_cur, ctx_cur, x_norm = m.x_all, m.gate0, m.x_cur, m.ctx_cur, m.x_norm
    ln_vector, ln_scalar, transpose_tiles = m.ln_vector, m.ln_scalar, m.transpose_tiles
    x_flat = x_cur[:, :, :].rearrange("q t c -> q (t c)")

    def part(at, n):
        return arena[:, at:at + n]

    hid = part(0, HC * GN).rearrange("k (c n) -> k c n", c=HC)
    yT = part(2048, GN)
    exp_hid = part(0, 2 * EC * GN).rearrange("k (u c n) -> k u c n", u=2, c=EC)
    cwT = part(2560, GN)
    redT = part(3072, GN)
    cw = part(3584, 10 * GT * E).rearrange("q (k t e) -> q k t e", k=10, t=GT)
    cw_s = part(3904, 10 * GT).rearrange("q (k t) -> q k t", k=10)
    fw_qT = part(0, PAIRS * GN).rearrange("r (p n) -> r p n", p=PAIRS)
    fw_kT = part(4096, PAIRS * GN).rearrange("r (p n) -> r p n", p=PAIRS)
    z, sqr, unit, grad = (part(8192 + 1024 * n, 1024) for n in range(4))
    xT = m.sb("c_xT", [P, GN], m.stack_c)
    h_cur = m.sb("h_cur", [P, GN], m.stack_c)
    SA = m.sb("fw_A", [P, H, SEQ], m.stack_c)
    zq = m.sb("fw_zq_sb", [P, TW], m.stack_c)
    sqq = m.sb("fw_sqq", [P, TW], m.stack_c)
    turned = m.sb("fw_turned", [P, PAIRS, P], m.stack_c)
    small = m.sb("fw_small", [P, 12, H], m.stack_c)
    eta = m.sb("fw_eta", [P, GT, H], m.stack_c)
    y = part(0, GT * C).rearrange("q (t c) -> q t c", t=GT)
    att = part(512, GT * P).rearrange("q (t k) -> q t k", t=GT)
    attT = part(1024, GN)
    ctxT = part(1536, GN)
    att_s = part(2048 + 512, 4 * GT).rearrange("q (k t) -> q k t", k=4)
    xhid = part(4096, HC * GN).rearrange("k (c n) -> k c n", c=HC)
    yT2 = part(3072, GN)
    by_head = lambda ap: ap.rearrange("q (h d) -> q h d", h=H)

    def lnT_scalar(act, S, tag):
        act.wait_ge(S[f"{tag}_turned"], GT)
        nc.scalar.activation(xT[:, :], bank(7), ACT.Copy).then_inc(S[f"{tag}_T"], 1)

    def dense_tensor(pe, S, tag, src, src_ready):
        pe.wait_ge(S[src_ready], 1)
        for c in range(HC):
            nc.tensor.matmul(bank(c), w[tag + "_w1"][:, c * P:(c + 1) * P], src, start=True, stop=True)\
                .then_inc(S[f"{tag}_pre"], 1)
        for c in range(HC):
            pe.wait_ge(S[f"{tag}_hid"], c + 1)
            mm = nc.tensor.matmul(bank(4), w[tag + "_w2"][:, c, :], hid_of[tag][:, c, :],
                                  start=(c == 0), stop=(c == HC - 1))
        mm.then_inc(S[f"{tag}_y"], 1)
        back_tensor(pe, S, tag, yT_of[tag])

    def dense_scalar(act, S, tag):
        for c in range(HC):
            act.wait_ge(S[f"{tag}_pre"], c + 1)
            nc.scalar.activation(hid_of[tag][:, c, :], bank(c), ACT.Relu, bias=w[tag + "_b1"][:, c:c + 1])\
                .then_inc(S[f"{tag}_hid"], 1)
        act.wait_ge(S[f"{tag}_y"], 1)
        nc.scalar.activation(yT_of[tag], bank(4), ACT.Identity, bias=w[tag + "_b2"][:, 0:1])\
            .then_inc(S[f"{tag}_yT"], 1)

    def back_tensor(pe, S, tag, src):
        pe.wait_ge(S[f"{tag}_yT"], 1)
        for t in range(GT):
            tr = nc.tensor.transpose(bank(5)[:, t * P:(t + 1) * P], src[:, t * P:(t + 1) * P], ident[:, :])
        tr.then_inc(S[f"{tag}_back"], 1)

    hid_of = {"hid0": hid, "hid1": xhid}
    yT_of = {"hid0": yT, "hid1": yT2}

    def experts_tensor(pe, S, tag):
        pe.wait_ge(S[f"{tag}_cw"], 1)
        for t in range(GT):
            tr = nc.tensor.transpose(bank(6)[0:E, t * P:(t + 1) * P], cw[:, 0, t, :], ident[:, :])
        tr.then_inc(S[f"{tag}_cw_turned"], 1)
        pe.wait_ge(S[f"{tag}_cwT"], 1)
        nc.tensor.matmul(bank(6), w[tag + "_b2"][:, :], cwT[0:E, :], start=True, stop=False)
        for e in range(E + 1):
            if e < E:
                if e >= 2:
                    pe.wait_ge(S[f"{tag}_scaled"], EC * (e - 1))
                nc.tensor.matmul(bank(4 + e % 2), w["sel"][:, e, :], cwT[0:E, :], start=True, stop=True)\
                    .then_inc(S[f"{tag}_cw_rows"], 1)
                for c in range(EC):
                    i = EC * e + c
                    if e >= 2:
                        pe.wait_ge(S[f"{tag}_act"], i - 3)
                    nc.tensor.matmul(bank(i % 4), w[tag + "_w1"][:, e, c * P:(c + 1) * P], xT[:, :],
                                     start=True, stop=True).then_inc(S[f"{tag}_pre"], 1)
            if e >= 1:
                for c in range(EC):
                    i = EC * (e - 1) + c
                    pe.wait_ge(S[f"{tag}_scaled"], i + 1)
                    nc.tensor.matmul(bank(6), w[tag + "_w2"][:, i, :], exp_hid[:, (e - 1) % 2, c, :],
                                     start=False, stop=(i == E * EC - 1)).then_inc(S[f"{tag}_used"], 1)
        back_tensor(pe, S, tag, yT)

    def experts_scalar(act, S, tag, func):
        act.wait_ge(S[f"{tag}_cw_turned"], 1)
        nc.scalar.activation(cwT[0:E, :], bank(6)[0:E, :], ACT.Copy).then_inc(S[f"{tag}_cwT"], 1)
        for i in range(E * EC):
            e, c = divmod(i, EC)
            act.wait_ge(S[f"{tag}_pre"], i + 1)
            if e >= 2:
                act.wait_ge(S[f"{tag}_used"], i - 3)
            nc.scalar.activation(exp_hid[:, e % 2, c, :], bank(i % 4), func, bias=w[tag + "_b1"][:, e, c:c + 1])\
                .then_inc(S[f"{tag}_act"], 1)
        act.wait_ge(S[f"{tag}_used"], E * EC)
        nc.scalar.activation(yT, bank(6), ACT.Copy).then_inc(S[f"{tag}_yT"], 1)

    def experts_vector(dve, S, tag):
        for i in range(E * EC):
            e, c = divmod(i, EC)
            dve.wait_ge(S[f"{tag}_cw_rows"], e + 1)
            dve.wait_ge(S[f"{tag}_act"], i + 1)
            nc.vector.tensor_tensor(exp_hid[:, e % 2, c, :], exp_hid[:, e % 2, c, :], bank(4 + e % 2), ALU.mult)\
                .then_inc(S[f"{tag}_scaled"], 1)
        dve.wait_ge(S[f"{tag}_back"], 1)
        nc.vector.tensor_tensor(x_flat, x_flat, bank(5), ALU.add).then_inc(S[f"{tag}_added"], 1)

    def first_of_max(dve, S, tag, values, top, tmp, key, hot, n0):
        nc.vector.tensor_reduce(top, values, AX_X, ALU.max).then_inc(S[f"{tag}_sel"], 1)
        dve.wait_ge(S[f"{tag}_sel"], n0 + 1)
        nc.vector.tensor_tensor(tmp, values, bcast(top, 2, E), ALU.is_equal).then_inc(S[f"{tag}_sel"], 1)
        dve.wait_ge(S[f"{tag}_sel"], n0 + 2)
        nc.vector.tensor_tensor(tmp, tmp, bcast(w["rank"][:, :], 1, GT), ALU.mult).then_inc(S[f"{tag}_sel"], 1)
        dve.wait_ge(S[f"{tag}_sel"], n0 + 3)
        nc.vector.tensor_reduce(key, tmp, AX_X, ALU.max).then_inc(S[f"{tag}_sel"], 1)
        dve.wait_ge(S[f"{tag}_sel"], n0 + 4)
        nc.vector.tensor_tensor(hot, tmp, bcast(key, 2, E), ALU.is_equal).then_inc(S[f"{tag}_sel"], 1)
        dve.wait_ge(S[f"{tag}_sel"], n0 + 5)

    def gate_exps_vector(dve, S, tag):
        dve.wait_ge(S[f"{tag}_logits"], 1)
        nc.vector.tensor_copy(cw[:, 1], bank(1)[:, 0:GT * E].rearrange("q (t e) -> q t e", t=GT))\
            .then_inc(S[f"{tag}_logits_sb"], 1)
        dve.wait_ge(S[f"{tag}_logits_sb"], 1)
        first_of_max(dve, S, tag, cw[:, 1], cw_s[:, 0], cw[:, 2], cw_s[:, 1], cw[:, 3], 0)
        nc.vector.tensor_tensor(cw[:, 4], cw[:, 1], bcast(cw_s[:, 0], 2, E), ALU.subtract)\
            .then_inc(S[f"{tag}_less_max"], 1)
        dve.wait_ge(S[f"{tag}_exp"], 1)
        nc.vector.tensor_reduce(cw_s[:, 2], cw[:, 5], AX_X, ALU.add).then_inc(S[f"{tag}_gate"], 1)
        dve.wait_ge(S[f"{tag}_gate"], 1)
        nc.vector.reciprocal(cw_s[:, 3], cw_s[:, 2]).then_inc(S[f"{tag}_gate"], 1)
        dve.wait_ge(S[f"{tag}_gate"], 2)

    def gate_exps_scalar(act, S, tag):
        act.wait_ge(S[f"{tag}_less_max"], 1)
        nc.scalar.activation(cw[:, 5], cw[:, 4], ACT.Exp).then_inc(S[f"{tag}_exp"], 1)

    def attend_tensor(pe, S, tag, kT, values):
        for t in range(GT):
            mm = nc.tensor.matmul(bank(0)[:, t * P:(t + 1) * P], xT[:, t * P:(t + 1) * P], kT[:, t * P:(t + 1) * P],
                                  start=True, stop=True)
        mm.then_inc(S[f"{tag}_score"], 1)
        pe.wait_ge(S[f"{tag}_prob"], 1)
        for t in range(GT):
            tr = nc.tensor.transpose(bank(1)[:, t * P:(t + 1) * P], att[:, t, :], ident[:, :])
        tr.then_inc(S[f"{tag}_turned"], 1)
        pe.wait_ge(S[f"{tag}_probT"], 1)
        for t in range(GT):
            mm = nc.tensor.matmul(bank(2)[:, t * P:(t + 1) * P], attT[:, t * P:(t + 1) * P], values[:, t, :],
                                  start=True, stop=True)
        mm.then_inc(S[f"{tag}_pv"], 1)

    def attend_scalar(act, S, tag):
        act.wait_ge(S[f"{tag}_less_max"], 1)
        nc.scalar.activation(att, att, ACT.Exp).then_inc(S[f"{tag}_prob"], 1)
        act.wait_ge(S[f"{tag}_turned"], 1)
        nc.scalar.activation(attT, bank(1), ACT.Copy).then_inc(S[f"{tag}_probT"], 1)

    def attend_vector(dve, S, tag, mask):
        dve.wait_ge(S[f"{tag}_score"], 1)
        nc.vector.scalar_tensor_tensor(out=att, in0=bank(0).rearrange("q (t k) -> q t k", t=GT), scalar=INV_SQRT_C,
                                       in1=bcast(w[mask][:, :], 1, GT), op0=ALU.mult, op1=ALU.add)\
            .then_inc(S[f"{tag}_masked"], 1)
        dve.wait_ge(S[f"{tag}_masked"], 1)
        nc.vector.tensor_reduce(att_s[:, 0], att, AX_X, ALU.max).then_inc(S[f"{tag}_max"], 1)
        dve.wait_ge(S[f"{tag}_max"], 1)
        nc.vector.tensor_tensor(att, att, bcast(att_s[:, 0], 2, P), ALU.subtract).then_inc(S[f"{tag}_less_max"], 1)
        dve.wait_ge(S[f"{tag}_prob"], 1)
        nc.vector.tensor_reduce(att_s[:, 1], att, AX_X, ALU.add).then_inc(S[f"{tag}_sum"], 1)
        dve.wait_ge(S[f"{tag}_sum"], 1)
        nc.vector.reciprocal(att_s[:, 2], att_s[:, 1]).then_inc(S[f"{tag}_rec"], 1)
        dve.wait_ge(S[f"{tag}_rec"], 1)
        dve.wait_ge(S[f"{tag}_pv"], 1)
        nc.vector.tensor_tensor(x_norm[:, :, :], bank(2).rearrange("q (t c) -> q t c", t=GT),
                                bcast(att_s[:, 2], 2, C), ALU.mult).then_inc(S[f"{tag}_out"], 1)
        dve.wait_ge(S[f"{tag}_out"], 1)
        nc.vector.tensor_tensor(y, y, x_norm[:, :, :], ALU.add).then_inc(S[f"{tag}_added"], 1)
        dve.wait_ge(S[f"{tag}_added"], 1)

    def fast_tensor(pe, S):
        pe.wait_ge(S["ln4_T"], 1)
        for j in range(2 * PAIRS):
            p, side = divmod(j, 2)
            if j >= 4:
                pe.wait_ge(S["fw_heads_act" if side == 0 else "fw_heads_dve"], j // 2 - 1)
            nc.tensor.matmul(bank(j % 4), w["fw_q" if side == 0 else "fw_k"][:, p * P:(p + 1) * P], xT[:, :],
                             start=True, stop=True).then_inc(S["fw_heads"], 1)
        for t in range(GT):
            mm = nc.tensor.matmul(bank(7)[:, t * H:(t + 1) * H], xT[:, t * P:(t + 1) * P], w["fw_lr"][:, :],
                                  start=True, stop=True)
        mm.then_inc(S["fw_lr"], 1)
        pe.wait_ge(S["fw_heads_act"], PAIRS)
        pe.wait_ge(S["fw_heads_dve"], PAIRS)
        for t in range(GT + 1):
            if t < GT:
                x_tile = xT[:, t * P:(t + 1) * P]
                if t >= 2:
                    pe.wait_ge(S["fw_turned_act"], t - 1)
                for half in range(2):
                    cols = slice(half * 512, half * 512 + 512)
                    mm = nc.tensor.matmul(pair[0][:, cols], x_tile, w["fw_z"][:, cols], start=True, stop=True)
                mm.then_inc(S["fw_z"], 1)
                if t >= 1:
                    pe.wait_ge(S["fw_gxh"], t)
                if t >= 2:
                    pe.wait_ge(S["fw_x"], t - 1)
                for half in range(2):
                    cols = slice(half * 512, half * 512 + 512)
                    nc.tensor.matmul(pair[1][:, cols], x_tile, w["fw_t"][:, cols], start=True, stop=False)
                    mm = nc.tensor.matmul(pair[1][:, cols], w["ones_row"][:, :], w["fw_gbe"][0:1, cols],
                                          start=False, stop=True)
                mm.then_inc(S["fw_t"], 1)
                if t >= 1:
                    pe.wait_ge(S["fw_A"], t)
                for b in range(2):
                    for h in range(H):
                        rows, cols = slice(TD * (h % 2), TD * (h % 2) + TD), slice((2 * t + b) * SEQ, (2 * t + b + 1) * SEQ)
                        mm = nc.tensor.matmul(bank(4 + h % 2)[b * SEQ:(b + 1) * SEQ, (h // 2) * SEQ:(h // 2 + 1) * SEQ],
                                              fw_kT[rows, h // 2, cols], fw_qT[rows, h // 2, cols],
                                              start=True, stop=True)
                mm.then_inc(S["fw_kq"], 1)
            if t >= 1:
                last = t - 1
                pe.wait_ge(S["fw_unit2"], last + 1)
                pe.wait_ge(S["fw_z_sb"], min(t + 1, GT))
                for p in range(PAIRS):
                    tr = nc.tensor.transpose(pair[0][:, p * P:(p + 1) * P], zq[:, p * P:(p + 1) * P], ident[:, :])
                tr.then_inc(S["fw_turned"], 1)
                pe.wait_ge(S["fw_turned_act"], last + 1)
                pe.wait_ge(S["fw_gxh"], min(t + 1, GT))
                for p in range(PAIRS):
                    nc.tensor.matmul(bank(2)[:, 0:C], turned[:, p, :], w["fw_go"][:, p, :], start=(p == 0), stop=False)
                nc.tensor.matmul(bank(2)[:, 0:C], xT[:, last * P:(last + 1) * P], w["fw_qo"][:, :],
                                 start=False, stop=True).then_inc(S["fw_y"], 1)
            if t < GT:
                if t == 0:
                    pe.wait_ge(S["fw_lr_e"], 1)
                else:
                    pe.wait_ge(S["fw_zq_sb"], t)
                for half in range(2):
                    cols = slice(half * 512, half * 512 + 512)
                    nc.tensor.matmul(pair[3][:, cols], x_tile, w["fw_zq"][:, cols], start=True, stop=False,
                                     skip_group_check=True)
                pe.wait_ge(S["fw_A"], t + 1)
                pe.wait_ge(S["fw_step"], t + 1)
                for b in range(2):
                    rows = slice(b * SEQ, (b + 1) * SEQ)
                    for h in range(H):
                        mm = nc.tensor.matmul(pair[3][rows, h * TD:(h + 1) * TD], SA[rows, h, :],
                                              grad[rows, h * TD:(h + 1) * TD], start=False,
                                              stop=(b == 1 and h in (H // 2 - 1, H - 1)), skip_group_check=True)
                mm.then_inc(S["fw_zq"], 1)

    def fast_scalar(act, S):
        for p in range(PAIRS):
            act.wait_ge(S["fw_heads"], 2 * p + 1)
            nc.scalar.activation(fw_qT[:, p, :], bank((2 * p) % 4), ACT.Copy).then_inc(S["fw_heads_act"], 1)
        act.wait_ge(S["fw_lr_in"], 1)
        nc.scalar.activation(eta[:, :, :], eta[:, :, :], ACT.Exp, scale=-1.0).then_inc(S["fw_lr_e"], 1)

        def rstd(src, log, dst, ready, count, tag):
            act.wait_ge(S[ready], count)
            nc.scalar.activation(log, src, ACT.Ln, bias=m.eps6[:, 0:1], scale=1.0 / TD).then_inc(S[f"{tag}_log"], 1)
            act.wait_ge(S[f"{tag}_log"], count)
            nc.scalar.activation(dst, log, ACT.Exp, scale=-0.5).then_inc(S[f"{tag}_rstd"], 1)

        for t in range(GT + 1):
            if t < GT:
                act.wait_ge(S["fw_z_sb"], t + 1)
                if t >= 1:
                    act.wait_ge(S["fw_step"], t)
                nc.scalar.activation(sqr, z, ACT.Square).then_inc(S["fw_sqr"], 1)
                rstd(small[:, 0, :], small[:, 1, :], small[:, 2, :], "fw_var", t + 1, "fw1")
                act.wait_ge(S["fw_kq"], t + 1)
                nc.scalar.activation(SA[:, :, :].rearrange("k (p two) q -> k two p q", two=2),
                                     pair[2].rearrange("k (two p q) -> k two p q", two=2, p=PAIRS), ACT.Identity,
                                     bias=m.one[:, 0:1]).then_inc(S["fw_A"], 1)
            if t >= 1:
                act.wait_ge(S["fw_zq_sb"], t)
                nc.scalar.activation(sqq[:, :], zq[:, :], ACT.Square).then_inc(S["fw_sqq"], 1)
                rstd(small[:, 3, :], small[:, 4, :], small[:, 5, :], "fw_var2", t, "fw2")
                act.wait_ge(S["fw_turned"], t)
                nc.scalar.activation(turned[:, :, :], pair[0].rearrange("r (p q) -> r p q", p=PAIRS), ACT.Copy)\
                    .then_inc(S["fw_turned_act"], 1)

    def fast_vector(dve, S):
        for p in range(PAIRS):
            dve.wait_ge(S["fw_heads"], 2 * p + 2)
            nc.vector.tensor_copy(fw_kT[:, p, :], bank((2 * p + 1) % 4)).then_inc(S["fw_heads_dve"], 1)
        dve.wait_ge(S["fw_lr"], 1)
        nc.vector.tensor_tensor(eta[:, :, :], bank(7)[:, 0:GT * H].rearrange("q (t h) -> q t h", t=GT),
                                bcast(w["fw_theta_b"][:, :], 1, GT), ALU.add).then_inc(S["fw_lr_in"], 1)
        dve.wait_ge(S["fw_lr_e"], 1)
        nc.vector.tensor_scalar(eta[:, :, :], eta[:, :, :], 1.0, None, ALU.add).then_inc(S["fw_eta"], 1)
        dve.wait_ge(S["fw_eta"], 1)
        nc.vector.reciprocal(eta[:, :, :], eta[:, :, :]).then_inc(S["fw_eta"], 1)
        dve.wait_ge(S["fw_eta"], 2)
        nc.vector.tensor_scalar(eta[:, :, :], eta[:, :, :], w["token_eta"][:, 0:1], None, ALU.mult)\
            .then_inc(S["fw_eta"], 1)
        dve.wait_ge(S["fw_eta"], 3)
        for t in range(GT + 1):
            if t < GT:
                dve.wait_ge(S["fw_z"], t + 1)
                nc.vector.tensor_tensor(z, pair[0][:, :], w["fw_b"][:, :], ALU.add).then_inc(S["fw_z_sb"], 1)
                dve.wait_ge(S["fw_sqr"], t + 1)
                nc.vector.tensor_reduce(small[:, 0, :], by_head(sqr), AX_X, ALU.add).then_inc(S["fw_var"], 1)
                dve.wait_ge(S["fw_t"], t + 1)
                dve.wait_ge(S["fw_gx"], t + 1)
                nc.vector.tensor_tensor(grad, grad, pair[1][:, :], ALU.add).then_inc(S["fw_gxh"], 1)
                dve.wait_ge(S["fw_gxh"], t + 1)
                nc.vector.tensor_reduce(small[:, 6, :], by_head(grad), AX_X, ALU.add).then_inc(S["fw_s1"], 1)
                dve.wait_ge(S["fw_p"], t + 1)
                nc.vector.tensor_reduce(small[:, 7, :], by_head(sqr), AX_X, ALU.add).then_inc(S["fw_s2"], 1)
                dve.wait_ge(S["fw1_rstd"], t + 1)
                nc.vector.tensor_tensor(small[:, 8, :], eta[:, t, :], small[:, 2, :], ALU.mult).then_inc(S["fw_coef"], 1)
                dve.wait_ge(S["fw_s1"], t + 1)
                dve.wait_ge(S["fw_s2"], t + 1)
                nc.vector.tensor_scalar(small[:, 6:8, :], small[:, 6:8, :], 1.0 / TD, None, ALU.mult)\
                    .then_inc(S["fw_means"], 1)
                dve.wait_ge(S["fw_means"], t + 1)
                nc.vector.tensor_tensor(by_head(grad), by_head(grad), bcast(small[:, 6, :], 2, TD), ALU.subtract)\
                    .then_inc(S["fw_less"], 1)
                dve.wait_ge(S["fw_less"], 2 * t + 1)
                dve.wait_ge(S["fw_u"], t + 1)
                nc.vector.tensor_tensor(grad, grad, sqr, ALU.subtract).then_inc(S["fw_less"], 1)
                dve.wait_ge(S["fw_less"], 2 * t + 2)
                dve.wait_ge(S["fw_coef"], t + 1)
                nc.vector.tensor_tensor(by_head(grad), by_head(grad), bcast(small[:, 8, :], 2, TD), ALU.mult)\
                    .then_inc(S["fw_step"], 1)
            if t >= 1:
                dve.wait_ge(S["fw_zq"], t)
                if t >= 2:
                    dve.wait_ge(S["fw_turned"], t - 1)
                nc.vector.tensor_tensor(zq[:, :], pair[3][:, :], w["fw_b"][:, :], ALU.add).then_inc(S["fw_zq_sb"], 1)
                dve.wait_ge(S["fw_sqq"], t)
                nc.vector.tensor_reduce(small[:, 3, :], by_head(sqq[:, :]), AX_X, ALU.add).then_inc(S["fw_var2"], 1)
                dve.wait_ge(S["fw_y"], t)
                nc.vector.tensor_tensor(x_cur[:, t - 1, :], x_cur[:, t - 1, :], bank(2)[:, 0:C], ALU.add)\
                    .then_inc(S["fw_x"], 1)
        dve.wait_ge(S["fw_x"], GT)
        nc.vector.tensor_tensor(x_cur[:, :, :], x_cur[:, :, :], bcast(w["fw_beo"][:, :], 1, GT), ALU.add)\
            .then_inc(S["fw_added"], 1)
        dve.wait_ge(S["fw_added"], 1)

    def fast_gpsimd(pool, S):
        for t in range(GT + 1):
            if t < GT:
                pool.wait_ge(S["fw1_rstd"], t + 1)
                nc.gpsimd.tensor_tensor(by_head(unit), by_head(z), bcast(small[:, 2, :], 2, TD), ALU.mult)\
                    .then_inc(S["fw_unit"], 1)
                pool.wait_ge(S["fw_unit"], t + 1)
                if t >= 1:
                    pool.wait_ge(S["fw_zq"], t)
                nc.gpsimd.tensor_tensor(grad, unit, w["fw_g2"][:, :], ALU.mult).then_inc(S["fw_gx"], 1)
                pool.wait_ge(S["fw_gxh"], t + 1)
                nc.gpsimd.tensor_tensor(sqr, grad, unit, ALU.mult).then_inc(S["fw_p"], 1)
                pool.wait_ge(S["fw_means"], t + 1)
                nc.gpsimd.tensor_tensor(by_head(sqr), by_head(unit), bcast(small[:, 7, :], 2, TD), ALU.mult)\
                    .then_inc(S["fw_u"], 1)
            if t >= 1:
                pool.wait_ge(S["fw2_rstd"], t)
                nc.gpsimd.tensor_tensor(by_head(zq[:, :]), by_head(zq[:, :]), bcast(small[:, 5, :], 2, TD), ALU.mult)\
                    .then_inc(S["fw_unit2"], 1)

    with ExitStack() as sems:
        S = Signals(nc, sems)
        with nc.Fori(0, GROUPS) as g:
            with nc.Block() as block:
                @block.tensor
                def _(pe):
                    dense_tensor(pe, S, "hid0", h_cur[:, :], "h_cur")
                    transpose_tiles(pe, S, "ln_unit", lambda t: GT * LN_TURN["ln3"] + t + 1, x_norm, bank(7), "ln3_turned")
                    pe.wait_ge(S["ln3_T"], 1)
                    nc.tensor.matmul(bank(0)[0:RED, :], w["w_red"][:, :], xT[:, :], start=True, stop=True)\
                        .then_inc(S["red"], 1)
                    pe.wait_ge(S["redT"], 1)
                    for t in range(GT):
                        mm = nc.tensor.matmul(bank(1)[:, t * E:(t + 1) * E], redT[0:RED, t * P:(t + 1) * P],
                                              w["wg_nT"][:, :], start=True, stop=True)
                    mm.then_inc(S["moe0_logits"], 1)
                    experts_tensor(pe, S, "moe0")
                    transpose_tiles(pe, S, "ln_unit", lambda t: GT * LN_TURN["ln4"] + t + 1, x_norm, bank(7), "ln4_turned")
                    fast_tensor(pe, S)

                @block.scalar
                def _(act):
                    dense_scalar(act, S, "hid0")
                    ln_scalar(act, S, "ln3")
                    lnT_scalar(act, S, "ln3")
                    act.wait_ge(S["red"], 1)
                    nc.scalar.activation(redT[0:RED, :], bank(0)[0:RED, :], ACT.Copy).then_inc(S["redT"], 1)
                    gate_exps_scalar(act, S, "moe0")
                    experts_scalar(act, S, "moe0", ACT.Gelu)
                    ln_scalar(act, S, "ln4")
                    lnT_scalar(act, S, "ln4")
                    fast_scalar(act, S)

                @block.vector
                def _(dve):
                    nc.vector.tensor_copy(x_cur[:, :, :], x_all[:, bass.ds(g * GT, GT), :]).then_inc(S["x_cur"], 1)
                    dve.wait_ge(S["x_cur"], 1)
                    dve.wait_ge(S["hid0_back"], 1)
                    nc.vector.tensor_tensor(x_flat, x_flat, bank(5), ALU.add).then_inc(S["hid0_added"], 1)
                    dve.wait_ge(S["hid0_added"], 1)
                    ln_vector(dve, S, "ln3", x_cur, x_norm)
                    gate_exps_vector(dve, S, "moe0")
                    nc.vector.tensor_tensor(cw[:, 0], cw[:, 3], bcast(cw_s[:, 3], 2, E), ALU.mult)\
                        .then_inc(S["moe0_cw"], 1)
                    experts_vector(dve, S, "moe0")
                    dve.wait_ge(S["moe0_added"], 1)
                    ln_vector(dve, S, "ln4", x_cur, x_norm)
                    fast_vector(dve, S)
                    nc.vector.tensor_copy(x_all[:, bass.ds(g * GT, GT), :], x_cur[:, :, :])

                @block.gpsimd
                def _(pool):
                    nc.gpsimd.tensor_copy(h_cur[:, :], gate0[:, bass.ds(g * GN, GN)]).then_inc(S["h_cur"], 1)
                    fast_gpsimd(pool, S)
            finish_phase(nc, S)

    with ExitStack() as sems:
        S = Signals(nc, sems)
        with nc.Fori(0, GROUPS) as g:
            with nc.Block() as block:
                @block.sync
                def _(sp):
                    sp.dma_start(ctx_cur[:, :, :], tiles(I["ctx_1024"])[:, bass.ds(g * GT, GT), :])\
                        .then_inc(S["ctx_loaded"], 16)
                    sp.wait_ge(S["result"], 1)
                    sp.dma_start(tiles(m.out)[:, bass.ds(g * GT, GT), :], x_cur[:, :, :]).then_inc(S["stored"], 16)
                    sp.wait_ge(S["stored"], 16)

                @block.tensor
                def _(pe):
                    transpose_tiles(pe, S, "ln_unit", lambda t: GT * LN_TURN["ln5"] + t + 1, y, bank(7), "ln5_turned")
                    pe.wait_ge(S["ctx_loaded"], 16)
                    for t in range(GT):
                        tr = nc.tensor.transpose(bank(3)[:, t * P:(t + 1) * P], ctx_cur[:, t, :], ident[:, :])
                    tr.then_inc(S["ctx_turned"], 1)
                    pe.wait_ge(S["ln5_T"], 1)
                    attend_tensor(pe, S, "self", xT, y)
                    transpose_tiles(pe, S, "g1_done", lambda t: 1, y, bank(7), "g1_turned")
                    pe.wait_ge(S["g1_T"], 1)
                    pe.wait_ge(S["ctx_T"], 1)
                    attend_tensor(pe, S, "cross", ctxT, ctx_cur)
                    transpose_tiles(pe, S, "g2_done", lambda t: 1, y, bank(7), "g2_turned")
                    dense_tensor(pe, S, "hid1", xT[:, :], "g2_T")
                    transpose_tiles(pe, S, "ln_unit", lambda t: GT * LN_TURN["ln6"] + t + 1, x_norm, bank(7), "ln6_turned")
                    pe.wait_ge(S["ln6_T"], 1)
                    for t in range(GT):
                        mm = nc.tensor.matmul(bank(1)[:, t * E:(t + 1) * E], xT[:, t * P:(t + 1) * P],
                                              w["gate_w"][:, :], start=True, stop=True)
                    mm.then_inc(S["moe1_logits"], 1)
                    experts_tensor(pe, S, "moe1")

                @block.scalar
                def _(act):
                    ln_scalar(act, S, "ln5")
                    lnT_scalar(act, S, "ln5")
                    act.wait_ge(S["ctx_turned"], 1)
                    nc.scalar.activation(ctxT, bank(3), ACT.Copy).then_inc(S["ctx_T"], 1)
                    attend_scalar(act, S, "self")
                    ln_scalar(act, S, "g1")
                    lnT_scalar(act, S, "g1")
                    attend_scalar(act, S, "cross")
                    ln_scalar(act, S, "g2")
                    lnT_scalar(act, S, "g2")
                    dense_scalar(act, S, "hid1")
                    ln_scalar(act, S, "g3")
                    ln_scalar(act, S, "ln6")
                    lnT_scalar(act, S, "ln6")
                    gate_exps_scalar(act, S, "moe1")
                    experts_scalar(act, S, "moe1", ACT.Relu)

                @block.vector
                def _(dve):
                    nc.vector.tensor_copy(x_cur[:, :, :], x_all[:, bass.ds(g * GT, GT), :]).then_inc(S["x_cur"], 1)
                    dve.wait_ge(S["x_cur"], 1)
                    ln_vector(dve, S, "ln5", x_cur, y)
                    dve.wait_ge(S["ln_unit"], GT * (LN_TURN["ln5"] + 1))
                    attend_vector(dve, S, "self", "causal_mask")
                    ln_vector(dve, S, "g1", y, y, (w["ln_g1"][:, :], w["ln_b1"][:, :]))
                    dve.wait_ge(S["g1_done"], 1)
                    attend_vector(dve, S, "cross", "block_mask")
                    ln_vector(dve, S, "g2", y, y, (w["ln_g2"][:, :], w["ln_b2"][:, :]))
                    dve.wait_ge(S["g2_done"], 1)
                    dve.wait_ge(S["hid1_back"], 1)
                    dve.wait_ge(S["g2_turned"], GT)
                    nc.vector.tensor_tensor(y, y, bank(5).rearrange("q (t c) -> q t c", t=GT), ALU.add)\
                        .then_inc(S["hid1_added"], 1)
                    dve.wait_ge(S["hid1_added"], 1)
                    ln_vector(dve, S, "g3", y, y, (w["ln_g3"][:, :], w["ln_b3"][:, :]))
                    dve.wait_ge(S["g3_done"], 1)
                    nc.vector.tensor_tensor(x_cur[:, :, :], x_cur[:, :, :], y, ALU.add).then_inc(S["x5"], 1)
                    dve.wait_ge(S["x5"], 1)
                    ln_vector(dve, S, "ln6", x_cur, x_norm)
                    gate_exps_vector(dve, S, "moe1")
                    nc.vector.scalar_tensor_tensor(out=cw[:, 6], in0=cw[:, 3], scalar=NEG, in1=cw[:, 1],
                                                   op0=ALU.mult, op1=ALU.add).then_inc(S["without_first"], 1)
                    dve.wait_ge(S["without_first"], 1)
                    first_of_max(dve, S, "moe1", cw[:, 6], cw_s[:, 4], cw[:, 2], cw_s[:, 5], cw[:, 7], 5)
                    nc.vector.tensor_tensor(cw[:, 8], cw[:, 3], cw[:, 7], ALU.add).then_inc(S["choose"], 1)
                    dve.wait_ge(S["choose"], 1)
                    nc.vector.tensor_tensor(cw[:, 8], cw[:, 8], cw[:, 5], ALU.mult).then_inc(S["choose"], 1)
                    dve.wait_ge(S["choose"], 2)
                    nc.vector.tensor_tensor(cw[:, 8], cw[:, 8], bcast(cw_s[:, 3], 2, E), ALU.mult)\
                        .then_inc(S["choose"], 1)
                    dve.wait_ge(S["choose"], 3)
                    nc.vector.tensor_reduce(cw_s[:, 6], cw[:, 8], AX_X, ALU.add).then_inc(S["choose"], 1)
                    dve.wait_ge(S["choose"], 4)
                    nc.vector.tensor_scalar(cw_s[:, 7], cw_s[:, 6], 1e-8, None, ALU.add).then_inc(S["choose"], 1)
                    dve.wait_ge(S["choose"], 5)
                    nc.vector.reciprocal(cw_s[:, 8], cw_s[:, 7]).then_inc(S["choose"], 1)
                    dve.wait_ge(S["choose"], 6)
                    nc.vector.tensor_tensor(cw[:, 0], cw[:, 8], bcast(cw_s[:, 8], 2, E), ALU.mult)\
                        .then_inc(S["moe1_cw"], 1)
                    experts_vector(dve, S, "moe1")
                    dve.wait_ge(S["moe1_added"], 1)
                    nc.vector.tensor_tensor(x_cur[:, :, :], x_cur[:, :, :], x_norm[:, :, :], ALU.add)\
                        .then_inc(S["result"], 1)
            finish_phase(nc, S)


_OUTS = [((BATCH, SEQ, C), "float32")]


def kernel(**inputs):
    import numpy as _np
    import concourse.bacc as _bacc
    from concourse import mybir as _mybir
    from concourse.bass_utils import run_bass_kernel_spmd as _run

    nc = _bacc.Bacc("TRN2", target_bir_lowering=False, num_devices=1)
    arrays, args = {}, {}
    for name in inputs:
        a = _np.ascontiguousarray(inputs[name])
        if a.ndim == 0:
            a = a.reshape(1)
        if name == "L0_xattn_tgt_bias":
            a = a.reshape(SEQ, SEQ)
        arrays[f"in_{name}_dram"] = a
        args[name] = nc.dram_tensor(f"in_{name}_dram", a.shape, _mybir.dt.from_np(a.dtype), kind="ExternalInput").ap()
    outs = [nc.dram_tensor(f"out_{i}_dram", shape, _mybir.dt.from_np(_np.dtype(dtype)), kind="ExternalOutput").ap()
            for i, (shape, dtype) in enumerate(_OUTS)]
    build(nc, args, outs[0])
    r = _run(nc, [arrays], core_ids=[0])
    return r.results[0]["out_0_dram"]
```

```python
from contextlib import ExitStack

import numpy as np

import concourse.bass as bass
from concourse import mybir

F32 = mybir.dt.float32
BF16 = mybir.dt.bfloat16
ACT = mybir.ActivationFunctionType
ALU = mybir.AluOpType
AX_X = mybir.AxisListType.X

P = 128
C = 128
SEQ = 64
BATCH = 64
TOKENS = SEQ * BATCH
TILES = TOKENS // P
GT = 4
GB = 2 * GT
GN = GT * P
GROUPS = TILES // GT
H = 16
D = C // H
STRIPS = 4
HG = H // STRIPS
PAIRS = H // 2
BUFFERS = 3
PARTS = 3
PART_ROWS = 32 * PARTS
PW = 2 * D + 2
GATES = 4
GATE_ORDER = (1, 0, 2, 3)
HID = 512
HC = HID // P
E = 8
EH = 256
EC = EH // P
RED = 16
TD = 64
TW = H * TD
LN_TURN = {"ln1": 0, "ln2": 1, "ln3": 0, "ln4": 1, "ln5": 0, "g1": 1, "g2": 2, "g3": 3, "ln6": 4}
NEG = -1e30
LN_AND_EXP = "natural_log_exp_and_others"
INV_SQRT_D = float(1.0 / np.sqrt(D))
INV_SQRT_C = float(1.0 / np.sqrt(C))


class Signals:

    def __init__(self, nc, stack):
        self.nc, self.stack, self.made = nc, stack, {}

    def __getitem__(self, name):
        if name not in self.made:
            self.made[name] = self.stack.enter_context(self.nc.semaphore(name))
        return self.made[name]

    def runs(self):
        nums = sorted(s.num for s in self.made.values())
        starts = [n for n in nums if n - 1 not in nums]
        ends = [n + 1 for n in nums if n + 1 not in nums]
        return [range(a, b) for a, b in zip(starts, ends)]


class Shared:

    def __init__(self, four_banks, nc, I, out, sb, tiles, pair, bank, x_all, gate0, gates123, arena, ident, eps5, eps6, one, x_cur,
                 ctx_cur, x_norm, lstm_wh, ln_vector, ln_scalar, transpose_tiles):
        self.nc, self.I, self.out, self.sb, self.tiles, self.pair, self.bank = nc, I, out, sb, tiles, pair, bank
        self.x_all, self.gate0, self.gates123, self.arena, self.ident = x_all, gate0, gates123, arena, ident
        self.eps5, self.eps6, self.one, self.x_cur, self.ctx_cur, self.x_norm = eps5, eps6, one, x_cur, ctx_cur, x_norm
        self.lstm_wh, self.ln_vector, self.ln_scalar = lstm_wh, ln_vector, ln_scalar
        self.transpose_tiles, self.four_banks = transpose_tiles, four_banks


def bcast(ap, axis, count):
    a = ap.unsqueeze(axis)
    shape = list(a.shape)
    shape[axis] = count
    return a.broadcast_to(shape)


def finish_phase(nc, signals):
    for run in signals.runs():
        nc.multi_engine_barrier(list(nc.engines), sems_to_clear=run)


def build(nc, I, out):
    with ExitStack() as whole, nc.allow_non_contiguous_dma(reason="bias columns and padded heads, once"):
        _build(nc, I, out, whole)


def _build(nc, I, out, whole):
    def sb(name, shape, stack=whole, dtype=F32):
        return stack.enter_context(nc.sbuf_tensor(name, shape, dtype))

    tiles = lambda ap: ap.rearrange("b s d -> (b s) d").rearrange("(t p) d -> p t d", p=P)

    lower = whole.enter_context(nc.psum_tensor("lower_banks", [P, 4, 512], F32))
    upper = whole.enter_context(nc.psum_tensor("upper_banks", [P, 4, 512], F32))
    pair = [half[:, 2 * i:2 * i + 2, :].rearrange("p k n -> p (k n)") for half in (lower, upper) for i in range(2)]

    def bank(i):
        return pair[i // 2][:, (i % 2) * 512:(i % 2) * 512 + 512]

    x_all = sb("x_all", [P, TILES, C])
    gate0 = sb("gate0", [P, TOKENS])
    ident = sb("ident", [P, P])
    eps5 = sb("eps5", [P, 1])
    eps6 = sb("eps6", [P, 1])
    x_cur = sb("x_cur", [P, GT, C])
    ctx_cur = sb("ctx_cur", [P, GT, C])
    x_norm = sb("x_norm", [P, GT, C])
    ln_stats = sb("ln_stats", [P, GT, 6])
    ln_moments = sb("ln_moments", [P, GT, 2])
    ln_logvar = sb("ln_logvar", [P, GT])
    ln_rstd = sb("ln_rstd", [P, GT])
    lstm_wh = sb("lstm_wh", [P, GATES * C])
    one = sb("one", [P, 1])
    arena = sb("arena", [P, (GATES - 1) * TOKENS])

    def ln_vector(e, S, tag, src, dst, affine=None):
        n = LN_TURN[tag]
        for t in range(GT):
            nc.vector.bn_stats(ln_stats[:, t, :], src[:, t, :]).then_inc(S["ln_stats"], 1)
        for t in range(GT):
            e.wait_ge(S["ln_stats"], GT * n + t + 1)
            nc.vector.bn_aggr(ln_moments[:, t, :], ln_stats[:, t, :]).then_inc(S["ln_moments"], 1)
        e.wait_ge(S["ln_rstd"], n + 1)
        for t in range(GT):
            nc.vector.tensor_scalar(dst[:, t, :], src[:, t, :], ln_moments[:, t, 0:1], ln_rstd[:, t:t + 1],
                                    ALU.subtract, ALU.mult).then_inc(S["ln_unit"], 1)
        if affine is not None:
            gain, shift = affine
            e.wait_ge(S["ln_unit"], GT * (n + 1))
            nc.vector.tensor_tensor(dst, dst, bcast(gain, 1, GT), ALU.mult).then_inc(S[f"{tag}_gained"], 1)
            e.wait_ge(S[f"{tag}_gained"], 1)
            nc.vector.tensor_tensor(dst, dst, bcast(shift, 1, GT), ALU.add).then_inc(S[f"{tag}_done"], 1)

    def ln_scalar(e, S, tag):
        n = LN_TURN[tag]
        e.wait_ge(S["ln_moments"], GT * (n + 1))
        nc.scalar.activation(ln_logvar[:, :], ln_moments[:, :, 1], ACT.Ln, bias=eps5[:, 0:1])\
            .then_inc(S["ln_logvar"], 1)
        e.wait_ge(S["ln_logvar"], n + 1)
        nc.scalar.activation(ln_rstd[:, :], ln_logvar[:, :], ACT.Exp, scale=-0.5).then_inc(S["ln_rstd"], 1)

    def transpose_tiles(e, S, ready, ready_count, src, dst_bank, done):
        for t in range(GT):
            e.wait_ge(S[ready], ready_count(t))
            nc.tensor.transpose(dst_bank[:, t * P:(t + 1) * P], src[:, t, :], ident[:, :]).then_inc(S[done], 1)

    gates123 = arena[:, :].rearrange("p (j n) -> p j n", j=GATES - 1)
    m = Shared(lower, nc, I, out, sb, tiles, pair, bank, x_all, gate0, gates123, arena, ident, eps5, eps6, one, x_cur, ctx_cur,
               x_norm, lstm_wh, ln_vector, ln_scalar, transpose_tiles)
    with ExitStack() as mem_a:
        phase_a(m, mem_a)
    with ExitStack() as mem_c:
        m.stack_c = mem_c
        w = phase_b(m, mem_c)
        prepare_c(m, w)
        phase_c(m, w)


def row(ap):
    n = len(ap.shape)
    flat = ap if n == 1 else ap.rearrange({2: "a b -> (a b)", 3: "a b c -> (a b c)"}[n])
    return flat.partition_broadcast(P)


def phase_a(m, stack):
    four_banks = m.four_banks
    nc, I, tiles, pair, bank, ident = m.nc, m.I, m.tiles, m.pair, m.bank, m.ident
    x_all, gate0, gates123, x_cur, ctx_cur, x_norm = m.x_all, m.gate0, m.gates123, m.x_cur, m.ctx_cur, m.x_norm
    eps5, eps6, one, lstm_wh = m.eps5, m.eps6, m.one, m.lstm_wh
    ln_vector, ln_scalar, transpose_tiles = m.ln_vector, m.ln_scalar, m.transpose_tiles

    def sb(name, shape):
        return m.sb(name, shape, stack)

    w_qk = sb("w_qk", [P, 2 * C + 1])
    b_qk = sb("b_qk", [P, 2 * C + 1])
    w_v = {k: sb(f"w_v_{k}", [P, C]) for k in ("lor", "src", "tgt")}
    b_v = {k: sb(f"b_v_{k}", [P, C]) for k in ("lor", "src", "tgt")}
    w_o = {k: sb(f"w_o_{k}", [P, C]) for k in ("lor", "src", "tgt")}
    b_o_lor = sb("b_o_lor", [P, C])
    w_head = {k + s: sb(f"w_head_{k}_{s}", [P, C]) for k in ("src", "tgt") for s in "qk"}
    b_head = {k + s: sb(f"b_head_{k}_{s}", [P, 1]) for k in ("src", "tgt") for s in "qk"}
    b_k_masked = {k: sb(f"b_k_masked_{k}", [P, HG]) for k in ("src", "tgt")}
    head_mask = sb("head_mask", [P, HG])
    head_rows = sb("head_rows", [P, STRIPS, HG])
    b_o_col = sb("b_o_col", [P, 2])
    b_o_sum = sb("b_o_sum", [P, 1])
    lstm_wx = sb("lstm_wx", [P, 2, GATES * C])
    lstm_b = sb("lstm_b", [P, GATES])
    threshold = sb("threshold", [P, 1])
    tgt_bias = sb("tgt_bias", [P, SEQ])
    causal = sb("causal", [P, SEQ])

    xT = sb("xT", [P, GB, 2, SEQ])
    ctxT = sb("ctxT", [P, GB, 2, SEQ])
    x_once = sb("x_once", [P, GN])
    qk = sb("qk", [P, GT, 2 * C + 1])
    n_h = GT * 2 * H
    m_mink, m_log, m_norm, m_ep, m_en, m_cosh2, m_sinh2, m_rn, m_s, m_p, m_small, m_x = (
        sb(f"map_{n}", [P, n_h]) for n in ("mink", "log", "norm", "ep", "en", "cosh2", "sinh2", "rn", "s", "p",
                                            "small", "x"))
    spike_e = sb("spike_e", [P, GT])
    spike_s = sb("spike_s", [P, GT])
    spike = sb("spike", [P, GT])
    mapped = sb("mapped", [P, GT, 2, C])
    heads = {k: (sb(f"qT_{k}", [P, GN]), sb(f"kT_{k}", [P, GB, HG, SEQ])) for k in ("tgt", "src")}
    heads["lor"] = heads["tgt"]
    V = {k: sb(f"V_{k}", [P, GB, PAIRS, PW]) for k in ("src", "tgt")}
    V["lor"] = V["tgt"]
    score = sb("score", [P, BUFFERS, H, SEQ])
    aux = sb("aux", [P, BUFFERS, H, SEQ])
    sq = heads["src"][1][:, 0:GT, :, :].rearrange("p t g k -> p t (g k)")
    row_max = sb("row_max", [P, BUFFERS, H])
    PT = sb("PT", [P, PAIRS, P])
    row_rec = sb("row_rec", [P, PAIRS, 2])
    o_tm = {k: sb(f"o_tm_{k}", [P, GT, C]) for k in ("lor", "src")}
    o_tm["tgt"] = o_tm["lor"]
    oT = {k: sb(f"oT_{k}", [P, GN]) for k in ("src", "tgt")}
    cT = sb("cT", [P, GN])

    with ExitStack() as sems:
        S = Signals(nc, sems)
        loads = [
            (x_all[:, :, :], tiles(I["x"])),
            (w_qk[:, 0:2 * C], I["L0_attn_W_qkv"][:, 0:2 * C]),
            (w_qk[:, 2 * C:], I["L0_attn_w_sur"].unsqueeze(1)),
            (b_qk[:, 0:2 * C], row(I["L0_attn_b_qkv"][0:2 * C])),
            (b_qk[:, 2 * C:], row(I["L0_attn_b_sur"])),
            (threshold[:, :], row(I["L0_attn_threshold"])),
            (w_v["lor"][:, :], I["L0_attn_W_qkv"][:, 2 * C:]),
            (b_v["lor"][:, :], row(I["L0_attn_b_qkv"][2 * C:])),
            (w_o["lor"][:, :], I["L0_attn_W_out"]),
            (b_o_lor[:, :], row(I["L0_attn_b_out"])),
            (lstm_wx[:, :, :], I["L0_xattn_lstm_w"][0:2 * C, :].rearrange("(k p) n -> p k n", p=P)),
            (lstm_wh[:, :], I["L0_xattn_lstm_w"][2 * C:, :]),
            (lstm_b[:, :], I["L0_xattn_lstm_b"].rearrange("(c p) -> p c", p=P)),
        ]
        for n, k in enumerate(("src", "tgt")):
            loads += [(w_v[k][:, :], I[f"L0_xattn_{k}_wv"]), (b_v[k][:, :], row(I[f"L0_xattn_{k}_bv"])),
                      (w_o[k][:, :], I[f"L0_xattn_{k}_wo"]),
                      (b_o_col[:, n:n + 1], I[f"L0_xattn_{k}_bo"].unsqueeze(1))]
            for s in "qk":
                loads += [(w_head[k + s][:, :], I[f"L0_xattn_{k}_w{s}"]),
                          (b_head[k + s][:, :], I[f"L0_xattn_{k}_b{s}"].unsqueeze(1))]
        for half in range(2):
            rows = slice(half * SEQ, half * SEQ + SEQ)
            loads += [(tgt_bias[rows, :], I["L0_xattn_tgt_bias"])]
        with nc.Block() as block:
            @block.sync
            def _(sp):
                for dst, src in loads:
                    sp.dma_start(dst, src).then_inc(S["inputs_loaded"], 16)
                sp.wait_ge(S["inputs_loaded"], 16 * len(loads))

            @block.vector
            def _(dve):
                nc.vector.memset(eps5[:, :], 1e-5)
                nc.vector.memset(eps6[:, :], 1e-6)
                nc.vector.memset(one[:, :], 1.0)
                for k in ("src", "tgt"):
                    nc.vector.memset(V[k][:, :, :, :], 0.0).then_inc(S["V_cleared"], 1)
                dve.wait_ge(S["V_cleared"], 2)
                for k in ("src", "tgt"):
                    for half in range(2):
                        rows = slice(half * SEQ, half * SEQ + SEQ)
                        col = 2 * D + half
                        nc.vector.memset(V[k][rows, :, :, col:col + 1], 1.0)
                dve.wait_ge(S["head_rows"], 3)
                nc.vector.tensor_reduce(head_mask[:, :], head_rows[:, :, :].rearrange("c s g -> c g s"), AX_X, ALU.add)\
                    .then_inc(S["head_mask"], 1)
                dve.wait_ge(S["head_mask"], 1)
                dve.wait_ge(S["inputs_loaded"], 16 * len(loads))
                for k in ("src", "tgt"):
                    nc.vector.tensor_scalar(b_k_masked[k][:, :], head_mask[:, :], b_head[k + "k"][:, 0:1], None, ALU.mult)
                nc.vector.tensor_tensor(b_o_sum[:, :], b_o_col[:, 0:1], b_o_col[:, 1:2], ALU.add)
                for k in ("srcq", "tgtq"):
                    nc.vector.tensor_scalar(b_head[k][:, :], b_head[k][:, :], INV_SQRT_D, None, ALU.mult)

            @block.gpsimd
            def _(pool):
                nc.gpsimd.memset(ident[:, :], 0.0).then_inc(S["ident_cleared"], 1)
                nc.gpsimd.memset(causal[:, :], 0.0).then_inc(S["causal_cleared"], 1)
                nc.gpsimd.memset(head_rows[:, :, :], 1.0).then_inc(S["head_rows"], 1)
                by_h = head_rows[:, :, :].rearrange("c s g -> c (s g)")
                pool.wait_ge(S["head_rows"], 1)
                nc.gpsimd.affine_select(out=by_h, in_=by_h, compare_op=ALU.is_ge, fill=0.0, base=0,
                                        pattern=[[-D, H]], channel_multiplier=1).then_inc(S["head_rows"], 1)
                pool.wait_ge(S["head_rows"], 2)
                nc.gpsimd.affine_select(out=by_h, in_=by_h, compare_op=ALU.is_ge, fill=0.0, base=D - 1,
                                        pattern=[[D, H]], channel_multiplier=-1).then_inc(S["head_rows"], 1)
                pool.wait_ge(S["ident_cleared"], 1)
                nc.gpsimd.affine_select(out=ident[:, :], in_=ident[:, :], compare_op=ALU.not_equal, fill=1.0,
                                        base=0, pattern=[[-1, P]], channel_multiplier=1)\
                    .then_inc(S["ident_made"], 1)
                pool.wait_ge(S["causal_cleared"], 1)
                for half in range(2):
                    rows = slice(half * SEQ, half * SEQ + SEQ)
                    pool.wait_ge(S["ident_made"], half + 1)
                    nc.gpsimd.affine_select(out=causal[rows, :], in_=causal[rows, :], compare_op=ALU.is_ge, fill=NEG,
                                            base=0, pattern=[[-1, SEQ]], channel_multiplier=1)\
                        .then_inc(S["ident_made"], 1)
        finish_phase(nc, S)

    def scores_tensor(e, S, tag, u, kind, t):
        qT, kT = heads[kind]
        if u >= 1:
            e.wait_ge(S[f"{tag}_score_read"], u)
        for b in range(2):
            for s in range(STRIPS):
                rows, cols = slice(32 * s, 32 * s + 32), slice((2 * t + b) * SEQ, (2 * t + b + 1) * SEQ)
                mm = nc.tensor.matmul(bank(s)[b * SEQ:(b + 1) * SEQ, 0:HG * SEQ], qT[rows, cols],
                                      kT[rows, 2 * t + b, :, :].rearrange("r g k -> r (g k)"), start=True, stop=True)
        mm.then_inc(S[f"{tag}_score"], 1)

    def turn_tensor(e, S, tag, u):
        e.wait_ge(S[f"{tag}_prob"], u + 1)
        for half in range(2):
            if u >= 1:
                e.wait_ge(S[f"{tag}_PT_act" if half == 0 else f"{tag}_PT_dve"], u)
            for p in range(4 * half, 4 * half + 4):
                tr = nc.tensor.transpose(pair[2][:, p * P:(p + 1) * P], score[:, u % BUFFERS, 2 * p:2 * p + 2, :],
                                         ident[:, :])
            tr.then_inc(S[f"{tag}_turned"], 1)

    def values_tensor(e, S, tag, u, kind, t):
        e.wait_ge(S[f"{tag}_PT_act"], u + 1)
        e.wait_ge(S[f"{tag}_PT_dve"], u + 1)
        if u >= 1:
            e.wait_ge(S[f"{tag}_normed"], u)
        for b in range(2):
            for p in range(PAIRS):
                mm = nc.tensor.matmul(bank(6)[b * SEQ:(b + 1) * SEQ, p * PW:(p + 1) * PW],
                                      PT[:, p, b * SEQ:(b + 1) * SEQ], V[kind][:, 2 * t + b, p, :],
                                      start=True, stop=True)
        mm.then_inc(S[f"{tag}_summed"], 1)

    ahead = {"lor": 3, "mha": 2}

    def steps(tag, units):
        return range(-ahead[tag], len(units))

    def attention_tensor(e, S, tag, units):
        for k in steps(tag, units):
            u = k + ahead[tag]
            if k >= 0:
                turn_tensor(e, S, tag, k)
            if u < len(units):
                scores_tensor(e, S, tag, u, *units[u])
            if k >= 0:
                values_tensor(e, S, tag, k, *units[k])

    def attention_vector(e, S, tag, units):
        for k in steps(tag, units):
            u = k + ahead[tag]
            if tag == "lor" and 0 <= k + 1 < len(units):
                max_vector(e, S, tag, k + 1, "lor")
            if k >= 0:
                turned_vector(e, S, tag, k)
            if u < len(units):
                front_vector(e, S, tag, u, *units[u])
                if tag == "mha":
                    max_vector(e, S, tag, u, units[u][0])
            if k >= 0:
                back_vector(e, S, tag, k, *units[k])

    def attention_scalar(e, S, tag, units):
        for k in steps(tag, units):
            u = k + ahead[tag]
            if k >= 0:
                turned_scalar(e, S, tag, k)
            if tag == "lor":
                if 0 <= k + 2 < len(units):
                    arccosh_scalar(e, S, k + 2)
                if 0 <= k + 1 < len(units):
                    exp_scalar(e, S, tag, k + 1)
                if u < len(units):
                    lorentz_scalar(e, S, u)
            elif u < len(units):
                exp_scalar(e, S, tag, u)

    def attention_gpsimd(e, S, tag, units):
        if tag == "mha":
            for u in range(len(units)):
                shift_gpsimd(e, S, tag, u)
        else:
            for k in steps(tag, units):
                u = k + 2
                if 0 <= u < len(units):
                    ax = aux[:, u % BUFFERS, :, :]
                    e.wait_ge(S["lor_root"], u + 1)
                    nc.gpsimd.tensor_tensor(ax, ax, score[:, u % BUFFERS, :, :], ALU.add).then_inc(S["lor_arg"], 1)
                if 0 <= k + 1 < len(units):
                    shift_gpsimd(e, S, tag, k + 1)

    def lorentz_scalar(act, S, u):
        ax = aux[:, u % BUFFERS, :, :]
        act.wait_ge(S["lor_w"], u + 1)
        nc.scalar.activation(ax, ax, ACT.Ln).then_inc(S["lor_logw"], 1)
        act.wait_ge(S["lor_logw"], u + 1)
        nc.scalar.activation(ax, ax, ACT.Exp, scale=0.5).then_inc(S["lor_root"], 1)

    def arccosh_scalar(act, S, u):
        ax = aux[:, u % BUFFERS, :, :]
        act.wait_ge(S["lor_arg"], u + 1)
        nc.scalar.activation(ax, ax, ACT.Ln, bias=one[:, 0:1]).then_inc(S["lor_dist"], 1)
        act.wait_ge(S["lor_dist"], u + 1)
        nc.scalar.activation(ax, ax, ACT.Square).then_inc(S["lor_dist2"], 1)

    def front_vector(e, S, tag, u, kind, t):
        ps = four_banks[:, :, 0:HG * SEQ]
        wide = score[:, u % BUFFERS, :, :].rearrange("q (s g) k -> q s (g k)", s=STRIPS)
        sc, ax = score[:, u % BUFFERS, :, :], aux[:, u % BUFFERS, :, :]
        e.wait_ge(S[f"{tag}_score"], u + 1)
        if u >= BUFFERS:
            e.wait_ge(S[f"{tag}_turned"], 2 * (u - BUFFERS + 1))
        if kind == "lor":
            nc.vector.tensor_scalar(wide, ps, float(np.float32(1.0 + 1e-7)), -1.0, ALU.max, ALU.add)\
                .then_inc(S[f"{tag}_score_read"], 1)
            e.wait_ge(S[f"{tag}_score_read"], u + 1)
            nc.vector.scalar_tensor_tensor(out=ax, in0=sc, scalar=2.0, in1=sc, op0=ALU.add, op1=ALU.mult)\
                .then_inc(S[f"{tag}_w"], 1)
        else:
            bias = src_cur[:, t, :] if kind == "src" else tgt_bias[:, :]
            nc.vector.tensor_tensor(score[:, u % BUFFERS, :, :].rearrange("q (s g) k -> q s g k", s=STRIPS),
                                    ps.rearrange("q s (g k) -> q s g k", g=HG), bcast(bcast(bias, 1, HG), 1, STRIPS),
                                    ALU.add).then_inc(S[f"{tag}_score_read"], 1)

    def max_vector(e, S, tag, u, kind):
        sc, ax = score[:, u % BUFFERS, :, :], aux[:, u % BUFFERS, :, :]
        if kind == "lor":
            e.wait_ge(S[f"{tag}_dist2"], u + 1)
            nc.vector.scalar_tensor_tensor(out=sc, in0=ax, scalar=-INV_SQRT_D, in1=bcast(causal[:, :], 1, H),
                                           op0=ALU.mult, op1=ALU.add).then_inc(S[f"{tag}_masked"], 1)
            e.wait_ge(S[f"{tag}_masked"], u + 1)
        else:
            e.wait_ge(S[f"{tag}_score_read"], u + 1)
        nc.vector.tensor_reduce(row_max[:, u % BUFFERS, :], sc, AX_X, ALU.max).then_inc(S[f"{tag}_max"], 1)

    def turned_vector(e, S, tag, u):
        e.wait_ge(S[f"{tag}_turned"], 2 * u + 2)
        if u >= 1:
            e.wait_ge(S[f"{tag}_summed"], u)
        nc.vector.tensor_copy(PT[:, 4:8, :], pair[2][:, 512:1024].rearrange("k (p q) -> k p q", p=4))\
            .then_inc(S[f"{tag}_PT_dve"], 1)

    def back_vector(e, S, tag, u, kind, t):
        e.wait_ge(S[f"{tag}_summed"], u + 1)
        O = bank(6)[:, 0:PAIRS * PW].rearrange("q (p w) -> q p w", w=PW)
        nc.vector.reciprocal(row_rec[:, :, :], O[:, :, 2 * D:]).then_inc(S[f"{tag}_rec"], 1)
        e.wait_ge(S[f"{tag}_rec"], u + 1)
        if kind == "lor":
            nc.vector.tensor_scalar(row_rec[:, :, :], row_rec[:, :, :], spike[:, t:t + 1], None, ALU.mult)\
                .then_inc(S[f"{tag}_spiked"], 1)
            e.wait_ge(S[f"{tag}_spiked"], u + 1)
        nc.vector.tensor_tensor(o_tm[kind][:, t, :].rearrange("q (p two d) -> q p two d", two=2, d=D),
                                O[:, :, 0:2 * D].rearrange("q p (two d) -> q p two d", two=2),
                                bcast(row_rec[:, :, :], 3, D), ALU.mult).then_inc(S[f"{tag}_normed"], 1)

    def shift_gpsimd(e, S, tag, u):
        e.wait_ge(S[f"{tag}_max"], u + 1)
        nc.gpsimd.tensor_tensor(score[:, u % BUFFERS, :, :], score[:, u % BUFFERS, :, :], bcast(row_max[:, u % BUFFERS, :], 2, SEQ),
                                ALU.subtract).then_inc(S[f"{tag}_shifted"], 1)

    def exp_scalar(e, S, tag, u):
        e.wait_ge(S[f"{tag}_shifted"], u + 1)
        nc.scalar.activation(score[:, u % BUFFERS, :, :], score[:, u % BUFFERS, :, :], ACT.Exp).then_inc(S[f"{tag}_prob"], 1)

    def turned_scalar(e, S, tag, u):
        e.wait_ge(S[f"{tag}_turned"], 2 * u + 1)
        if u >= 1:
            e.wait_ge(S[f"{tag}_summed"], u)
        nc.scalar.activation(PT[:, 0:4, :], pair[2][:, 0:512].rearrange("k (p q) -> k p q", p=4), ACT.Copy)\
            .then_inc(S[f"{tag}_PT_act"], 1)

    def fill_V_vector(e, S, kind, b0):
        src = pair[2].rearrange("k (b p two d) -> k b p two d", b=GB, p=PAIRS, two=2)
        for half in range(2):
            rows = slice(half * SEQ, half * SEQ + SEQ)
            bias = b_v[kind][rows, :].rearrange("k (p two d) -> k p two d", p=PAIRS, two=2)[:, :, half, :]
            nc.vector.tensor_tensor(V[kind][rows, :, :, half * D:half * D + D], src[rows, :, :, half, :],
                                    bcast(bias, 1, GB), ALU.add).then_inc(S[f"{kind}_V"], 1)

    src_cur = sb("src_cur", [P, GT, SEQ])
    masks = I["mask_Bx1x1xS2_ff0"].rearrange("(t two) a b s -> two t (a b s)", two=2)
    by_seq = lambda ap: ap.rearrange("c (b s) -> c b s", s=SEQ)
    projections = (("src", "q"), ("src", "k"), ("tgt", "q"), ("tgt", "k"))
    lor_units = [("lor", t) for t in range(GT)]
    mha_units = [(k, t) for k in ("src", "tgt") for t in range(GT)]
    n_l, n_m = len(lor_units), len(mha_units)

    with ExitStack() as sems:
        S = Signals(nc, sems)
        with nc.Fori(0, GROUPS) as g:
            with nc.Block() as block:
                @block.tensor
                def _(pe):
                    transpose_tiles(pe, S, "ln_unit", lambda t: GT * LN_TURN["ln1"] + t + 1, x_norm, bank(7), "ln1_turned")
                    pe.wait_ge(S["ctx_loaded"], 16)
                    for t in range(GT):
                        nc.tensor.transpose(bank(6)[:, t * P:(t + 1) * P], ctx_cur[:, t, :], ident[:, :])\
                            .then_inc(S["ctx_turned"], 1)
                    pe.wait_ge(S["ln1_T"], 2)
                    for t in range(GT):
                        nc.tensor.matmul(bank(t)[:, 0:2 * C + 1], x_once[:, t * P:(t + 1) * P], w_qk[:, :],
                                         start=True, stop=True).then_inc(S["lor_qk"], 1)
                    for b in range(GB):
                        mm = nc.tensor.matmul(pair[2][:, b * C:(b + 1) * C], xT[:, b, :, :], w_v["lor"][:, :],
                                              start=True, stop=True)
                    mm.then_inc(S["lor_v"], 1)
                    for half in range(2):
                        pe.wait_ge(S["mapped"], 2 * (half + 1))
                        for side in range(2):
                            for t in (2 * half, 2 * half + 1):
                                dst = bank(0)[:, t * P:(t + 1) * P] if side == 0 else \
                                    bank(1 + half)[:, (t % 2) * P:(t % 2 + 1) * P]
                                tr = nc.tensor.transpose(dst, mapped[:, t, side, :], ident[:, :])
                            tr.then_inc(S["mapped_turned"], 1)
                    pe.wait_ge(S["lor_qT"], 1)
                    pe.wait_ge(S["lor_kT_act"], HG)
                    pe.wait_ge(S["lor_kT_dve"], HG)
                    pe.wait_ge(S["lor_V"], 2)
                    pe.wait_ge(S["ctx_T"], 1)
                    attention_tensor(pe, S, "lor", lor_units)
                    pe.wait_ge(S["lor_normed"], n_l)
                    for t in range(GT):
                        tr = nc.tensor.transpose(bank(7)[:, t * P:(t + 1) * P], o_tm["lor"][:, t, :], ident[:, :])
                    tr.then_inc(S["lor_o_turned"], 1)
                    pe.wait_ge(S["lor_oT"], 1)
                    for t in range(GT):
                        mm = nc.tensor.matmul(bank(6)[:, t * P:(t + 1) * P], oT["src"][:, t * P:(t + 1) * P],
                                              w_o["lor"][:, :], start=True, stop=True)
                    mm.then_inc(S["lor_y"], 1)

                    transpose_tiles(pe, S, "ln_unit", lambda t: GT * LN_TURN["ln2"] + t + 1, x_norm, bank(7), "ln2_turned")
                    pe.wait_ge(S["ln2_T"], 1)
                    for k, src in (("src", ctxT), ("tgt", xT)):
                        if k == "tgt":
                            pe.wait_ge(S["src_V"], 2)
                        for b in range(GB):
                            mm = nc.tensor.matmul(pair[2][:, b * C:(b + 1) * C], src[:, b, :, :], w_v[k][:, :],
                                                  start=True, stop=True)
                        mm.then_inc(S[f"{k}_v"], 1)
                    for j, (k, s) in enumerate(projections):
                        src = ctxT if (k, s) == ("src", "k") else xT
                        nc.tensor.matmul(bank(j), w_head[k + s][:, :], src[:, :, 0, :], start=True, stop=True)\
                            .then_inc(S["proj"], 1)
                    pe.wait_ge(S["tgt_V"], 2)
                    pe.wait_ge(S["q_heads"], 2)
                    pe.wait_ge(S["src_k_heads"], HG)
                    pe.wait_ge(S["tgt_k_heads"], HG)
                    attention_tensor(pe, S, "mha", mha_units)
                    for n, k in enumerate(("src", "tgt")):
                        pe.wait_ge(S["mha_normed"], GT * (n + 1))
                        for t in range(GT):
                            tr = nc.tensor.transpose(bank(n)[:, t * P:(t + 1) * P], o_tm[k][:, t, :], ident[:, :])
                        tr.then_inc(S["mha_o_turned"], 1)
                    pe.wait_ge(S["mha_oT"], 2)
                    nc.tensor.matmul(bank(7), w_o["src"][:, :], oT["src"][:, :], start=True, stop=False)
                    nc.tensor.matmul(bank(7), w_o["tgt"][:, :], oT["tgt"][:, :], start=False, stop=True)\
                        .then_inc(S["c"], 1)
                    for n, j in enumerate(GATE_ORDER):
                        nc.tensor.matmul(bank(2 + n), lstm_wx[:, 0, j * C:(j + 1) * C], xT[:, :, 0, :],
                                         start=True, stop=False)
                        if n == 0:
                            pe.wait_ge(S["cT"], 1)
                        nc.tensor.matmul(bank(2 + n), lstm_wx[:, 1, j * C:(j + 1) * C], cT[:, :],
                                         start=False, stop=True).then_inc(S["gate_x"], 1)

                @block.scalar
                def _(act):
                    nc.scalar.preload_act_table_set(LN_AND_EXP)
                    ln_scalar(act, S, "ln1")
                    act.wait_ge(S["ln1_turned"], GT)
                    nc.scalar.activation(x_once[:, :], bank(7), ACT.Copy).then_inc(S["ln1_T"], 1)
                    nc.scalar.activation(xT[:, :, :, :], bcast(bank(7).rearrange("c (b s) -> c b s", b=GB), 2, 2),
                                         ACT.Copy).then_inc(S["ln1_T"], 1)
                    act.wait_ge(S["ctx_turned"], GT)
                    nc.scalar.activation(ctxT[:, :, :, :], bcast(bank(6).rearrange("c (b s) -> c b s", b=GB), 2, 2),
                                         ACT.Copy).then_inc(S["ctx_T"], 1)
                    act.wait_ge(S["mink"], 1)
                    nc.scalar.activation(m_log[:, :], m_mink[:, :], ACT.Ln).then_inc(S["norm_log"], 1)
                    act.wait_ge(S["norm_log"], 1)
                    nc.scalar.activation(m_norm[:, :], m_log[:, :], ACT.Exp, scale=0.5).then_inc(S["norm"], 1)
                    act.wait_ge(S["norm"], 1)
                    nc.scalar.activation(m_ep[:, :], m_norm[:, :], ACT.Exp).then_inc(S["exps"], 1)
                    nc.scalar.activation(m_en[:, :], m_norm[:, :], ACT.Exp, scale=-1.0).then_inc(S["exps"], 1)
                    act.wait_ge(S["lor_qk_sb"], GT)
                    nc.scalar.activation(spike_e[:, :], qk[:, :, 2 * C], ACT.Exp, scale=-1.0).then_inc(S["spike_e"], 1)
                    act.wait_ge(S["mapped_turned"], 2)
                    for hg in range(HG):
                        nc.scalar.activation(heads["lor"][1][:, 0:GT, hg, :], by_seq(bank(1)[:, 0:2 * P]), ACT.Copy,
                                             scale=head_mask[:, hg:hg + 1]).then_inc(S["lor_kT_act"], 1)
                    act.wait_ge(S["mapped_turned"], 3)
                    nc.scalar.activation(heads["lor"][0][:, :], bank(0), ACT.Copy).then_inc(S["lor_qT"], 1)

                    attention_scalar(act, S, "lor", lor_units)
                    act.wait_ge(S["lor_o_turned"], 1)
                    nc.scalar.activation(oT["src"][:, :], bank(7), ACT.Copy).then_inc(S["lor_oT"], 1)

                    ln_scalar(act, S, "ln2")
                    act.wait_ge(S["ln2_turned"], GT)
                    nc.scalar.activation(xT[:, :, :, :], bcast(bank(7).rearrange("c (b s) -> c b s", b=GB), 2, 2),
                                         ACT.Copy).then_inc(S["ln2_T"], 1)
                    for j, (k, s) in enumerate(projections[:3]):
                        act.wait_ge(S["proj"], j + 1)
                        if s == "q":
                            nc.scalar.activation(heads[k][0][:, :], bank(j), ACT.Identity, bias=b_head[k + s][:, 0:1],
                                                 scale=INV_SQRT_D).then_inc(S["q_heads"], 1)
                        else:
                            for hg in range(HG):
                                nc.scalar.activation(heads[k][1][:, :, hg, :], by_seq(bank(j)), ACT.Identity,
                                                     bias=b_k_masked[k][:, hg:hg + 1],
                                                     scale=head_mask[:, hg:hg + 1]).then_inc(S["src_k_heads"], 1)
                    attention_scalar(act, S, "mha", mha_units)
                    for n, k in enumerate(("src", "tgt")):
                        act.wait_ge(S["mha_o_turned"], n + 1)
                        nc.scalar.activation(oT[k][:, :], bank(n), ACT.Copy).then_inc(S["mha_oT"], 1)
                    act.wait_ge(S["c"], 1)
                    nc.scalar.activation(cT[:, :], bank(7), ACT.Identity, bias=b_o_sum[:, 0:1]).then_inc(S["cT"], 1)
                    for n, j in enumerate(GATE_ORDER):
                        act.wait_ge(S["gate_x"], n + 1)
                        dst = gate0[:, bass.ds(g * GN, GN)] if n == 0 else gates123[:, n - 1, bass.ds(g * GN, GN)]
                        nc.scalar.activation(dst, bank(2 + n), ACT.Identity, bias=lstm_b[:, j:j + 1])\
                            .then_inc(S["gates_stored"], 1)

                @block.vector
                def _(dve):
                    nc.vector.tensor_copy(x_cur[:, :, :], x_all[:, bass.ds(g * GT, GT), :]).then_inc(S["x_cur"], 1)
                    dve.wait_ge(S["x_cur"], 1)
                    ln_vector(dve, S, "ln1", x_cur, x_norm)
                    for t in range(GT):
                        dve.wait_ge(S["lor_qk"], t + 1)
                        nc.vector.tensor_tensor(qk[:, t, :], bank(t)[:, 0:2 * C + 1], b_qk[:, :], ALU.add)\
                            .then_inc(S["lor_qk_sb"], 1)
                    dve.wait_ge(S["lor_v"], 1)
                    fill_V_vector(dve, S, "lor", 0)
                    dve.wait_ge(S["sq"], 1)
                    sq4 = sq[:, :, :].rearrange("q t (h d) -> q (t h) d", d=D)
                    nc.vector.tensor_reduce(m_x[:, :], sq4[:, :, 1:D], AX_X, ALU.add).then_inc(S["map_v"], 1)
                    dve.wait_ge(S["map_v"], 1)
                    nc.vector.tensor_tensor(m_x[:, :], m_x[:, :], sq4[:, :, 0], ALU.subtract).then_inc(S["map_v"], 1)
                    dve.wait_ge(S["map_v"], 2)
                    nc.vector.tensor_scalar(m_mink[:, :], m_x[:, :], 1e-8, None, ALU.max).then_inc(S["mink"], 1)
                    dve.wait_ge(S["mink"], 1)
                    nc.vector.tensor_scalar(m_x[:, :], m_mink[:, :], 1.0, None, ALU.min).then_inc(S["map_v"], 1)
                    nc.vector.tensor_scalar(m_small[:, :], m_mink[:, :], 1.0, None, ALU.is_lt).then_inc(S["map_small"], 1)
                    dve.wait_ge(S["map_v"], 3)
                    nc.vector.tensor_scalar(m_p[:, :], m_x[:, :], 1.0 / 362880, None, ALU.mult).then_inc(S["map_v"], 1)
                    for n, coeff in enumerate((1.0 / 5040, 1.0 / 120, 1.0 / 6)):
                        dve.wait_ge(S["map_v"], 4 + n)
                        nc.vector.scalar_tensor_tensor(out=m_p[:, :], in0=m_p[:, :], scalar=coeff, in1=m_x[:, :],
                                                       op0=ALU.add, op1=ALU.mult).then_inc(S["map_v"], 1)
                    dve.wait_ge(S["map_v"], 7)
                    dve.wait_ge(S["exps"], 2)
                    nc.vector.tensor_tensor(m_cosh2[:, :], m_ep[:, :], m_en[:, :], ALU.add).then_inc(S["cosh2"], 1)
                    nc.vector.tensor_tensor(m_sinh2[:, :], m_ep[:, :], m_en[:, :], ALU.subtract).then_inc(S["map_e"], 1)
                    nc.vector.reciprocal(m_rn[:, :], m_norm[:, :]).then_inc(S["map_e"], 1)
                    dve.wait_ge(S["map_e"], 2)
                    nc.vector.scalar_tensor_tensor(out=m_s[:, :], in0=m_sinh2[:, :], scalar=0.5, in1=m_rn[:, :],
                                                   op0=ALU.mult, op1=ALU.mult).then_inc(S["map_e"], 1)
                    dve.wait_ge(S["map_e"], 3)
                    nc.vector.scalar_tensor_tensor(out=m_p[:, :], in0=m_p[:, :], scalar=1.0, in1=m_s[:, :],
                                                   op0=ALU.add, op1=ALU.subtract).then_inc(S["map_e"], 1)
                    dve.wait_ge(S["map_e"], 4)
                    dve.wait_ge(S["map_small"], 1)
                    nc.vector.tensor_tensor(m_p[:, :], m_p[:, :], m_small[:, :], ALU.mult).then_inc(S["map_e"], 1)
                    dve.wait_ge(S["map_e"], 5)
                    nc.vector.tensor_tensor(m_s[:, :], m_s[:, :], m_p[:, :], ALU.add).then_inc(S["map_s"], 1)
                    dve.wait_ge(S["map_s"], 1)
                    dve.wait_ge(S["cosh2"], 1)
                    dve.wait_ge(S["spike_e"], 1)
                    nc.vector.tensor_scalar(spike_s[:, :], spike_e[:, :], 1.0, None, ALU.add).then_inc(S["spike_v"], 1)
                    dve.wait_ge(S["spike_v"], 1)
                    nc.vector.reciprocal(spike_s[:, :], spike_s[:, :]).then_inc(S["spike_v"], 1)
                    dve.wait_ge(S["spike_v"], 2)
                    nc.vector.tensor_scalar(spike[:, :], spike_s[:, :], threshold[:, 0:1], None, ALU.is_gt)\
                        .then_inc(S["spike_v"], 1)
                    dve.wait_ge(S["spike_v"], 3)
                    s4 = m_s[:, :].rearrange("q (t side h) -> q t side h", t=GT, side=2)
                    nc.vector.tensor_scalar(s4[:, :, 0, :], s4[:, :, 0, :], -1.0, None, ALU.mult).then_inc(S["map_s"], 1)
                    dve.wait_ge(S["map_s"], 2)
                    by_head = mapped[:, :, :, :].rearrange("q t side (h d) -> q t (side h) d", d=D)
                    of_qk = qk[:, :, 0:2 * C].rearrange("q t (e d) -> q t e d", d=D)
                    c3, s3 = (ap[:, :].rearrange("q (t e) -> q t e", t=GT) for ap in (m_cosh2, m_s))
                    for half in range(2):
                        ts = slice(2 * half, 2 * half + 2)
                        nc.vector.tensor_scalar(by_head[:, ts, :, 0], c3[:, ts], 0.5, None, ALU.mult)\
                            .then_inc(S["mapped"], 1)
                        nc.vector.tensor_tensor(by_head[:, ts, :, 1:D], of_qk[:, ts, :, 1:D], bcast(s3[:, ts], 3, D - 1),
                                                ALU.mult).then_inc(S["mapped"], 1)
                    dve.wait_ge(S["mapped_turned"], 4)
                    for hg in range(HG):
                        nc.vector.tensor_scalar(heads["lor"][1][:, GT:, hg, :], by_seq(bank(2)[:, 0:2 * P]),
                                                head_mask[:, hg:hg + 1], None, ALU.mult).then_inc(S["lor_kT_dve"], 1)
                    attention_vector(dve, S, "lor", lor_units)
                    dve.wait_ge(S["lor_y"], 1)
                    x_flat = x_cur[:, :, :].rearrange("q t c -> q (t c)")
                    nc.vector.tensor_tensor(x_flat, x_flat, bank(6), ALU.add).then_inc(S["lor_added"], 1)
                    dve.wait_ge(S["lor_added"], 1)
                    nc.vector.tensor_tensor(x_cur[:, :, :], x_cur[:, :, :], bcast(b_o_lor[:, :], 1, GT), ALU.add)\
                        .then_inc(S["lor_added"], 1)
                    dve.wait_ge(S["lor_added"], 2)
                    dve.wait_ge(S["ln1_turned"], GT)
                    nc.vector.tensor_copy(x_all[:, bass.ds(g * GT, GT), :], x_cur[:, :, :])
                    ln_vector(dve, S, "ln2", x_cur, x_norm)
                    for k in ("src", "tgt"):
                        dve.wait_ge(S[f"{k}_v"], 1)
                        fill_V_vector(dve, S, k, 0)
                    dve.wait_ge(S["proj"], 4)
                    for hg in range(HG):
                        nc.vector.tensor_scalar(heads["tgt"][1][:, :, hg, :], by_seq(bank(3)), head_mask[:, hg:hg + 1],
                                                b_k_masked["tgt"][:, hg:hg + 1], ALU.mult, ALU.add)\
                            .then_inc(S["tgt_k_heads"], 1)
                    dve.wait_ge(S["mask_loaded"], 32)
                    attention_vector(dve, S, "mha", mha_units)

                @block.sync
                def _(sp):
                    sp.dma_start(ctx_cur[:, :, :], tiles(I["ctx_1024"])[:, bass.ds(g * GT, GT), :])\
                        .then_inc(S["ctx_loaded"], 16)
                    for half in range(2):
                        sp.dma_start(src_cur[half * SEQ:(half + 1) * SEQ, :, :],
                                     masks[half][bass.ds(g * GT, GT), :].partition_broadcast(SEQ))\
                            .then_inc(S["mask_loaded"], 16)

                @block.gpsimd
                def _(pool):
                    pool.wait_ge(S["lor_qk_sb"], GT)
                    nc.gpsimd.tensor_tensor(sq[:, :, :], qk[:, :, 0:2 * C], qk[:, :, 0:2 * C], ALU.mult)\
                        .then_inc(S["sq"], 1)
                    attention_gpsimd(pool, S, "lor", lor_units)
                    attention_gpsimd(pool, S, "mha", mha_units)
            finish_phase(nc, S)


LSTM_UNROLL = 8


def phase_b(m, stack):
    nc, I, bank, gate0, gates123, lstm_wh = m.nc, m.I, m.bank, m.gate0, m.gates123, m.lstm_wh

    def sb(name, shape, where=None):
        return m.sb(name, shape, where or stack)

    w = {}
    loads = []

    def load(name, shape, *parts):
        w[name] = sb(name, shape)
        for index, src in parts:
            loads.append((w[name][index], src))

    all2, all3 = np.s_[:, :], np.s_[:, :, :]
    for tag, w1, b1, w2, b2 in (("hid0", "L0_xattn_ffn_w1", "L0_xattn_ffn_b1", "L0_xattn_ffn_w2", "L0_xattn_ffn_b2"),
                                ("hid1", "L1_xattn_w1", "L1_xattn_b1", "L1_xattn_w2", "L1_xattn_b2")):
        load(tag + "_w1", [P, HID], (all2, I[w1]))
        load(tag + "_b1", [P, HC], (all2, I[b1].rearrange("(c p) -> p c", p=P)))
        load(tag + "_w2", [P, HC, C], (all3, I[w2].rearrange("(c p) n -> p c n", p=P)))
        load(tag + "_b2", [P, 1], (all2, I[b2].unsqueeze(1)))
    for tag, name in (("moe0", "L0_ffn"), ("moe1", "L1_ffn")):
        load(tag + "_w1", [P, E, EH], (all3, I[name + "_W1"].rearrange("e c h -> c e h")))
        load(tag + "_b1", [P, E, EC], (all3, I[name + "_b1"].rearrange("e (k p) -> p e k", p=P)))
        load(tag + "_w2", [P, E * EC, C], (all3, I[name + "_W2"].rearrange("e (k p) c -> p (e k) c", p=P)))
        load(tag + "_b2", [PART_ROWS, C], *[(np.s_[32 * k:32 * k + E, :], I[name + "_b2"]) for k in range(PARTS)])
    load("w_red", [P, RED], (all2, I["L0_ffn_w_red"]))
    load("wg", [E, RED], (all2, I["L0_ffn_wg"]))
    load("gate_w", [P, E], (all2, I["L1_ffn_gate_W"]))
    load("fw_q", [P, TW], (all2, I["L1_attn_wq"]))
    load("fw_k", [P, TW], (all2, I["L1_attn_wk"]))
    load("fw_t", [P, TW], (all2, I["L1_attn_wv"]))
    load("fw_o", [P, PAIRS, C], (all3, I["L1_attn_wo"].rearrange("(p r) c -> r p c", r=P)))
    load("fw_theta", [P, PAIRS], (all2, I["L1_attn_theta"].rearrange("(p two) c one -> (two c) (p one)", two=2)))
    load("fw_theta_b", [P, H], (all2, row(I["L1_attn_theta_bias"])))
    load("fw_b", [P, TW], (all2, row(I["L1_attn_b1"])))
    load("fw_g2", [P, TW], (all2, row(I["L1_attn_gamma"])))
    load("fw_gbe", [P, TW], (all2, row(I["L1_attn_beta"])))
    load("fw_g_col", [P, PAIRS], (all2, I["L1_attn_gamma"].rearrange("(p two) one d -> (two d) (p one)", two=2)))
    load("fw_be_col", [P, PAIRS], (all2, I["L1_attn_beta"].rearrange("(p two) one d -> (two d) (p one)", two=2)))
    load("fw_alpha", [P, 1], *[(np.s_[half * TD:half * TD + TD, :], I["L1_attn_alpha"].unsqueeze(1))
                               for half in range(2)])
    for n in (1, 2, 3):
        load(f"ln_g{n}", [P, C], (all2, row(I[f"L1_xattn_g{n}"])))
        load(f"ln_b{n}", [P, C], (all2, row(I[f"L1_xattn_beta{n}"])))
    w["fw_w1"] = m.x_norm[:, :, :].rearrange("q t c -> q (t c)").rearrange("q (p d) -> q p d", p=PAIRS)
    loads.append((w["fw_w1"], I["L1_attn_W1"].rearrange("(p two) c d -> (two c) p d", two=2)))

    with ExitStack() as mem:
        h = sb("lstm_h", [P, BATCH], mem)
        c = sb("lstm_c", [P, BATCH], mem)
        pre = sb("lstm_pre", [P, GATES, BATCH], mem)
        cand = sb("lstm_cand", [P, BATCH], mem)
        sig = sb("lstm_sig", [P, GATES - 1, BATCH], mem)
        kept = sb("lstm_kept", [P, BATCH], mem)
        new = sb("lstm_new", [P, BATCH], mem)
        c_tanh = sb("lstm_c_tanh", [P, BATCH], mem)
        with ExitStack() as sems:
            S = Signals(nc, sems)
            with nc.Block() as block:
                @block.sync
                def _(sp):
                    sp.wait_ge(S["b2_cleared"], 2)
                    for dst, src in loads:
                        sp.dma_start(dst, src).then_inc(S["weights_loaded"], 16)
                    sp.wait_ge(S["weights_loaded"], 16 * len(loads))

                @block.vector
                def _(dve):
                    for tag in ("moe0", "moe1"):
                        nc.vector.memset(w[tag + "_b2"][:, :], 0.0).then_inc(S["b2_cleared"], 1)
                    nc.vector.memset(h[:, :], 0.0)
                    nc.vector.memset(c[:, :], 0.0)
            finish_phase(nc, S)

        at0 = gate0[:, :].rearrange("c (b s) -> c b s", s=SEQ)
        at123 = gates123.rearrange("c j (b s) -> c j b s", s=SEQ)
        with ExitStack() as sems:
            S = Signals(nc, sems)
            with nc.Fori(0, SEQ // LSTM_UNROLL) as i:
                with nc.Block() as block:
                    @block.tensor
                    def _(pe):
                        for k in range(LSTM_UNROLL):
                            if k >= 1:
                                pe.wait_ge(S["h"], k)
                            for n, j in enumerate(GATE_ORDER):
                                nc.tensor.matmul(bank(2 * (k % 2) + (n > 0))[:, n * BATCH:(n + 1) * BATCH],
                                                 lstm_wh[:, j * C:(j + 1) * C], h[:, :],
                                                 start=True, stop=True).then_inc(S["gate_h"], 1)

                    @block.vector
                    def _(dve):
                        for k in range(LSTM_UNROLL):
                            step = i * LSTM_UNROLL + k
                            dve.wait_ge(S["gate_h"], GATES * k + 1)
                            nc.vector.tensor_tensor(pre[:, 0, :], bank(2 * (k % 2))[:, 0:BATCH],
                                                    at0[:, :, bass.ds(step, 1)].rearrange("c b s -> c (b s)"),
                                                    ALU.add).then_inc(S["pre_cand"], 1)
                            dve.wait_ge(S["gate_h"], GATES * k + 4)
                            nc.vector.tensor_tensor(pre[:, 1:, :], bank(2 * (k % 2) + 1)[:, BATCH:GATES * BATCH].rearrange(
                                                        "c (j b) -> c j b", b=BATCH),
                                                    at123[:, :, :, bass.ds(step, 1)].rearrange("c j b s -> c j (b s)"),
                                                    ALU.add).then_inc(S["pre_gates"], 1)
                            dve.wait_ge(S["cand"], k + 1)
                            dve.wait_ge(S["gates"], k + 1)
                            nc.vector.tensor_tensor(kept[:, :], sig[:, 1, :], c[:, :], ALU.mult)\
                                .then_inc(S["kept"], 1)
                            nc.vector.tensor_tensor(new[:, :], sig[:, 0, :], cand[:, :], ALU.mult)\
                                .then_inc(S["new"], 1)
                            dve.wait_ge(S["kept"], k + 1)
                            dve.wait_ge(S["new"], k + 1)
                            nc.vector.tensor_tensor(c[:, :], kept[:, :], new[:, :], ALU.add).then_inc(S["c"], 1)
                            dve.wait_ge(S["c_tanh"], k + 1)
                            if k >= 1:
                                dve.wait_ge(S["h_stored"], k)
                            nc.vector.tensor_tensor(h[:, :], sig[:, 2, :], c_tanh[:, :], ALU.mult)\
                                .then_inc(S["h"], 1)

                    @block.scalar
                    def _(act):
                        nc.scalar.preload_act_table(ACT.Sigmoid)
                        for k in range(LSTM_UNROLL):
                            act.wait_ge(S["pre_cand"], k + 1)
                            nc.scalar.activation(cand[:, :], pre[:, 0, :], ACT.Tanh).then_inc(S["cand"], 1)
                            act.wait_ge(S["pre_gates"], k + 1)
                            nc.scalar.activation(sig[:, :, :], pre[:, 1:, :], ACT.Sigmoid).then_inc(S["gates"], 1)
                            act.wait_ge(S["c"], k + 1)
                            nc.scalar.activation(c_tanh[:, :], c[:, :], ACT.Tanh).then_inc(S["c_tanh"], 1)

                    @block.gpsimd
                    def _(pool):
                        for k in range(LSTM_UNROLL):
                            step = i * LSTM_UNROLL + k
                            pool.wait_ge(S["h"], k + 1)
                            nc.gpsimd.tensor_copy(at0[:, :, bass.ds(step, 1)].rearrange("c b s -> c (b s)"), h[:, :])\
                                .then_inc(S["h_stored"], 1)
                finish_phase(nc, S)

    for name, shape in (("wg_nT", [RED, E]), ("rank", [P, E]), ("block_mask", [P, P]),
                        ("causal_mask", [P, P]), ("fw_z", [P, TW]), ("fw_zq", [P, TW]), ("fw_go", [P, PAIRS, C]),
                        ("fw_qo", [P, C]), ("fw_beo", [P, C]), ("fw_lr", [P, H]), ("token_eta", [P, 1]),
                        ):
        w[name] = sb(name, shape)
    for name, shape in (("ones", [PART_ROWS, P]), ("ident_bf16", [P, P]), ("cw_parts", [P, GT, PARTS, 32]), ("sel", [PART_ROWS, E, P]), ("fw_b_rows", [PART_ROWS, TW]), ("fw_gbe_rows", [PART_ROWS, TW])):
        w[name] = m.sb(name, shape, stack, BF16)
    return w


def prepare_c(m, w):
    nc, pair, bank, ident = m.nc, m.pair, m.bank, m.ident
    with ExitStack() as mem, ExitStack() as sems:
        S = Signals(nc, sems)

        def sb(name, shape, dtype=F32):
            return m.sb(name, shape, mem, dtype)

        arena = m.arena
        wkT = arena[:, 0:1024].rearrange("r (p c) -> r p c", p=PAIRS)
        wqT = arena[:, 1024:2048].rearrange("r (p c) -> r p c", p=PAIRS)
        be_mat = arena[:, 2048:3072].rearrange("r (p q) -> r p q", p=PAIRS)
        mean = arena[:, 3072:3120].rearrange("q (n h) -> q n h", n=3)
        wg_sq = arena[0:E, 3200:3216]
        wg_v = arena[0:E, 3216:3224]
        rest = arena[:, 4096:4096 + 2 * TW].rearrange("q (n d) -> q n d", n=2)
        part = sb("bf16_part", [P, 2, TW], BF16)
        sel = arena[0:PART_ROWS, 8192:8192 + E * P].rearrange("r (e q) -> r e q", e=E)
        by_bank = lambda ap: ap.rearrange("q (two p d) -> q p two d", two=2, p=PAIRS)
        pos_i = sb("pos_i", [P, 1])
        pos = sb("pos", [P, 1])
        by_head = lambda ap: ap.rearrange("q (h d) -> q h d", h=H)

        with nc.Block() as block:
            @block.tensor
            def _(pe):
                for p in range(PAIRS):
                    tr = nc.tensor.transpose(pair[0][:, p * P:(p + 1) * P], w["fw_k"][:, p * P:(p + 1) * P], ident[:, :])
                tr.then_inc(S["wk_turned"], 1)
                for p in range(PAIRS):
                    tr = nc.tensor.transpose(pair[1][:, p * P:(p + 1) * P], w["fw_q"][:, p * P:(p + 1) * P], ident[:, :])
                tr.then_inc(S["wq_turned"], 1)
                pe.wait_ge(S["wkT"], 1)
                pe.wait_ge(S["wqT"], 1)
                for dst, src, done in ((2, wkT, "wk_w1"), (3, wqT, "wq_w1")):
                    for h in range(H):
                        rows = slice(TD * (h % 2), TD * (h % 2) + TD)
                        mm = nc.tensor.matmul(bank(2 * dst + h % 2)[:, (h // 2) * TD:(h // 2 + 1) * TD], src[rows, h // 2, :],
                                              w["fw_w1"][rows, h // 2, :], start=True, stop=True)
                    mm.then_inc(S[done], 1)
                for h in range(H):
                    rows = slice(TD * (h % 2), TD * (h % 2) + TD)
                    mm = nc.tensor.matmul(bank(h % 2)[:, h // 2:h // 2 + 1], wkT[rows, h // 2, :],
                                          w["fw_theta"][rows, h // 2:h // 2 + 1], start=True, stop=True)
                mm.then_inc(S["wk_theta"], 1)
                for p in range(PAIRS):
                    mm = nc.tensor.matmul(bank(2)[:, 0:C], wqT[:, p, :], w["fw_o"][:, p, :],
                                          start=(p == 0), stop=(p == PAIRS - 1))
                mm.then_inc(S["wq_wo"], 1)
                pe.wait_ge(S["be_mat"], 1)
                for p in range(PAIRS):
                    mm = nc.tensor.matmul(bank(3)[:, 0:C], be_mat[:, p, :], w["fw_o"][:, p, :],
                                          start=(p == 0), stop=(p == PAIRS - 1))
                mm.then_inc(S["be_wo"], 1)
                pe.wait_ge(S["wg_n"], 1)
                pe.wait_ge(S["wk_theta_sb"], 1)
                nc.tensor.transpose(bank(0)[0:RED, 128:128 + E], w["wg"][:, :], ident[0:E, 0:E])\
                    .then_inc(S["wg_turned"], 1)

            @block.scalar
            def _(act):
                act.wait_ge(S["wk_turned"], 1)
                nc.scalar.activation(wkT, pair[0].rearrange("r (p c) -> r p c", p=PAIRS), ACT.Copy)\
                    .then_inc(S["wkT"], 1)
                act.wait_ge(S["wq_turned"], 1)
                nc.scalar.activation(wqT, pair[1].rearrange("r (p c) -> r p c", p=PAIRS), ACT.Copy)\
                    .then_inc(S["wqT"], 1)
                act.wait_ge(S["wg_norm2"], 1)
                nc.scalar.activation(wg_v[:, 1:2], wg_v[:, 0:1], ACT.Ln).then_inc(S["wg_log"], 1)
                act.wait_ge(S["wg_log"], 1)
                nc.scalar.activation(wg_v[:, 2:3], wg_v[:, 1:2], ACT.Exp, scale=0.5).then_inc(S["wg_norm"], 1)
                act.wait_ge(S["wk_theta"], 1)
                nc.scalar.activation(w["fw_lr"][:, :].rearrange("q (p two) -> q two p", two=2),
                                     m.four_banks[:, 0:2, 0:PAIRS], ACT.Copy).then_inc(S["wk_theta_sb"], 1)
                act.wait_ge(S["wq_wo"], 1)
                nc.scalar.activation(w["fw_qo"][:, :], bank(2)[:, 0:C], ACT.Copy)
                act.wait_ge(S["be_wo"], 1)
                nc.scalar.activation(w["fw_beo"][:, :], bank(3)[:, 0:C], ACT.Copy)
                act.wait_ge(S["wg_turned"], 1)
                nc.scalar.activation(w["wg_nT"][:, :], bank(0)[0:RED, 128:128 + E], ACT.Copy)

            @block.vector
            def _(dve):
                nc.vector.tensor_copy(be_mat, bcast(w["fw_be_col"][:, :], 2, P)).then_inc(S["be_mat"], 1)
                nc.vector.memset(w["cw_parts"][:, :, :, :], 0.0)
                for name in ("fw_b_rows", "fw_gbe_rows"):
                    nc.vector.memset(w[name][:, :], 0.0).then_inc(S["rows_cleared"], 1)
                nc.vector.tensor_tensor(wg_sq, w["wg"][:, :], w["wg"][:, :], ALU.mult).then_inc(S["wg_v"], 1)
                dve.wait_ge(S["wg_v"], 1)
                nc.vector.tensor_reduce(wg_v[:, 3:4], wg_sq, AX_X, ALU.add).then_inc(S["wg_v"], 1)
                dve.wait_ge(S["wg_v"], 2)
                nc.vector.tensor_scalar(wg_v[:, 0:1], wg_v[:, 3:4], 1e-18, None, ALU.max).then_inc(S["wg_norm2"], 1)
                dve.wait_ge(S["wg_norm"], 1)
                nc.vector.tensor_scalar(wg_v[:, 4:5], wg_v[:, 2:3], 1e-4, None, ALU.max).then_inc(S["wg_v"], 1)
                dve.wait_ge(S["wg_v"], 3)
                nc.vector.reciprocal(wg_v[:, 5:6], wg_v[:, 4:5]).then_inc(S["wg_v"], 1)
                dve.wait_ge(S["wg_v"], 4)
                nc.vector.tensor_scalar(w["wg"][:, :], w["wg"][:, :], wg_v[:, 5:6], None, ALU.mult)\
                    .then_inc(S["wg_n"], 1)
                nc.vector.tensor_tensor(w["fw_t"][:, :], w["fw_k"][:, :], w["fw_t"][:, :], ALU.subtract)\
                    .then_inc(S["fold"], 1)
                nc.vector.tensor_tensor(w["fw_gbe"][:, :], w["fw_gbe"][:, :], w["fw_g2"][:, :], ALU.mult)\
                    .then_inc(S["gbe"], 1)
                dve.wait_ge(S["fold"], 1)
                nc.vector.tensor_tensor(w["fw_t"][:, :], w["fw_t"][:, :], w["fw_g2"][:, :], ALU.mult)\
                    .then_inc(S["fold"], 1)
                dve.wait_ge(S["fold"], 2)
                nc.vector.tensor_tensor(w["fw_g2"][:, :], w["fw_g2"][:, :], w["fw_g2"][:, :], ALU.mult)
                nc.vector.tensor_tensor(w["fw_go"][:, :, :], w["fw_o"][:, :, :], bcast(w["fw_g_col"][:, :], 2, C), ALU.mult)
                nc.vector.tensor_reduce(mean[:, 0, :], by_head(w["fw_b"][:, :]), AX_X, ALU.add).then_inc(S["mean"], 1)
                dve.wait_ge(S["wk_w1"], 1)
                nc.vector.tensor_reduce(mean[:, 1, :].rearrange("q (p two) -> q p two", two=2), by_bank(pair[2]), AX_X, ALU.add).then_inc(S["mean"], 1)
                dve.wait_ge(S["wq_w1"], 1)
                nc.vector.tensor_reduce(mean[:, 2, :].rearrange("q (p two) -> q p two", two=2), by_bank(pair[3]), AX_X, ALU.add).then_inc(S["mean"], 1)
                dve.wait_ge(S["mean"], 3)
                nc.vector.tensor_scalar(mean, mean, 1.0 / TD, None, ALU.mult).then_inc(S["mean"], 1)
                dve.wait_ge(S["mean"], 4)
                nc.vector.tensor_tensor(by_head(w["fw_b"][:, :]), by_head(w["fw_b"][:, :]), bcast(mean[:, 0, :], 2, TD),
                                        ALU.subtract).then_inc(S["b_less"], 1)
                for n, (name, ready) in enumerate((("fw_b", "b_less"), ("fw_gbe", "gbe"))):
                    dve.wait_ge(S["rows_cleared"], 2)
                    dve.wait_ge(S[ready], 1)
                    left = w[name][:, :]
                    for k in range(PARTS):
                        nc.vector.tensor_copy(part[:, n, :], left).then_inc(S[f"{name}_parts"], 1)
                        dve.wait_ge(S[f"{name}_parts"], 2 * k + 1)
                        nc.vector.tensor_copy(w[name + "_rows"][32 * k:32 * k + 1, :], part[32 * k:32 * k + 1, n, :])
                        if k < PARTS - 1:
                            nc.vector.tensor_tensor(rest[:, n, :], left, part[:, n, :], ALU.subtract)\
                                .then_inc(S[f"{name}_parts"], 1)
                            dve.wait_ge(S[f"{name}_parts"], 2 * k + 2)
                            left = rest[:, n, :]
                for n, (dst, src) in enumerate(((w["fw_z"], pair[2]), (w["fw_zq"], pair[3])), start=1):
                    in_pairs = lambda ap: ap.rearrange("q (p two) d -> q p two d", two=2)
                    nc.vector.tensor_tensor(in_pairs(by_head(dst[:, :])), by_bank(src),
                                            in_pairs(bcast(mean[:, n, :], 2, TD)), ALU.subtract)
                dve.wait_ge(S["pos"], 2)
                nc.vector.tensor_copy(pos[:, :], pos_i[:, :].bitcast(mybir.dt.int32)).then_inc(S["pos_v"], 1)
                dve.wait_ge(S["pos_v"], 1)
                nc.vector.reciprocal(pos[:, :], pos[:, :]).then_inc(S["pos_v"], 1)
                dve.wait_ge(S["pos_v"], 2)
                nc.vector.tensor_scalar(w["token_eta"][:, :], pos[:, :], w["fw_alpha"][:, 0:1], 0.0, ALU.add, ALU.max)\
                    .then_inc(S["pos_v"], 1)
                dve.wait_ge(S["pos_v"], 3)
                nc.vector.tensor_scalar(w["token_eta"][:, :], w["token_eta"][:, :], -1.0 / TD, None, ALU.mult)

            @block.gpsimd
            def _(pool):
                for half in range(2):
                    if half == 1:
                        pool.wait_ge(S["pos"], 1)
                    nc.gpsimd.iota(pos_i[half * SEQ:(half + 1) * SEQ, :].bitcast(mybir.dt.int32), pattern=[[0, 1]],
                                   base=1, channel_multiplier=1).then_inc(S["pos"], 1)
                pool.wait_ge(S["pos"], 2)
                nc.gpsimd.memset(w["ones"][:, :], 1.0)
                for e in range(E):
                    nc.gpsimd.memset(w["rank"][:, e:e + 1], float(E - e))
                nc.gpsimd.memset(sel[:, :, :], 0.0).then_inc(S["cleared"], 1)
                nc.gpsimd.memset(w["block_mask"][:, :], NEG).then_inc(S["cleared"], 1)
                pool.wait_ge(S["cleared"], 2)
                for k in range(PARTS):
                    if k >= 1:
                        pool.wait_ge(S["sel_made"], k)
                    nc.gpsimd.affine_select(out=sel[:, :, :], in_=sel[:, :, :], compare_op=ALU.not_equal, fill=1.0,
                                            base=-32 * k, pattern=[[-1, E], [0, P]], channel_multiplier=1)\
                        .then_inc(S["sel_made"], 1)
                pool.wait_ge(S["sel_made"], PARTS)
                nc.gpsimd.tensor_copy(w["sel"][:, :, :], sel[:, :, :])
                nc.gpsimd.tensor_copy(w["ident_bf16"][:, :], ident[:, :])
                for half in range(2):
                    if half == 1:
                        pool.wait_ge(S["cleared"], 3)
                    rows = slice(half * SEQ, (half + 1) * SEQ)
                    nc.gpsimd.memset(w["block_mask"][rows, rows], 0.0).then_inc(S["cleared"], 1)
                pool.wait_ge(S["cleared"], 4)
                nc.gpsimd.affine_select(out=w["causal_mask"][:, :], in_=w["block_mask"][:, :], compare_op=ALU.is_ge,
                                        fill=NEG, base=0, pattern=[[-1, P]], channel_multiplier=1)
        finish_phase(nc, S)


def phase_c(m, w):
    nc, I, tiles, pair, bank, ident, arena = m.nc, m.I, m.tiles, m.pair, m.bank, m.ident, m.arena
    x_all, gate0, x_cur, ctx_cur, x_norm = m.x_all, m.gate0, m.x_cur, m.ctx_cur, m.x_norm
    ln_vector, ln_scalar, transpose_tiles = m.ln_vector, m.ln_scalar, m.transpose_tiles
    x_flat = x_cur[:, :, :].rearrange("q t c -> q (t c)")

    def part(at, n):
        return arena[:, at:at + n]

    hid = part(0, HC * GN).rearrange("k (c n) -> k c n", c=HC)
    yT = part(2048, GN)
    exp_hid = part(0, 2 * EC * GN).rearrange("k (u c n) -> k u c n", u=2, c=EC)
    cwT = part(2560, GN)[0:PART_ROWS]
    cw_rest = m.sb("cw_rest", [P, 2, GT, E], m.stack_c)
    cw_parts = w["cw_parts"]
    cwT_parts = m.sb("cwT_parts", [PART_ROWS, GN], m.stack_c, BF16)
    redT = part(3072, GN)
    cw = part(3584, 10 * GT * E).rearrange("q (k t e) -> q k t e", k=10, t=GT)
    cw_s = part(3904, 10 * GT).rearrange("q (k t) -> q k t", k=10)
    fw_qT = part(0, PAIRS * GN).rearrange("r (p n) -> r p n", p=PAIRS)
    fw_kT = part(4096, PAIRS * GN).rearrange("r (p n) -> r p n", p=PAIRS)
    z_sq, sqr, unit, grad = (part(8192 + 1024 * n, 1024) for n in range(4))
    xT = m.sb("c_xT", [P, GN], m.stack_c)
    h_cur = m.sb("h_cur", [P, GN], m.stack_c)
    SA = m.sb("fw_A", [P, H, SEQ], m.stack_c)
    zq = m.sb("fw_zq_sb", [P, TW], m.stack_c)
    sqq = m.sb("fw_sqq", [P, TW], m.stack_c)
    turned = m.sb("fw_turned", [P, PAIRS, P], m.stack_c)
    small = m.sb("fw_small", [P, 12, H], m.stack_c)
    eta = m.sb("fw_eta", [P, GT, H], m.stack_c)
    y = part(0, GT * C).rearrange("q (t c) -> q t c", t=GT)
    att = part(512, GT * P).rearrange("q (t k) -> q t k", t=GT)
    attT = part(1024, GN)
    ctxT = part(1536, GN)
    att_s = part(2048 + 512, 4 * GT).rearrange("q (k t) -> q k t", k=4)
    xhid = part(4096, HC * GN).rearrange("k (c n) -> k c n", c=HC)
    yT2 = part(3072, GN)
    by_head = lambda ap: ap.rearrange("q (h d) -> q h d", h=H)

    def lnT_scalar(act, S, tag):
        act.wait_ge(S[f"{tag}_turned"], GT)
        nc.scalar.activation(xT[:, :], bank(7), ACT.Copy).then_inc(S[f"{tag}_T"], 1)

    def dense_tensor(pe, S, tag, src, src_ready):
        pe.wait_ge(S[src_ready], 1)
        for c in range(HC):
            nc.tensor.matmul(bank(c), w[tag + "_w1"][:, c * P:(c + 1) * P], src, start=True, stop=True)\
                .then_inc(S[f"{tag}_pre"], 1)
        for c in range(HC):
            pe.wait_ge(S[f"{tag}_hid"], c + 1)
            mm = nc.tensor.matmul(bank(4), w[tag + "_w2"][:, c, :], hid_of[tag][:, c, :],
                                  start=(c == 0), stop=(c == HC - 1))
        mm.then_inc(S[f"{tag}_y"], 1)
        back_tensor(pe, S, tag, yT_of[tag])

    def dense_scalar(act, S, tag):
        for c in range(HC):
            act.wait_ge(S[f"{tag}_pre"], c + 1)
            nc.scalar.activation(hid_of[tag][:, c, :], bank(c), ACT.Relu, bias=w[tag + "_b1"][:, c:c + 1])\
                .then_inc(S[f"{tag}_hid"], 1)
        act.wait_ge(S[f"{tag}_y"], 1)
        nc.scalar.activation(yT_of[tag], bank(4), ACT.Identity, bias=w[tag + "_b2"][:, 0:1])\
            .then_inc(S[f"{tag}_yT"], 1)

    def back_tensor(pe, S, tag, src):
        pe.wait_ge(S[f"{tag}_yT"], 1)
        for t in range(GT):
            tr = nc.tensor.transpose(bank(5)[:, t * P:(t + 1) * P], src[:, t * P:(t + 1) * P], ident[:, :])
        tr.then_inc(S[f"{tag}_back"], 1)

    hid_of = {"hid0": hid, "hid1": xhid}
    yT_of = {"hid0": yT, "hid1": yT2}

    def experts_tensor(pe, S, tag):
        pe.wait_ge(S[f"{tag}_cw"], PARTS)
        for t in range(GT):
            mm = nc.tensor.matmul(bank(6)[0:PART_ROWS, t * P:(t + 1) * P], cw_parts[:, t, :, :], w["ident_bf16"][:, :],
                                  start=True, stop=True)
        mm.then_inc(S[f"{tag}_cw_turned"], 1)
        pe.wait_ge(S[f"{tag}_cwT"], 2)
        nc.tensor.matmul(bank(6), w[tag + "_b2"][:, :], cwT, start=True, stop=False)
        for e in range(E + 1):
            if e < E:
                if e >= 2:
                    pe.wait_ge(S[f"{tag}_scaled"], EC * (e - 1))
                nc.tensor.matmul(bank(4 + e % 2), w["sel"][:, e, :], cwT_parts[:, :], start=True, stop=True)\
                    .then_inc(S[f"{tag}_cw_rows"], 1)
                for c in range(EC):
                    i = EC * e + c
                    if e >= 2:
                        pe.wait_ge(S[f"{tag}_act"], i - 3)
                    nc.tensor.matmul(bank(i % 4), w[tag + "_w1"][:, e, c * P:(c + 1) * P], xT[:, :],
                                     start=True, stop=True).then_inc(S[f"{tag}_pre"], 1)
            if e >= 1:
                for c in range(EC):
                    i = EC * (e - 1) + c
                    pe.wait_ge(S[f"{tag}_scaled"], i + 1)
                    nc.tensor.matmul(bank(6), w[tag + "_w2"][:, i, :], exp_hid[:, (e - 1) % 2, c, :],
                                     start=False, stop=(i == E * EC - 1)).then_inc(S[f"{tag}_used"], 1)
        back_tensor(pe, S, tag, yT)

    def experts_scalar(act, S, tag, func):
        act.wait_ge(S[f"{tag}_cw_turned"], 1)
        nc.scalar.activation(cwT_parts[:, :], bank(6)[0:PART_ROWS, :], ACT.Copy).then_inc(S[f"{tag}_cwT"], 1)
        nc.scalar.activation(cwT, bank(6)[0:PART_ROWS, :], ACT.Copy).then_inc(S[f"{tag}_cwT"], 1)
        for i in range(E * EC):
            e, c = divmod(i, EC)
            act.wait_ge(S[f"{tag}_pre"], i + 1)
            if e >= 2:
                act.wait_ge(S[f"{tag}_used"], i - 3)
            nc.scalar.activation(exp_hid[:, e % 2, c, :], bank(i % 4), func, bias=w[tag + "_b1"][:, e, c:c + 1])\
                .then_inc(S[f"{tag}_act"], 1)
        act.wait_ge(S[f"{tag}_used"], E * EC)
        nc.scalar.activation(yT, bank(6), ACT.Copy).then_inc(S[f"{tag}_yT"], 1)

    def split_weights_vector(dve, S, tag):
        left = cw[:, 0]
        for k in range(PARTS):
            nc.vector.tensor_copy(cw_parts[:, :, k, 0:E], left).then_inc(S[f"{tag}_cw"], 1)
            if k < PARTS - 1:
                dve.wait_ge(S[f"{tag}_cw"], k + 1)
                nc.vector.tensor_tensor(cw_rest[:, k], left, cw_parts[:, :, k, 0:E], ALU.subtract)\
                    .then_inc(S[f"{tag}_cw_rest"], 1)
                dve.wait_ge(S[f"{tag}_cw_rest"], k + 1)
                left = cw_rest[:, k]

    def experts_vector(dve, S, tag):
        for i in range(E * EC):
            e, c = divmod(i, EC)
            dve.wait_ge(S[f"{tag}_cw_rows"], e + 1)
            dve.wait_ge(S[f"{tag}_act"], i + 1)
            nc.vector.tensor_tensor(exp_hid[:, e % 2, c, :], exp_hid[:, e % 2, c, :], bank(4 + e % 2), ALU.mult)\
                .then_inc(S[f"{tag}_scaled"], 1)
        dve.wait_ge(S[f"{tag}_back"], 1)
        nc.vector.tensor_tensor(x_flat, x_flat, bank(5), ALU.add).then_inc(S[f"{tag}_added"], 1)

    def first_of_max(dve, S, tag, values, top, tmp, key, hot, n0):
        nc.vector.tensor_reduce(top, values, AX_X, ALU.max).then_inc(S[f"{tag}_sel"], 1)
        dve.wait_ge(S[f"{tag}_sel"], n0 + 1)
        nc.vector.tensor_tensor(tmp, values, bcast(top, 2, E), ALU.is_equal).then_inc(S[f"{tag}_sel"], 1)
        dve.wait_ge(S[f"{tag}_sel"], n0 + 2)
        nc.vector.tensor_tensor(tmp, tmp, bcast(w["rank"][:, :], 1, GT), ALU.mult).then_inc(S[f"{tag}_sel"], 1)
        dve.wait_ge(S[f"{tag}_sel"], n0 + 3)
        nc.vector.tensor_reduce(key, tmp, AX_X, ALU.max).then_inc(S[f"{tag}_sel"], 1)
        dve.wait_ge(S[f"{tag}_sel"], n0 + 4)
        nc.vector.tensor_tensor(hot, tmp, bcast(key, 2, E), ALU.is_equal).then_inc(S[f"{tag}_sel"], 1)
        dve.wait_ge(S[f"{tag}_sel"], n0 + 5)

    def gate_exps_vector(dve, S, tag):
        dve.wait_ge(S[f"{tag}_logits"], 1)
        nc.vector.tensor_copy(cw[:, 1], bank(1)[:, 0:GT * E].rearrange("q (t e) -> q t e", t=GT))\
            .then_inc(S[f"{tag}_logits_sb"], 1)
        dve.wait_ge(S[f"{tag}_logits_sb"], 1)
        first_of_max(dve, S, tag, cw[:, 1], cw_s[:, 0], cw[:, 2], cw_s[:, 1], cw[:, 3], 0)
        nc.vector.tensor_tensor(cw[:, 4], cw[:, 1], bcast(cw_s[:, 0], 2, E), ALU.subtract)\
            .then_inc(S[f"{tag}_less_max"], 1)
        dve.wait_ge(S[f"{tag}_exp"], 1)
        nc.vector.tensor_reduce(cw_s[:, 2], cw[:, 5], AX_X, ALU.add).then_inc(S[f"{tag}_gate"], 1)
        dve.wait_ge(S[f"{tag}_gate"], 1)
        nc.vector.reciprocal(cw_s[:, 3], cw_s[:, 2]).then_inc(S[f"{tag}_gate"], 1)
        dve.wait_ge(S[f"{tag}_gate"], 2)

    def gate_exps_scalar(act, S, tag):
        act.wait_ge(S[f"{tag}_less_max"], 1)
        nc.scalar.activation(cw[:, 5], cw[:, 4], ACT.Exp).then_inc(S[f"{tag}_exp"], 1)

    def attend_tensor(pe, S, tag, kT, values):
        for t in range(GT):
            mm = nc.tensor.matmul(bank(0)[:, t * P:(t + 1) * P], xT[:, t * P:(t + 1) * P], kT[:, t * P:(t + 1) * P],
                                  start=True, stop=True)
        mm.then_inc(S[f"{tag}_score"], 1)
        pe.wait_ge(S[f"{tag}_prob"], 1)
        for t in range(GT):
            tr = nc.tensor.transpose(bank(1)[:, t * P:(t + 1) * P], att[:, t, :], ident[:, :])
        tr.then_inc(S[f"{tag}_turned"], 1)
        pe.wait_ge(S[f"{tag}_probT"], 1)
        for t in range(GT):
            mm = nc.tensor.matmul(bank(2)[:, t * P:(t + 1) * P], attT[:, t * P:(t + 1) * P], values[:, t, :],
                                  start=True, stop=True)
        mm.then_inc(S[f"{tag}_pv"], 1)

    def attend_scalar(act, S, tag):
        act.wait_ge(S[f"{tag}_less_max"], 1)
        nc.scalar.activation(att, att, ACT.Exp).then_inc(S[f"{tag}_prob"], 1)
        act.wait_ge(S[f"{tag}_turned"], 1)
        nc.scalar.activation(attT, bank(1), ACT.Copy).then_inc(S[f"{tag}_probT"], 1)

    def attend_vector(dve, S, tag, mask):
        dve.wait_ge(S[f"{tag}_score"], 1)
        nc.vector.scalar_tensor_tensor(out=att, in0=bank(0).rearrange("q (t k) -> q t k", t=GT), scalar=INV_SQRT_C,
                                       in1=bcast(w[mask][:, :], 1, GT), op0=ALU.mult, op1=ALU.add)\
            .then_inc(S[f"{tag}_masked"], 1)
        dve.wait_ge(S[f"{tag}_masked"], 1)
        nc.vector.tensor_reduce(att_s[:, 0], att, AX_X, ALU.max).then_inc(S[f"{tag}_max"], 1)
        dve.wait_ge(S[f"{tag}_max"], 1)
        nc.vector.tensor_tensor(att, att, bcast(att_s[:, 0], 2, P), ALU.subtract).then_inc(S[f"{tag}_less_max"], 1)
        dve.wait_ge(S[f"{tag}_prob"], 1)
        nc.vector.tensor_reduce(att_s[:, 1], att, AX_X, ALU.add).then_inc(S[f"{tag}_sum"], 1)
        dve.wait_ge(S[f"{tag}_sum"], 1)
        nc.vector.reciprocal(att_s[:, 2], att_s[:, 1]).then_inc(S[f"{tag}_rec"], 1)
        dve.wait_ge(S[f"{tag}_rec"], 1)
        dve.wait_ge(S[f"{tag}_pv"], 1)
        nc.vector.tensor_tensor(x_norm[:, :, :], bank(2).rearrange("q (t c) -> q t c", t=GT),
                                bcast(att_s[:, 2], 2, C), ALU.mult).then_inc(S[f"{tag}_out"], 1)
        dve.wait_ge(S[f"{tag}_out"], 1)
        nc.vector.tensor_tensor(y, y, x_norm[:, :, :], ALU.add).then_inc(S[f"{tag}_added"], 1)
        dve.wait_ge(S[f"{tag}_added"], 1)

    def fast_tensor(pe, S):
        pe.wait_ge(S["ln4_T"], 1)
        for j in range(2 * PAIRS):
            p, side = divmod(j, 2)
            if j >= 4:
                pe.wait_ge(S["fw_heads_act" if side == 0 else "fw_heads_dve"], j // 2 - 1)
            nc.tensor.matmul(bank(j % 4), w["fw_q" if side == 0 else "fw_k"][:, p * P:(p + 1) * P], xT[:, :],
                             start=True, stop=True).then_inc(S["fw_heads"], 1)
        for t in range(GT):
            mm = nc.tensor.matmul(bank(7)[:, t * H:(t + 1) * H], xT[:, t * P:(t + 1) * P], w["fw_lr"][:, :],
                                  start=True, stop=True)
        mm.then_inc(S["fw_lr"], 1)
        pe.wait_ge(S["fw_heads_act"], PAIRS)
        pe.wait_ge(S["fw_heads_dve"], PAIRS)
        def with_row(dst, x_tile, weights, rows, last):
            for half in range(2):
                cols = slice(half * 512, half * 512 + 512)
                nc.tensor.matmul(dst[:, cols], x_tile, weights[:, cols], start=True, stop=False, skip_group_check=True)
                mm = nc.tensor.matmul(dst[:, cols], w["ones"][:, :], rows[:, cols], start=False, stop=last,
                                      skip_group_check=True)
            return mm

        for t in range(-1, GT + 1):
            new, old = t + 1, t - 1
            if new < GT:
                x_tile = xT[:, new * P:(new + 1) * P]
                if new >= 1:
                    pe.wait_ge(S["fw_unit"], new)
                with_row(pair[0], x_tile, w["fw_z"], w["fw_b_rows"], True).then_inc(S["fw_z"], 1)
                if new >= 1:
                    pe.wait_ge(S["fw_gxh"], new)
                with_row(pair[1], x_tile, w["fw_t"], w["fw_gbe_rows"], True).then_inc(S["fw_t"], 1)
            if old >= 0:
                pe.wait_ge(S["fw_unit2"], old + 1)
                pe.wait_ge(S["fw_A"], min(t + 1, GT))
                for p in range(PAIRS):
                    tr = nc.tensor.transpose(pair[2][:, p * P:(p + 1) * P], zq[:, p * P:(p + 1) * P], ident[:, :])
                tr.then_inc(S["fw_turned"], 1)
            if 0 <= t < GT:
                if t == 0:
                    pe.wait_ge(S["fw_lr_in"], 1)
                with_row(pair[3], xT[:, t * P:(t + 1) * P], w["fw_zq"], w["fw_b_rows"], False)
            if old >= 0:
                pe.wait_ge(S["fw_turned_act"], old + 1)
                nc.tensor.matmul(bank(4)[:, 0:C], xT[:, old * P:(old + 1) * P], w["fw_qo"][:, :], start=True, stop=False)
                for p in range(PAIRS):
                    mm = nc.tensor.matmul(bank(4)[:, 0:C], turned[:, p, :], w["fw_go"][:, p, :], start=False,
                                          stop=(p == PAIRS - 1))
                mm.then_inc(S["fw_y"], 1)
            if 0 <= t < GT:
                pe.wait_ge(S["fw_A"], t + 1)
                pe.wait_ge(S["fw_step"], t + 1)
                for b in range(2):
                    rows = slice(b * SEQ, (b + 1) * SEQ)
                    for h in range(H):
                        mm = nc.tensor.matmul(pair[3][rows, h * TD:(h + 1) * TD], SA[rows, h, :],
                                              grad[rows, h * TD:(h + 1) * TD], start=False,
                                              stop=(b == 1 and h in (H // 2 - 1, H - 1)), skip_group_check=True)
                mm.then_inc(S["fw_zq"], 1)
            if new < GT:
                if old >= 0:
                    pe.wait_ge(S["fw_x"], old + 1)
                elif new >= 1:
                    pe.wait_ge(S["fw_A"], new)
                for b in range(2):
                    for h in range(H):
                        rows, cols = slice(TD * (h % 2), TD * (h % 2) + TD), slice((2 * new + b) * SEQ, (2 * new + b + 1) * SEQ)
                        mm = nc.tensor.matmul(bank(4 + h % 2)[b * SEQ:(b + 1) * SEQ, (h // 2) * SEQ:(h // 2 + 1) * SEQ],
                                              fw_kT[rows, h // 2, cols], fw_qT[rows, h // 2, cols],
                                              start=True, stop=True)
                mm.then_inc(S["fw_kq"], 1)

    def fast_scalar(act, S):
        for p in range(PAIRS):
            act.wait_ge(S["fw_heads"], 2 * p + 1)
            nc.scalar.activation(fw_qT[:, p, :], bank((2 * p) % 4), ACT.Copy).then_inc(S["fw_heads_act"], 1)
        act.wait_ge(S["fw_lr_in"], 1)
        nc.scalar.activation(eta[:, :, :], eta[:, :, :], ACT.Exp, scale=-1.0).then_inc(S["fw_lr_e"], 1)

        def rstd(src, log, dst, ready, count, tag):
            act.wait_ge(S[ready], count)
            nc.scalar.activation(log, src, ACT.Ln, bias=m.eps6[:, 0:1], scale=1.0 / TD).then_inc(S[f"{tag}_log"], 1)
            act.wait_ge(S[f"{tag}_log"], count)
            nc.scalar.activation(dst, log, ACT.Exp, scale=-0.5).then_inc(S[f"{tag}_rstd"], 1)

        for t in range(-1, GT + 1):
            new, old = t + 1, t - 1
            if old >= 0:
                act.wait_ge(S["fw_zq"], old + 1)
                if old >= 1:
                    act.wait_ge(S["fw_var2"], old)
                nc.scalar.activation(sqq[:, :], pair[3][:, :], ACT.Square).then_inc(S["fw_sqq"], 1)
            if 0 <= t < GT:
                act.wait_ge(S["fw_kq"], t + 1)
                if t >= 1:
                    act.wait_ge(S["fw_zq"], t)
                nc.scalar.activation(SA[:, :, :].rearrange("k (p two) q -> k two p q", two=2),
                                     pair[2].rearrange("k (two p q) -> k two p q", two=2, p=PAIRS), ACT.Identity,
                                     bias=m.one[:, 0:1]).then_inc(S["fw_A"], 1)
            if new < GT:
                act.wait_ge(S["fw_z"], new + 1)
                if new >= 1:
                    act.wait_ge(S["fw_var"], new)
                nc.scalar.activation(z_sq, pair[0][:, :], ACT.Square).then_inc(S["fw_sqr"], 1)
            if old >= 0:
                rstd(small[:, 3, :], small[:, 4, :], small[:, 5, :], "fw_var2", old + 1, "fw2")
                act.wait_ge(S["fw_turned"], old + 1)
                nc.scalar.activation(turned[:, :, :], pair[2].rearrange("r (p q) -> r p q", p=PAIRS), ACT.Copy)\
                    .then_inc(S["fw_turned_act"], 1)
            if new < GT:
                rstd(small[:, 0, :], small[:, 1, :], small[:, 2, :], "fw_var", new + 1, "fw1")

    def fast_vector(dve, S):
        for p in range(PAIRS):
            dve.wait_ge(S["fw_heads"], 2 * p + 2)
            nc.vector.tensor_copy(fw_kT[:, p, :], bank((2 * p + 1) % 4)).then_inc(S["fw_heads_dve"], 1)
        dve.wait_ge(S["fw_lr"], 1)
        nc.vector.tensor_tensor(eta[:, :, :], bank(7)[:, 0:GT * H].rearrange("q (t h) -> q t h", t=GT),
                                bcast(w["fw_theta_b"][:, :], 1, GT), ALU.add).then_inc(S["fw_lr_in"], 1)
        dve.wait_ge(S["fw_lr_e"], 1)
        nc.vector.tensor_scalar(eta[:, :, :], eta[:, :, :], 1.0, None, ALU.add).then_inc(S["fw_eta"], 1)
        dve.wait_ge(S["fw_eta"], 1)
        nc.vector.reciprocal(eta[:, :, :], eta[:, :, :]).then_inc(S["fw_eta"], 1)
        dve.wait_ge(S["fw_eta"], 2)
        nc.vector.tensor_scalar(eta[:, :, :], eta[:, :, :], w["token_eta"][:, 0:1], None, ALU.mult)\
            .then_inc(S["fw_eta"], 1)
        dve.wait_ge(S["fw_eta"], 3)
        for t in range(-1, GT + 1):
            new, old = t + 1, t - 1
            if 0 <= t < GT:
                dve.wait_ge(S["fw_t"], t + 1)
                dve.wait_ge(S["fw_gx"], t + 1)
                nc.vector.tensor_tensor(grad, grad, pair[1][:, :], ALU.add).then_inc(S["fw_gxh"], 1)
            if old >= 0:
                dve.wait_ge(S["fw_sqq"], old + 1)
                nc.vector.tensor_reduce(small[:, 3, :], by_head(sqq[:, :]), AX_X, ALU.add).then_inc(S["fw_var2"], 1)
            if 0 <= t < GT:
                dve.wait_ge(S["fw_gxh"], t + 1)
                nc.vector.tensor_reduce(small[:, 6, :], by_head(grad), AX_X, ALU.add).then_inc(S["fw_s1"], 1)
            if old >= 0:
                dve.wait_ge(S["fw2_rstd"], old + 1)
                if old >= 1:
                    dve.wait_ge(S["fw_turned"], old)
                nc.vector.tensor_tensor(by_head(zq[:, :]), by_head(pair[3]), bcast(small[:, 5, :], 2, TD), ALU.mult)\
                    .then_inc(S["fw_unit2"], 1)
            if 0 <= t < GT:
                dve.wait_ge(S["fw_p"], t + 1)
                nc.vector.tensor_reduce(small[:, 7, :], by_head(sqr), AX_X, ALU.add).then_inc(S["fw_s2"], 1)
                nc.vector.tensor_tensor(small[:, 8, :], eta[:, t, :], small[:, 2, :], ALU.mult).then_inc(S["fw_coef"], 1)
                dve.wait_ge(S["fw_s1"], t + 1)
                dve.wait_ge(S["fw_s2"], t + 1)
                nc.vector.tensor_scalar(small[:, 6:8, :], small[:, 6:8, :], 1.0 / TD, None, ALU.mult)\
                    .then_inc(S["fw_means"], 1)
                dve.wait_ge(S["fw_means"], t + 1)
                nc.vector.tensor_tensor(by_head(grad), by_head(grad), bcast(small[:, 6, :], 2, TD), ALU.subtract)\
                    .then_inc(S["fw_less"], 1)
                dve.wait_ge(S["fw_less"], 2 * t + 1)
                dve.wait_ge(S["fw_u"], t + 1)
                nc.vector.tensor_tensor(grad, grad, sqr, ALU.subtract).then_inc(S["fw_less"], 1)
                dve.wait_ge(S["fw_less"], 2 * t + 2)
                dve.wait_ge(S["fw_coef"], t + 1)
                nc.vector.tensor_tensor(by_head(grad), by_head(grad), bcast(small[:, 8, :], 2, TD), ALU.mult)\
                    .then_inc(S["fw_step"], 1)
            if new < GT:
                dve.wait_ge(S["fw_sqr"], new + 1)
                nc.vector.tensor_reduce(small[:, 0, :], by_head(z_sq), AX_X, ALU.add).then_inc(S["fw_var"], 1)
            if old >= 0:
                dve.wait_ge(S["fw_y"], old + 1)
                nc.vector.tensor_tensor(x_cur[:, old, :], x_cur[:, old, :], bank(4)[:, 0:C], ALU.add)\
                    .then_inc(S["fw_x"], 1)
            if new < GT:
                dve.wait_ge(S["fw1_rstd"], new + 1)
                nc.vector.tensor_tensor(by_head(unit), by_head(pair[0]), bcast(small[:, 2, :], 2, TD), ALU.mult)\
                    .then_inc(S["fw_unit"], 1)
        dve.wait_ge(S["fw_x"], GT)
        nc.vector.tensor_tensor(x_cur[:, :, :], x_cur[:, :, :], bcast(w["fw_beo"][:, :], 1, GT), ALU.add)\
            .then_inc(S["fw_added"], 1)
        dve.wait_ge(S["fw_added"], 1)

    def fast_gpsimd(pool, S):
        for t in range(GT):
            pool.wait_ge(S["fw_unit"], t + 1)
            if t >= 1:
                pool.wait_ge(S["fw_zq"], t)
            nc.gpsimd.tensor_tensor(grad, unit, w["fw_g2"][:, :], ALU.mult).then_inc(S["fw_gx"], 1)
            pool.wait_ge(S["fw_gxh"], t + 1)
            nc.gpsimd.tensor_tensor(sqr, grad, unit, ALU.mult).then_inc(S["fw_p"], 1)
            pool.wait_ge(S["fw_means"], t + 1)
            nc.gpsimd.tensor_tensor(by_head(sqr), by_head(unit), bcast(small[:, 7, :], 2, TD), ALU.mult)\
                .then_inc(S["fw_u"], 1)

    with ExitStack() as sems:
        S = Signals(nc, sems)
        with nc.Fori(0, GROUPS) as g:
            with nc.Block() as block:
                @block.tensor
                def _(pe):
                    dense_tensor(pe, S, "hid0", h_cur[:, :], "h_cur")
                    transpose_tiles(pe, S, "ln_unit", lambda t: GT * LN_TURN["ln3"] + t + 1, x_norm, bank(7), "ln3_turned")
                    pe.wait_ge(S["ln3_T"], 1)
                    nc.tensor.matmul(bank(0)[0:RED, :], w["w_red"][:, :], xT[:, :], start=True, stop=True)\
                        .then_inc(S["red"], 1)
                    pe.wait_ge(S["redT"], 1)
                    for t in range(GT):
                        mm = nc.tensor.matmul(bank(1)[:, t * E:(t + 1) * E], redT[0:RED, t * P:(t + 1) * P],
                                              w["wg_nT"][:, :], start=True, stop=True)
                    mm.then_inc(S["moe0_logits"], 1)
                    experts_tensor(pe, S, "moe0")
                    transpose_tiles(pe, S, "ln_unit", lambda t: GT * LN_TURN["ln4"] + t + 1, x_norm, bank(7), "ln4_turned")
                    fast_tensor(pe, S)

                @block.scalar
                def _(act):
                    nc.scalar.preload_act_table_set(LN_AND_EXP)
                    dense_scalar(act, S, "hid0")
                    ln_scalar(act, S, "ln3")
                    lnT_scalar(act, S, "ln3")
                    act.wait_ge(S["red"], 1)
                    nc.scalar.activation(redT[0:RED, :], bank(0)[0:RED, :], ACT.Copy).then_inc(S["redT"], 1)
                    gate_exps_scalar(act, S, "moe0")
                    experts_scalar(act, S, "moe0", ACT.Gelu)
                    nc.scalar.preload_act_table_set(LN_AND_EXP)
                    ln_scalar(act, S, "ln4")
                    lnT_scalar(act, S, "ln4")
                    fast_scalar(act, S)

                @block.vector
                def _(dve):
                    nc.vector.tensor_copy(x_cur[:, :, :], x_all[:, bass.ds(g * GT, GT), :]).then_inc(S["x_cur"], 1)
                    dve.wait_ge(S["x_cur"], 1)
                    dve.wait_ge(S["hid0_back"], 1)
                    nc.vector.tensor_tensor(x_flat, x_flat, bank(5), ALU.add).then_inc(S["hid0_added"], 1)
                    dve.wait_ge(S["hid0_added"], 1)
                    ln_vector(dve, S, "ln3", x_cur, x_norm)
                    gate_exps_vector(dve, S, "moe0")
                    nc.vector.tensor_tensor(cw[:, 0], cw[:, 3], bcast(cw_s[:, 3], 2, E), ALU.mult)\
                        .then_inc(S["moe0_choice"], 1)
                    dve.wait_ge(S["moe0_choice"], 1)
                    split_weights_vector(dve, S, "moe0")
                    experts_vector(dve, S, "moe0")
                    dve.wait_ge(S["moe0_added"], 1)
                    ln_vector(dve, S, "ln4", x_cur, x_norm)
                    fast_vector(dve, S)
                    nc.vector.tensor_copy(x_all[:, bass.ds(g * GT, GT), :], x_cur[:, :, :])

                @block.gpsimd
                def _(pool):
                    nc.gpsimd.tensor_copy(h_cur[:, :], gate0[:, bass.ds(g * GN, GN)]).then_inc(S["h_cur"], 1)
                    fast_gpsimd(pool, S)
            finish_phase(nc, S)

    with ExitStack() as sems:
        S = Signals(nc, sems)
        with nc.Fori(0, GROUPS) as g:
            with nc.Block() as block:
                @block.sync
                def _(sp):
                    sp.dma_start(ctx_cur[:, :, :], tiles(I["ctx_1024"])[:, bass.ds(g * GT, GT), :])\
                        .then_inc(S["ctx_loaded"], 16)
                    sp.wait_ge(S["result"], 1)
                    sp.dma_start(tiles(m.out)[:, bass.ds(g * GT, GT), :], x_cur[:, :, :]).then_inc(S["stored"], 16)
                    sp.wait_ge(S["stored"], 16)

                @block.tensor
                def _(pe):
                    transpose_tiles(pe, S, "ln_unit", lambda t: GT * LN_TURN["ln5"] + t + 1, y, bank(7), "ln5_turned")
                    pe.wait_ge(S["ctx_loaded"], 16)
                    for t in range(GT):
                        tr = nc.tensor.transpose(bank(3)[:, t * P:(t + 1) * P], ctx_cur[:, t, :], ident[:, :])
                    tr.then_inc(S["ctx_turned"], 1)
                    pe.wait_ge(S["ln5_T"], 1)
                    attend_tensor(pe, S, "self", xT, y)
                    transpose_tiles(pe, S, "g1_done", lambda t: 1, y, bank(7), "g1_turned")
                    pe.wait_ge(S["g1_T"], 1)
                    pe.wait_ge(S["ctx_T"], 1)
                    attend_tensor(pe, S, "cross", ctxT, ctx_cur)
                    transpose_tiles(pe, S, "g2_done", lambda t: 1, y, bank(7), "g2_turned")
                    dense_tensor(pe, S, "hid1", xT[:, :], "g2_T")
                    transpose_tiles(pe, S, "ln_unit", lambda t: GT * LN_TURN["ln6"] + t + 1, x_norm, bank(7), "ln6_turned")
                    pe.wait_ge(S["ln6_T"], 1)
                    for t in range(GT):
                        mm = nc.tensor.matmul(bank(1)[:, t * E:(t + 1) * E], xT[:, t * P:(t + 1) * P],
                                              w["gate_w"][:, :], start=True, stop=True)
                    mm.then_inc(S["moe1_logits"], 1)
                    experts_tensor(pe, S, "moe1")

                @block.scalar
                def _(act):
                    nc.scalar.preload_act_table_set(LN_AND_EXP)
                    ln_scalar(act, S, "ln5")
                    lnT_scalar(act, S, "ln5")
                    act.wait_ge(S["ctx_turned"], 1)
                    nc.scalar.activation(ctxT, bank(3), ACT.Copy).then_inc(S["ctx_T"], 1)
                    attend_scalar(act, S, "self")
                    ln_scalar(act, S, "g1")
                    lnT_scalar(act, S, "g1")
                    attend_scalar(act, S, "cross")
                    ln_scalar(act, S, "g2")
                    lnT_scalar(act, S, "g2")
                    dense_scalar(act, S, "hid1")
                    ln_scalar(act, S, "g3")
                    ln_scalar(act, S, "ln6")
                    lnT_scalar(act, S, "ln6")
                    gate_exps_scalar(act, S, "moe1")
                    experts_scalar(act, S, "moe1", ACT.Relu)

                @block.vector
                def _(dve):
                    nc.vector.tensor_copy(x_cur[:, :, :], x_all[:, bass.ds(g * GT, GT), :]).then_inc(S["x_cur"], 1)
                    dve.wait_ge(S["x_cur"], 1)
                    ln_vector(dve, S, "ln5", x_cur, y)
                    dve.wait_ge(S["ln_unit"], GT * (LN_TURN["ln5"] + 1))
                    attend_vector(dve, S, "self", "causal_mask")
                    ln_vector(dve, S, "g1", y, y, (w["ln_g1"][:, :], w["ln_b1"][:, :]))
                    dve.wait_ge(S["g1_done"], 1)
                    attend_vector(dve, S, "cross", "block_mask")
                    ln_vector(dve, S, "g2", y, y, (w["ln_g2"][:, :], w["ln_b2"][:, :]))
                    dve.wait_ge(S["g2_done"], 1)
                    dve.wait_ge(S["hid1_back"], 1)
                    dve.wait_ge(S["g2_turned"], GT)
                    nc.vector.tensor_tensor(y, y, bank(5).rearrange("q (t c) -> q t c", t=GT), ALU.add)\
                        .then_inc(S["hid1_added"], 1)
                    dve.wait_ge(S["hid1_added"], 1)
                    ln_vector(dve, S, "g3", y, y, (w["ln_g3"][:, :], w["ln_b3"][:, :]))
                    dve.wait_ge(S["g3_done"], 1)
                    nc.vector.tensor_tensor(x_cur[:, :, :], x_cur[:, :, :], y, ALU.add).then_inc(S["x5"], 1)
                    dve.wait_ge(S["x5"], 1)
                    ln_vector(dve, S, "ln6", x_cur, x_norm)
                    gate_exps_vector(dve, S, "moe1")
                    nc.vector.scalar_tensor_tensor(out=cw[:, 6], in0=cw[:, 3], scalar=NEG, in1=cw[:, 1],
                                                   op0=ALU.mult, op1=ALU.add).then_inc(S["without_first"], 1)
                    dve.wait_ge(S["without_first"], 1)
                    first_of_max(dve, S, "moe1", cw[:, 6], cw_s[:, 4], cw[:, 2], cw_s[:, 5], cw[:, 7], 5)
                    nc.vector.tensor_tensor(cw[:, 8], cw[:, 3], cw[:, 7], ALU.add).then_inc(S["choose"], 1)
                    dve.wait_ge(S["choose"], 1)
                    nc.vector.tensor_tensor(cw[:, 8], cw[:, 8], cw[:, 5], ALU.mult).then_inc(S["choose"], 1)
                    dve.wait_ge(S["choose"], 2)
                    nc.vector.tensor_tensor(cw[:, 8], cw[:, 8], bcast(cw_s[:, 3], 2, E), ALU.mult)\
                        .then_inc(S["choose"], 1)
                    dve.wait_ge(S["choose"], 3)
                    nc.vector.tensor_reduce(cw_s[:, 6], cw[:, 8], AX_X, ALU.add).then_inc(S["choose"], 1)
                    dve.wait_ge(S["choose"], 4)
                    nc.vector.tensor_scalar(cw_s[:, 7], cw_s[:, 6], 1e-8, None, ALU.add).then_inc(S["choose"], 1)
                    dve.wait_ge(S["choose"], 5)
                    nc.vector.reciprocal(cw_s[:, 8], cw_s[:, 7]).then_inc(S["choose"], 1)
                    dve.wait_ge(S["choose"], 6)
                    nc.vector.tensor_tensor(cw[:, 0], cw[:, 8], bcast(cw_s[:, 8], 2, E), ALU.mult)\
                        .then_inc(S["moe1_choice"], 1)
                    dve.wait_ge(S["moe1_choice"], 1)
                    split_weights_vector(dve, S, "moe1")
                    experts_vector(dve, S, "moe1")
                    dve.wait_ge(S["moe1_added"], 1)
                    nc.vector.tensor_tensor(x_cur[:, :, :], x_cur[:, :, :], x_norm[:, :, :], ALU.add)\
                        .then_inc(S["result"], 1)
            finish_phase(nc, S)


_OUTS = [((BATCH, SEQ, C), "float32")]


def kernel(**inputs):
    import numpy as _np
    import concourse.bacc as _bacc
    from concourse import mybir as _mybir
    from concourse.bass_utils import run_bass_kernel_spmd as _run

    nc = _bacc.Bacc("TRN2", target_bir_lowering=False, num_devices=1)
    arrays, args = {}, {}
    for name in inputs:
        a = _np.ascontiguousarray(inputs[name])
        if a.ndim == 0:
            a = a.reshape(1)
        if name == "L0_xattn_tgt_bias":
            a = a.reshape(SEQ, SEQ)
        arrays[f"in_{name}_dram"] = a
        args[name] = nc.dram_tensor(f"in_{name}_dram", a.shape, _mybir.dt.from_np(a.dtype), kind="ExternalInput").ap()
    outs = [nc.dram_tensor(f"out_{i}_dram", shape, _mybir.dt.from_np(_np.dtype(dtype)), kind="ExternalOutput").ap()
            for i, (shape, dtype) in enumerate(_OUTS)]
    build(nc, args, outs[0])
    r = _run(nc, [arrays], core_ids=[0])
    return r.results[0]["out_0_dram"]
```

```python
from contextlib import ExitStack

import numpy as np

import concourse.bass as bass
from concourse import mybir

F32 = mybir.dt.float32
BF16 = mybir.dt.bfloat16
ACT = mybir.ActivationFunctionType
ALU = mybir.AluOpType
AX_X = mybir.AxisListType.X

P = 128
C = 128
SEQ = 64
BATCH = 64
TOKENS = SEQ * BATCH
TILES = TOKENS // P
GT = 4
GB = 2 * GT
GN = GT * P
GROUPS = TILES // GT
H = 16
D = C // H
STRIPS = 4
HG = H // STRIPS
PAIRS = H // 2
BUFFERS = 3
PARTS = 3
PART_ROWS = 32 * PARTS
PW = 2 * D + 2
GATES = 4
GATE_ORDER = (1, 0, 2, 3)
HID = 512
HC = HID // P
E = 8
EH = 256
EC = EH // P
RED = 16
TD = 64
TW = H * TD
LN_TURN = {"ln1": 0, "ln2": 1, "ln3_first": 0, "ln4": 0, "ln3": 1, "ln5": 0, "g1": 1, "g2": 2, "g3": 3, "ln6": 4}
NEG = -1e30
LN_AND_EXP = "natural_log_exp_and_others"
INV_SQRT_D = float(1.0 / np.sqrt(D))
INV_SQRT_C = float(1.0 / np.sqrt(C))


class Signals:

    def __init__(self, nc, stack):
        self.nc, self.stack, self.made = nc, stack, {}

    def __getitem__(self, name):
        if name not in self.made:
            self.made[name] = self.stack.enter_context(self.nc.semaphore(name))
        return self.made[name]

    def runs(self):
        nums = sorted(s.num for s in self.made.values())
        starts = [n for n in nums if n - 1 not in nums]
        ends = [n + 1 for n in nums if n + 1 not in nums]
        return [range(a, b) for a, b in zip(starts, ends)]


class Shared:

    def __init__(self, four_banks, nc, I, out, sb, tiles, pair, bank, x_all, gate0, gates123, arena, ident, eps5, eps6, one, x_cur,
                 ctx_cur, x_norm, lstm_wh, ln_vector, ln_scalar, transpose_tiles):
        self.nc, self.I, self.out, self.sb, self.tiles, self.pair, self.bank = nc, I, out, sb, tiles, pair, bank
        self.x_all, self.gate0, self.gates123, self.arena, self.ident = x_all, gate0, gates123, arena, ident
        self.eps5, self.eps6, self.one, self.x_cur, self.ctx_cur, self.x_norm = eps5, eps6, one, x_cur, ctx_cur, x_norm
        self.lstm_wh, self.ln_vector, self.ln_scalar = lstm_wh, ln_vector, ln_scalar
        self.transpose_tiles, self.four_banks = transpose_tiles, four_banks


def bcast(ap, axis, count):
    a = ap.unsqueeze(axis)
    shape = list(a.shape)
    shape[axis] = count
    return a.broadcast_to(shape)


def finish_phase(nc, signals):
    for run in signals.runs():
        nc.multi_engine_barrier(list(nc.engines), sems_to_clear=run)


def build(nc, I, out):
    with ExitStack() as whole, nc.allow_non_contiguous_dma(reason="bias columns, once"):
        _build(nc, I, out, whole)


def _build(nc, I, out, whole):
    def sb(name, shape, stack=whole, dtype=F32):
        return stack.enter_context(nc.sbuf_tensor(name, shape, dtype))

    tiles = lambda ap: ap.rearrange("b s d -> (b s) d").rearrange("(t p) d -> p t d", p=P)

    lower = whole.enter_context(nc.psum_tensor("lower_banks", [P, 4, 512], F32))
    upper = whole.enter_context(nc.psum_tensor("upper_banks", [P, 4, 512], F32))
    pair = [half[:, 2 * i:2 * i + 2, :].rearrange("p k n -> p (k n)") for half in (lower, upper) for i in range(2)]

    def bank(i):
        return pair[i // 2][:, (i % 2) * 512:(i % 2) * 512 + 512]

    x_all = sb("x_all", [P, TILES, C])
    gate0 = sb("gate0", [P, TOKENS])
    ident = sb("ident", [P, P])
    eps5 = sb("eps5", [P, 1])
    eps6 = sb("eps6", [P, 1])
    x_cur = sb("x_cur", [P, GT, C])
    ctx_cur = sb("ctx_cur", [P, GT, C])
    x_norm = sb("x_norm", [P, GT, C])
    ln_stats = sb("ln_stats", [P, GT, 6])
    ln_moments = sb("ln_moments", [P, GT, 2])
    ln_logvar = sb("ln_logvar", [P, GT])
    ln_rstd = sb("ln_rstd", [P, GT])
    lstm_wh = sb("lstm_wh", [P, GATES * C])
    one = sb("one", [P, 1])
    arena = sb("arena", [P, (GATES - 1) * TOKENS])

    def ln_vector(e, S, tag, src, dst, affine=None):
        n = LN_TURN[tag]
        for t in range(GT):
            nc.vector.bn_stats(ln_stats[:, t, :], src[:, t, :]).then_inc(S["ln_stats"], 1)
        for t in range(GT):
            e.wait_ge(S["ln_stats"], GT * n + t + 1)
            nc.vector.bn_aggr(ln_moments[:, t, :], ln_stats[:, t, :]).then_inc(S["ln_moments"], 1)
        e.wait_ge(S["ln_rstd"], n + 1)
        for t in range(GT):
            nc.vector.tensor_scalar(dst[:, t, :], src[:, t, :], ln_moments[:, t, 0:1], ln_rstd[:, t:t + 1],
                                    ALU.subtract, ALU.mult).then_inc(S["ln_unit"], 1)
        if affine is not None:
            gain, shift = affine
            e.wait_ge(S["ln_unit"], GT * (n + 1))
            nc.vector.tensor_tensor(dst, dst, bcast(gain, 1, GT), ALU.mult).then_inc(S[f"{tag}_gained"], 1)
            e.wait_ge(S[f"{tag}_gained"], 1)
            nc.vector.tensor_tensor(dst, dst, bcast(shift, 1, GT), ALU.add).then_inc(S[f"{tag}_done"], 1)

    def ln_scalar(e, S, tag):
        n = LN_TURN[tag]
        e.wait_ge(S["ln_moments"], GT * (n + 1))
        nc.scalar.activation(ln_logvar[:, :], ln_moments[:, :, 1], ACT.Ln, bias=eps5[:, 0:1])\
            .then_inc(S["ln_logvar"], 1)
        e.wait_ge(S["ln_logvar"], n + 1)
        nc.scalar.activation(ln_rstd[:, :], ln_logvar[:, :], ACT.Exp, scale=-0.5).then_inc(S["ln_rstd"], 1)

    def transpose_tiles(e, S, ready, ready_count, src, dst_bank, done):
        for t in range(GT):
            e.wait_ge(S[ready], ready_count(t))
            nc.tensor.transpose(dst_bank[:, t * P:(t + 1) * P], src[:, t, :], ident[:, :]).then_inc(S[done], 1)

    gates123 = arena[:, :].rearrange("p (j n) -> p j n", j=GATES - 1)
    m = Shared(lower, nc, I, out, sb, tiles, pair, bank, x_all, gate0, gates123, arena, ident, eps5, eps6, one, x_cur, ctx_cur,
               x_norm, lstm_wh, ln_vector, ln_scalar, transpose_tiles)
    with ExitStack() as mem_a:
        phase_a(m, mem_a)
    with ExitStack() as mem_c:
        m.stack_c = mem_c
        w = phase_b(m, mem_c)
        prepare_c(m, w)
        phase_c(m, w)


def row(ap):
    n = len(ap.shape)
    flat = ap if n == 1 else ap.rearrange({2: "a b -> (a b)", 3: "a b c -> (a b c)"}[n])
    return flat.partition_broadcast(P)


def phase_a(m, stack):
    four_banks = m.four_banks
    nc, I, tiles, pair, bank, ident = m.nc, m.I, m.tiles, m.pair, m.bank, m.ident
    x_all, gate0, gates123, x_cur, ctx_cur, x_norm = m.x_all, m.gate0, m.gates123, m.x_cur, m.ctx_cur, m.x_norm
    eps5, eps6, one, lstm_wh = m.eps5, m.eps6, m.one, m.lstm_wh
    ln_vector, ln_scalar, transpose_tiles = m.ln_vector, m.ln_scalar, m.transpose_tiles

    def sb(name, shape):
        return m.sb(name, shape, stack)

    w_qk = sb("w_qk", [P, 2 * C + 1])
    b_qk = sb("b_qk", [P, 2 * C + 1])
    w_v = {k: sb(f"w_v_{k}", [P, C]) for k in ("lor", "src", "tgt")}
    b_v = {k: sb(f"b_v_{k}", [P, C]) for k in ("lor", "src", "tgt")}
    w_o = {k: sb(f"w_o_{k}", [P, C]) for k in ("lor", "src", "tgt")}
    b_o_lor = sb("b_o_lor", [P, C])
    w_head = {k + s: sb(f"w_head_{k}_{s}", [P, C]) for k in ("src", "tgt") for s in "qk"}
    b_head = {k + s: sb(f"b_head_{k}_{s}", [P, 1]) for k in ("src", "tgt") for s in "qk"}
    b_k_masked = {k: sb(f"b_k_masked_{k}", [P, HG]) for k in ("src", "tgt")}
    head_mask = sb("head_mask", [P, HG])
    head_rows = sb("head_rows", [P, STRIPS, HG])
    b_o_col = sb("b_o_col", [P, 2])
    b_o_sum = sb("b_o_sum", [P, 1])
    lstm_wx = sb("lstm_wx", [P, 2, GATES * C])
    lstm_b = sb("lstm_b", [P, GATES])
    threshold = sb("threshold", [P, 1])
    tgt_bias = sb("tgt_bias", [P, SEQ])
    causal = sb("causal", [P, SEQ])

    xT = sb("xT", [P, GB, 2, SEQ])
    ctxT = sb("ctxT", [P, GB, 2, SEQ])
    x_once = sb("x_once", [P, GN])
    x_twice = sb("x_twice", [P, GB, 2, SEQ])
    qk = sb("qk", [P, GT, 2 * C + 1])
    n_h = GT * 2 * H
    spike_e = sb("spike_e", [P, GT])
    spike_s = sb("spike_s", [P, GT])
    spike = sb("spike", [P, GT])
    heads = {k: (sb(f"qT_{k}", [P, GN]), sb(f"kT_{k}", [P, GB, HG, SEQ])) for k in ("lor", "src", "tgt")}
    V = {k: sb(f"V_{k}", [P, GB, PAIRS, PW]) for k in ("lor", "src", "tgt")}
    score = sb("score", [P, BUFFERS, H, SEQ])
    aux = sb("aux", [P, BUFFERS, H, SEQ])
    spare = aux[:, :, :, :].rearrange("q u h k -> q u (h k)")
    sq = spare[:, 0].rearrange("q (t c) -> q t c", t=GT)
    mapped = spare[:, 1].rearrange("q (t side c) -> q t side c", t=GT, side=2)
    m_mink, m_norm, m_ep, m_en, m_cosh2, m_s, m_p, m_x = (spare[:, 2, n * n_h:(n + 1) * n_h] for n in range(8))
    m_log, m_sinh2, m_rn, m_small = (sb(f"map_{n}", [P, n_h]) for n in ("log", "sinh2", "rn", "small"))
    row_max = sb("row_max", [P, BUFFERS, H])
    PT = sb("PT", [P, PAIRS, P])
    row_rec = sb("row_rec", [P, PAIRS, 2])
    o_tm = {k: sb(f"o_tm_{k}", [P, GT, C]) for k in ("lor", "src")}
    o_tm["tgt"] = o_tm["lor"]
    oT = {k: sb(f"oT_{k}", [P, GN]) for k in ("src", "tgt")}
    cT = sb("cT", [P, GN])

    with ExitStack() as sems:
        S = Signals(nc, sems)
        loads = [
            (x_all[:, :, :], tiles(I["x"])),
            (w_qk[:, 0:2 * C], I["L0_attn_W_qkv"][:, 0:2 * C]),
            (w_qk[:, 2 * C:], I["L0_attn_w_sur"].unsqueeze(1)),
            (b_qk[:, 0:2 * C], row(I["L0_attn_b_qkv"][0:2 * C])),
            (b_qk[:, 2 * C:], row(I["L0_attn_b_sur"])),
            (threshold[:, :], row(I["L0_attn_threshold"])),
            (w_v["lor"][:, :], I["L0_attn_W_qkv"][:, 2 * C:]),
            (b_v["lor"][:, :], row(I["L0_attn_b_qkv"][2 * C:])),
            (w_o["lor"][:, :], I["L0_attn_W_out"]),
            (b_o_lor[:, :], row(I["L0_attn_b_out"])),
            (lstm_wx[:, :, :], I["L0_xattn_lstm_w"][0:2 * C, :].rearrange("(k p) n -> p k n", p=P)),
            (lstm_wh[:, :], I["L0_xattn_lstm_w"][2 * C:, :]),
            (lstm_b[:, :], I["L0_xattn_lstm_b"].rearrange("(c p) -> p c", p=P)),
        ]
        for n, k in enumerate(("src", "tgt")):
            loads += [(w_v[k][:, :], I[f"L0_xattn_{k}_wv"]), (b_v[k][:, :], row(I[f"L0_xattn_{k}_bv"])),
                      (w_o[k][:, :], I[f"L0_xattn_{k}_wo"]),
                      (b_o_col[:, n:n + 1], I[f"L0_xattn_{k}_bo"].unsqueeze(1))]
            for s in "qk":
                loads += [(w_head[k + s][:, :], I[f"L0_xattn_{k}_w{s}"]),
                          (b_head[k + s][:, :], I[f"L0_xattn_{k}_b{s}"].unsqueeze(1))]
        for half in range(2):
            rows = slice(half * SEQ, half * SEQ + SEQ)
            loads += [(tgt_bias[rows, :], I["L0_xattn_tgt_bias"])]
        with nc.Block() as block:
            @block.sync
            def _(sp):
                for dst, src in loads:
                    sp.dma_start(dst, src).then_inc(S["inputs_loaded"], 16)
                sp.wait_ge(S["inputs_loaded"], 16 * len(loads))

            @block.vector
            def _(dve):
                nc.vector.memset(eps5[:, :], 1e-5)
                nc.vector.memset(eps6[:, :], 1e-6)
                nc.vector.memset(one[:, :], 1.0)
                for k in V:
                    nc.vector.memset(V[k][:, :, :, :], 0.0).then_inc(S["V_cleared"], 1)
                dve.wait_ge(S["V_cleared"], len(V))
                for k in V:
                    for half in range(2):
                        rows = slice(half * SEQ, half * SEQ + SEQ)
                        col = 2 * D + half
                        nc.vector.memset(V[k][rows, :, :, col:col + 1], 1.0)
                dve.wait_ge(S["head_rows"], 3)
                nc.vector.tensor_reduce(head_mask[:, :], head_rows[:, :, :].rearrange("c s g -> c g s"), AX_X, ALU.add)\
                    .then_inc(S["head_mask"], 1)
                dve.wait_ge(S["head_mask"], 1)
                dve.wait_ge(S["inputs_loaded"], 16 * len(loads))
                for k in ("src", "tgt"):
                    nc.vector.tensor_scalar(b_k_masked[k][:, :], head_mask[:, :], b_head[k + "k"][:, 0:1], None, ALU.mult)
                nc.vector.tensor_tensor(b_o_sum[:, :], b_o_col[:, 0:1], b_o_col[:, 1:2], ALU.add)
                for k in ("srcq", "tgtq"):
                    nc.vector.tensor_scalar(b_head[k][:, :], b_head[k][:, :], INV_SQRT_D, None, ALU.mult)

            @block.gpsimd
            def _(pool):
                nc.gpsimd.memset(ident[:, :], 0.0).then_inc(S["ident_cleared"], 1)
                nc.gpsimd.memset(causal[:, :], 0.0).then_inc(S["causal_cleared"], 1)
                nc.gpsimd.memset(head_rows[:, :, :], 1.0).then_inc(S["head_rows"], 1)
                by_h = head_rows[:, :, :].rearrange("c s g -> c (s g)")
                pool.wait_ge(S["head_rows"], 1)
                nc.gpsimd.affine_select(out=by_h, in_=by_h, compare_op=ALU.is_ge, fill=0.0, base=0,
                                        pattern=[[-D, H]], channel_multiplier=1).then_inc(S["head_rows"], 1)
                pool.wait_ge(S["head_rows"], 2)
                nc.gpsimd.affine_select(out=by_h, in_=by_h, compare_op=ALU.is_ge, fill=0.0, base=D - 1,
                                        pattern=[[D, H]], channel_multiplier=-1).then_inc(S["head_rows"], 1)
                pool.wait_ge(S["ident_cleared"], 1)
                nc.gpsimd.affine_select(out=ident[:, :], in_=ident[:, :], compare_op=ALU.not_equal, fill=1.0,
                                        base=0, pattern=[[-1, P]], channel_multiplier=1)\
                    .then_inc(S["ident_made"], 1)
                pool.wait_ge(S["causal_cleared"], 1)
                for half in range(2):
                    rows = slice(half * SEQ, half * SEQ + SEQ)
                    pool.wait_ge(S["ident_made"], half + 1)
                    nc.gpsimd.affine_select(out=causal[rows, :], in_=causal[rows, :], compare_op=ALU.is_ge, fill=NEG,
                                            base=0, pattern=[[-1, SEQ]], channel_multiplier=1)\
                        .then_inc(S["ident_made"], 1)
        finish_phase(nc, S)

    def scores_tensor(e, S, tag, u, kind, t):
        qT, kT = heads[kind]
        if u >= 1:
            e.wait_ge(S[f"{tag}_score_read"], u)
        for b in range(2):
            for s in range(STRIPS):
                rows, cols = slice(32 * s, 32 * s + 32), slice((2 * t + b) * SEQ, (2 * t + b + 1) * SEQ)
                mm = nc.tensor.matmul(bank(s)[b * SEQ:(b + 1) * SEQ, 0:HG * SEQ], qT[rows, cols],
                                      kT[rows, 2 * t + b, :, :].rearrange("r g k -> r (g k)"), start=True, stop=True)
        mm.then_inc(S[f"{tag}_score"], 1)

    def turn_tensor(e, S, tag, u):
        e.wait_ge(S[f"{tag}_prob"], u + 1)
        for half in range(2):
            if u >= 1:
                e.wait_ge(S[f"{tag}_PT_act" if half == 0 else f"{tag}_PT_dve"], u)
            for p in range(4 * half, 4 * half + 4):
                tr = nc.tensor.transpose(pair[2][:, p * P:(p + 1) * P], score[:, u % BUFFERS, 2 * p:2 * p + 2, :],
                                         ident[:, :])
            tr.then_inc(S[f"{tag}_turned"], 1)

    def values_tensor(e, S, tag, u, kind, t):
        e.wait_ge(S[f"{tag}_PT_act"], u + 1)
        e.wait_ge(S[f"{tag}_PT_dve"], u + 1)
        if u >= 1:
            e.wait_ge(S[f"{tag}_normed"], u)
        for b in range(2):
            for p in range(PAIRS):
                mm = nc.tensor.matmul(bank(6)[b * SEQ:(b + 1) * SEQ, p * PW:(p + 1) * PW],
                                      PT[:, p, b * SEQ:(b + 1) * SEQ], V[kind][:, 2 * t + b, p, :],
                                      start=True, stop=True)
        mm.then_inc(S[f"{tag}_summed"], 1)

    lead = {"lor": 3, "mha": 2}

    def steps(tag):
        return range(-lead[tag], len(units[tag]))

    def is_unit(tag, u):
        return 0 <= u < len(units[tag])

    def scores_step_tensor(e, S, tag, k):
        u = k + lead[tag]
        if k >= 0:
            turn_tensor(e, S, tag, k)
        if is_unit(tag, u):
            scores_tensor(e, S, tag, u, *units[tag][u])

    def values_step_tensor(e, S, tag, k):
        if k >= 0:
            values_tensor(e, S, tag, k, *units[tag][k])

    def scores_step_vector(e, S, tag, k):
        u = k + lead[tag]
        if tag == "lor" and is_unit(tag, k + 1):
            max_vector(e, S, tag, k + 1, "lor")
        if k >= 0:
            turned_vector(e, S, tag, k)
        if is_unit(tag, u):
            front_vector(e, S, tag, u, *units[tag][u])
            if tag == "mha":
                max_vector(e, S, tag, u, units[tag][u][0])

    def values_step_vector(e, S, tag, k):
        if k >= 0:
            back_vector(e, S, tag, k, *units[tag][k])

    def step_scalar(e, S, tag, k):
        u = k + lead[tag]
        if k >= 0:
            turned_scalar(e, S, tag, k)
        if tag == "lor":
            if is_unit(tag, k + 2):
                arccosh_scalar(e, S, k + 2)
            if is_unit(tag, k + 1):
                exp_scalar(e, S, tag, k + 1)
            if is_unit(tag, u):
                lorentz_scalar(e, S, u)
        elif is_unit(tag, u):
            exp_scalar(e, S, tag, u)

    def step_gpsimd(e, S, tag, k):
        if tag == "lor":
            u = k + 2
            if is_unit(tag, u):
                ax = aux[:, u % BUFFERS, :, :]
                e.wait_ge(S["lor_root"], u + 1)
                nc.gpsimd.tensor_tensor(ax, ax, score[:, u % BUFFERS, :, :], ALU.add).then_inc(S["lor_arg"], 1)
            if is_unit(tag, k + 1):
                shift_gpsimd(e, S, tag, k + 1)
        elif is_unit(tag, k + lead[tag]):
            shift_gpsimd(e, S, tag, k + lead[tag])

    def lorentz_scalar(act, S, u):
        ax = aux[:, u % BUFFERS, :, :]
        act.wait_ge(S["lor_w"], u + 1)
        nc.scalar.activation(ax, ax, ACT.Ln).then_inc(S["lor_logw"], 1)
        act.wait_ge(S["lor_logw"], u + 1)
        nc.scalar.activation(ax, ax, ACT.Exp, scale=0.5).then_inc(S["lor_root"], 1)

    def arccosh_scalar(act, S, u):
        ax = aux[:, u % BUFFERS, :, :]
        act.wait_ge(S["lor_arg"], u + 1)
        nc.scalar.activation(ax, ax, ACT.Ln, bias=one[:, 0:1]).then_inc(S["lor_dist"], 1)
        act.wait_ge(S["lor_dist"], u + 1)
        nc.scalar.activation(ax, ax, ACT.Square).then_inc(S["lor_dist2"], 1)

    def front_vector(e, S, tag, u, kind, t):
        ps = four_banks[:, :, 0:HG * SEQ]
        wide = score[:, u % BUFFERS, :, :].rearrange("q (s g) k -> q s (g k)", s=STRIPS)
        sc, ax = score[:, u % BUFFERS, :, :], aux[:, u % BUFFERS, :, :]
        e.wait_ge(S[f"{tag}_score"], u + 1)
        if u >= BUFFERS:
            e.wait_ge(S[f"{tag}_turned"], 2 * (u - BUFFERS + 1))
        if kind == "lor":
            nc.vector.tensor_scalar(wide, ps, float(np.float32(1.0 + 1e-7)), -1.0, ALU.max, ALU.add)\
                .then_inc(S[f"{tag}_score_read"], 1)
            e.wait_ge(S[f"{tag}_score_read"], u + 1)
            nc.vector.scalar_tensor_tensor(out=ax, in0=sc, scalar=2.0, in1=sc, op0=ALU.add, op1=ALU.mult)\
                .then_inc(S[f"{tag}_w"], 1)
        else:
            bias = src_cur[:, t, :] if kind == "src" else tgt_bias[:, :]
            nc.vector.tensor_tensor(score[:, u % BUFFERS, :, :].rearrange("q (s g) k -> q s g k", s=STRIPS),
                                    ps.rearrange("q s (g k) -> q s g k", g=HG), bcast(bcast(bias, 1, HG), 1, STRIPS),
                                    ALU.add).then_inc(S[f"{tag}_score_read"], 1)

    def max_vector(e, S, tag, u, kind):
        sc, ax = score[:, u % BUFFERS, :, :], aux[:, u % BUFFERS, :, :]
        if kind == "lor":
            e.wait_ge(S[f"{tag}_dist2"], u + 1)
            nc.vector.scalar_tensor_tensor(out=sc, in0=ax, scalar=-INV_SQRT_D, in1=bcast(causal[:, :], 1, H),
                                           op0=ALU.mult, op1=ALU.add).then_inc(S[f"{tag}_masked"], 1)
            e.wait_ge(S[f"{tag}_masked"], u + 1)
        else:
            e.wait_ge(S[f"{tag}_score_read"], u + 1)
        nc.vector.tensor_reduce(row_max[:, u % BUFFERS, :], sc, AX_X, ALU.max).then_inc(S[f"{tag}_max"], 1)

    def turned_vector(e, S, tag, u):
        e.wait_ge(S[f"{tag}_turned"], 2 * u + 2)
        if u >= 1:
            e.wait_ge(S[f"{tag}_summed"], u)
        nc.vector.tensor_copy(PT[:, 4:8, :], pair[2][:, 512:1024].rearrange("k (p q) -> k p q", p=4))\
            .then_inc(S[f"{tag}_PT_dve"], 1)

    def back_vector(e, S, tag, u, kind, t):
        e.wait_ge(S[f"{tag}_summed"], u + 1)
        O = bank(6)[:, 0:PAIRS * PW].rearrange("q (p w) -> q p w", w=PW)
        nc.vector.reciprocal(row_rec[:, :, :], O[:, :, 2 * D:]).then_inc(S[f"{tag}_rec"], 1)
        e.wait_ge(S[f"{tag}_rec"], u + 1)
        if kind == "lor":
            nc.vector.tensor_scalar(row_rec[:, :, :], row_rec[:, :, :], spike[:, t:t + 1], None, ALU.mult)\
                .then_inc(S[f"{tag}_spiked"], 1)
            e.wait_ge(S[f"{tag}_spiked"], u + 1)
        nc.vector.tensor_tensor(o_tm[kind][:, t, :].rearrange("q (p two d) -> q p two d", two=2, d=D),
                                O[:, :, 0:2 * D].rearrange("q p (two d) -> q p two d", two=2),
                                bcast(row_rec[:, :, :], 3, D), ALU.mult).then_inc(S[f"{tag}_normed"], 1)

    def shift_gpsimd(e, S, tag, u):
        e.wait_ge(S[f"{tag}_max"], u + 1)
        nc.gpsimd.tensor_tensor(score[:, u % BUFFERS, :, :], score[:, u % BUFFERS, :, :], bcast(row_max[:, u % BUFFERS, :], 2, SEQ),
                                ALU.subtract).then_inc(S[f"{tag}_shifted"], 1)

    def exp_scalar(e, S, tag, u):
        e.wait_ge(S[f"{tag}_shifted"], u + 1)
        nc.scalar.activation(score[:, u % BUFFERS, :, :], score[:, u % BUFFERS, :, :], ACT.Exp).then_inc(S[f"{tag}_prob"], 1)

    def turned_scalar(e, S, tag, u):
        e.wait_ge(S[f"{tag}_turned"], 2 * u + 1)
        if u >= 1:
            e.wait_ge(S[f"{tag}_summed"], u)
        nc.scalar.activation(PT[:, 0:4, :], pair[2][:, 0:512].rearrange("k (p q) -> k p q", p=4), ACT.Copy)\
            .then_inc(S[f"{tag}_PT_act"], 1)

    def fill_V_vector(kind, src, b0, count):
        src = src.rearrange("k (b p two d) -> k b p two d", b=count, p=PAIRS, two=2)
        for half in range(2):
            rows = slice(half * SEQ, half * SEQ + SEQ)
            bias = b_v[kind][rows, :].rearrange("k (p two d) -> k p two d", p=PAIRS, two=2)[:, :, half, :]
            fill = nc.vector.tensor_tensor(V[kind][rows, b0:b0 + count, :, half * D:half * D + D],
                                           src[rows, :, :, half, :], bcast(bias, 1, count), ALU.add)
        return fill

    src_cur = sb("src_cur", [P, GT, SEQ])
    masks = I["mask_Bx1x1xS2_ff0"].rearrange("(t two) a b s -> two t (a b s)", two=2)
    by_seq = lambda ap: ap.rearrange("c (b s) -> c b s", s=SEQ)
    units = {"lor": [("lor", t) for t in range(GT)], "mha": [(k, t) for k in ("src", "tgt") for t in range(GT)]}
    n_l, n_m = len(units["lor"]), len(units["mha"])

    def qk_tensor(pe, S, t):
        pe.wait_ge(S["ln1_T"], 2)
        if t >= 1:
            pe.wait_ge(S["lor_qk_sb"], t)
        nc.tensor.matmul(bank(7)[:, 0:2 * C + 1], x_once[:, t * P:(t + 1) * P], w_qk[:, :],
                         start=True, stop=True).then_inc(S["lor_qk"], 1)

    def qk_vector(dve, S, t):
        dve.wait_ge(S["lor_qk"], t + 1)
        nc.vector.tensor_tensor(qk[:, t, :], bank(7)[:, 0:2 * C + 1], b_qk[:, :], ALU.add)\
            .then_inc(S["lor_qk_sb"], 1)

    def lor_values_tensor(pe, S, half):
        if half == 0:
            pe.wait_ge(S["lor_qk_sb"], GT)
        else:
            pe.wait_ge(S["lor_V"], 1)
        for n in range(GB // 2):
            mm = nc.tensor.matmul(bank(7)[:, n * C:(n + 1) * C], x_twice[:, half * GB // 2 + n, :, :],
                                  w_v["lor"][:, :], start=True, stop=True)
        mm.then_inc(S["lor_v"], 1)

    def lor_values_vector(dve, S, half):
        dve.wait_ge(S["lor_v"], half + 1)
        fill_V_vector("lor", bank(7), half * GB // 2, GB // 2).then_inc(S["lor_V"], 1)

    def context_tensor(pe, S):
        pe.wait_ge(S["ctx_loaded"], 16)
        pe.wait_ge(S["lor_V"], 2)
        for t in range(GT):
            tr = nc.tensor.transpose(bank(7)[:, t * P:(t + 1) * P], ctx_cur[:, t, :], ident[:, :])
        tr.then_inc(S["ctx_turned"], 1)

    def mapped_tensor(pe, S, side):
        if side == 0:
            pe.wait_ge(S["ctx_T"], 1)
            pe.wait_ge(S["mapped"], 4)
        else:
            pe.wait_ge(S["lor_qT"], 1)
        for t in range(GT):
            tr = nc.tensor.transpose(bank(7)[:, t * P:(t + 1) * P], mapped[:, t, side, :], ident[:, :])
        tr.then_inc(S["mapped_turned"], 1)

    def twice_scalar(dst, b):
        return nc.scalar.activation(dst, bcast(bank(b).rearrange("c (b s) -> c b s", b=GB), 2, 2), ACT.Copy)

    def ln1_turned_scalar(act, S):
        act.wait_ge(S["ln1_turned"], GT)
        nc.scalar.activation(x_once[:, :], bank(7), ACT.Copy).then_inc(S["ln1_T"], 1)
        twice_scalar(x_twice[:, :, :, :], 7).then_inc(S["ln1_T"], 1)

    def context_scalar(act, S):
        act.wait_ge(S["ctx_turned"], 1)
        twice_scalar(ctxT[:, :, :, :], 7).then_inc(S["ctx_T"], 1)

    def map_exps_scalar(act, S):
        act.wait_ge(S["mink"], 1)
        nc.scalar.activation(m_log[:, :], m_mink[:, :], ACT.Ln).then_inc(S["norm_log"], 1)
        act.wait_ge(S["norm_log"], 1)
        nc.scalar.activation(m_norm[:, :], m_log[:, :], ACT.Exp, scale=0.5).then_inc(S["norm"], 1)
        act.wait_ge(S["norm"], 1)
        nc.scalar.activation(m_ep[:, :], m_norm[:, :], ACT.Exp).then_inc(S["exps"], 1)
        nc.scalar.activation(m_en[:, :], m_norm[:, :], ACT.Exp, scale=-1.0).then_inc(S["exps"], 1)
        nc.scalar.activation(spike_e[:, :], qk[:, :, 2 * C], ACT.Exp, scale=-1.0).then_inc(S["spike_e"], 1)

    def mapped_q_scalar(act, S):
        act.wait_ge(S["mapped_turned"], 1)
        nc.scalar.activation(heads["lor"][0][:, :], bank(7), ACT.Copy).then_inc(S["lor_qT"], 1)

    def mapped_k_scalar(act, S):
        act.wait_ge(S["mapped_turned"], 2)
        for hg in range(HG):
            nc.scalar.activation(heads["lor"][1][:, :, hg, :], by_seq(bank(7)), ACT.Copy,
                                 scale=head_mask[:, hg:hg + 1]).then_inc(S["lor_kT"], 1)

    def map_norm_vector(dve, S):
        dve.wait_ge(S["sq"], 1)
        sq4 = sq.rearrange("q t (h d) -> q (t h) d", d=D)
        nc.vector.tensor_reduce(m_x[:, :], sq4[:, :, 1:D], AX_X, ALU.add).then_inc(S["map_v"], 1)
        dve.wait_ge(S["map_v"], 1)
        nc.vector.tensor_tensor(m_x[:, :], m_x[:, :], sq4[:, :, 0], ALU.subtract).then_inc(S["map_v"], 1)
        dve.wait_ge(S["map_v"], 2)
        nc.vector.tensor_scalar(m_mink[:, :], m_x[:, :], 1e-8, None, ALU.max).then_inc(S["mink"], 1)
        dve.wait_ge(S["mink"], 1)

    def map_series_vector(dve, S):
        nc.vector.tensor_scalar(m_x[:, :], m_mink[:, :], 1.0, None, ALU.min).then_inc(S["map_v"], 1)
        nc.vector.tensor_scalar(m_small[:, :], m_mink[:, :], 1.0, None, ALU.is_lt).then_inc(S["map_small"], 1)
        dve.wait_ge(S["map_v"], 3)
        nc.vector.tensor_scalar(m_p[:, :], m_x[:, :], 1.0 / 362880, None, ALU.mult).then_inc(S["map_v"], 1)
        for n, coeff in enumerate((1.0 / 5040, 1.0 / 120, 1.0 / 6)):
            dve.wait_ge(S["map_v"], 4 + n)
            nc.vector.scalar_tensor_tensor(out=m_p[:, :], in0=m_p[:, :], scalar=coeff, in1=m_x[:, :],
                                           op0=ALU.add, op1=ALU.mult).then_inc(S["map_v"], 1)
        dve.wait_ge(S["map_v"], 7)

    def map_scale_vector(dve, S):
        dve.wait_ge(S["exps"], 2)
        nc.vector.tensor_tensor(m_cosh2[:, :], m_ep[:, :], m_en[:, :], ALU.add).then_inc(S["cosh2"], 1)
        nc.vector.tensor_tensor(m_sinh2[:, :], m_ep[:, :], m_en[:, :], ALU.subtract).then_inc(S["map_e"], 1)
        nc.vector.reciprocal(m_rn[:, :], m_norm[:, :]).then_inc(S["map_e"], 1)
        dve.wait_ge(S["map_e"], 2)
        nc.vector.scalar_tensor_tensor(out=m_s[:, :], in0=m_sinh2[:, :], scalar=0.5, in1=m_rn[:, :],
                                       op0=ALU.mult, op1=ALU.mult).then_inc(S["map_e"], 1)
        dve.wait_ge(S["map_e"], 3)
        nc.vector.scalar_tensor_tensor(out=m_p[:, :], in0=m_p[:, :], scalar=1.0, in1=m_s[:, :],
                                       op0=ALU.add, op1=ALU.subtract).then_inc(S["map_e"], 1)
        dve.wait_ge(S["map_e"], 4)
        dve.wait_ge(S["map_small"], 1)
        nc.vector.tensor_tensor(m_p[:, :], m_p[:, :], m_small[:, :], ALU.mult).then_inc(S["map_e"], 1)
        dve.wait_ge(S["map_e"], 5)
        nc.vector.tensor_tensor(m_s[:, :], m_s[:, :], m_p[:, :], ALU.add).then_inc(S["map_s"], 1)
        dve.wait_ge(S["map_s"], 1)
        dve.wait_ge(S["cosh2"], 1)
        dve.wait_ge(S["spike_e"], 1)
        nc.vector.tensor_scalar(spike_s[:, :], spike_e[:, :], 1.0, None, ALU.add).then_inc(S["spike_v"], 1)
        dve.wait_ge(S["spike_v"], 1)
        nc.vector.reciprocal(spike_s[:, :], spike_s[:, :]).then_inc(S["spike_v"], 1)
        dve.wait_ge(S["spike_v"], 2)
        nc.vector.tensor_scalar(spike[:, :], spike_s[:, :], threshold[:, 0:1], None, ALU.is_gt)\
            .then_inc(S["spike_v"], 1)
        dve.wait_ge(S["spike_v"], 3)
        s4 = m_s[:, :].rearrange("q (t side h) -> q t side h", t=GT, side=2)
        nc.vector.tensor_scalar(s4[:, :, 0, :], s4[:, :, 0, :], -1.0, None, ALU.mult).then_inc(S["map_s"], 1)
        dve.wait_ge(S["map_s"], 2)

    def mapped_vector(dve, S):
        by_head = mapped[:, :, :, :].rearrange("q t side (h d) -> q t (side h) d", d=D)
        of_qk = qk[:, :, 0:2 * C].rearrange("q t (e d) -> q t e d", d=D)
        c3, s3 = (ap[:, :].rearrange("q (t e) -> q t e", t=GT) for ap in (m_cosh2, m_s))
        for half in range(2):
            ts = slice(2 * half, 2 * half + 2)
            nc.vector.tensor_scalar(by_head[:, ts, :, 0], c3[:, ts], 0.5, None, ALU.mult)\
                .then_inc(S["mapped"], 1)
            nc.vector.tensor_tensor(by_head[:, ts, :, 1:D], of_qk[:, ts, :, 1:D], bcast(s3[:, ts], 3, D - 1),
                                    ALU.mult).then_inc(S["mapped"], 1)

    def mha_turn_tensor(pe, S, n, k):
        pe.wait_ge(S["mha_normed"], n_m)
        for t in range(GT):
            tr = nc.tensor.transpose(bank(6 + n)[:, t * P:(t + 1) * P], o_tm[k][:, t, :], ident[:, :])
        tr.then_inc(S["mha_o_turned"], 1)

    def context_sum_tensor(pe, S):
        pe.wait_ge(S["mha_oT"], 2)
        nc.tensor.matmul(bank(4), w_o["src"][:, :], oT["src"][:, :], start=True, stop=False)
        nc.tensor.matmul(bank(4), w_o["tgt"][:, :], oT["tgt"][:, :], start=False, stop=True).then_inc(S["c"], 1)

    gate_bank = (5, 6, 7, 4)

    def gate_tensor(pe, S, n):
        j = GATE_ORDER[n]
        nc.tensor.matmul(bank(gate_bank[n]), lstm_wx[:, 0, j * C:(j + 1) * C], xT[:, :, 0, :], start=True, stop=False)
        if n == 0:
            pe.wait_ge(S["cT"], 1)
        nc.tensor.matmul(bank(gate_bank[n]), lstm_wx[:, 1, j * C:(j + 1) * C], cT[:, :],
                         start=False, stop=True).then_inc(S["gate_x"], 1)

    def mha_turned_scalar(act, S, n, k):
        act.wait_ge(S["mha_o_turned"], n + 1)
        nc.scalar.activation(oT[k][:, :], bank(6 + n), ACT.Copy).then_inc(S["mha_oT"], 1)

    def context_sum_scalar(act, S):
        act.wait_ge(S["c"], 1)
        nc.scalar.activation(cT[:, :], bank(4), ACT.Identity, bias=b_o_sum[:, 0:1]).then_inc(S["cT"], 1)

    def gate_scalar(act, S, n, group):
        act.wait_ge(S["gate_x"], n + 1)
        cols = bass.ds(group * GN, GN)
        nc.scalar.activation(gate0[:, cols] if n == 0 else gates123[:, n - 1, cols], bank(gate_bank[n]), ACT.Identity,
                             bias=lstm_b[:, GATE_ORDER[n]:GATE_ORDER[n] + 1]).then_inc(S["gates_stored"], 1)

    def first_stage(S, ahead, behind):
        has_ahead, has_behind = ahead is not None, behind is not None
        with nc.Block() as block:
            @block.sync
            def _(sp):
                if has_ahead:
                    sp.dma_start(ctx_cur[:, :, :], tiles(I["ctx_1024"])[:, bass.ds(ahead * GT, GT), :])\
                        .then_inc(S["ctx_loaded"], 16)
                    if has_behind:
                        sp.wait_ge(S["mha_score_read"], GT)
                    for half in range(2):
                        sp.dma_start(src_cur[half * SEQ:(half + 1) * SEQ, :, :],
                                     masks[half][bass.ds(ahead * GT, GT), :].partition_broadcast(SEQ))\
                            .then_inc(S["mask_loaded"], 16)
                    sp.wait_ge(S["ctx_loaded"], 16)
                    sp.wait_ge(S["mask_loaded"], 32)

            @block.tensor
            def _(pe):
                for k in steps("mha"):
                    if has_behind:
                        scores_step_tensor(pe, S, "mha", k)
                    if has_ahead and k in (0, 1):
                        qk_tensor(pe, S, 2 * k)
                    if has_ahead and k == 2:
                        lor_values_tensor(pe, S, 0)
                    if has_ahead and k == 3:
                        context_tensor(pe, S)
                    if has_ahead and k in (5, 6):
                        mapped_tensor(pe, S, k - 5)
                    if has_behind:
                        values_step_tensor(pe, S, "mha", k)
                    if has_ahead and k == -1:
                        transpose_tiles(pe, S, "ln_unit", lambda t: GT * LN_TURN["ln1"] + t + 1, x_norm, bank(7), "ln1_turned")
                    if has_ahead and k in (0, 1):
                        qk_tensor(pe, S, 2 * k + 1)
                    if has_ahead and k == 2:
                        lor_values_tensor(pe, S, 1)
                if has_ahead:
                    pe.wait_ge(S["lor_kT"], HG)
                for k in steps("lor"):
                    if has_behind and k == 0:
                        pe.wait_ge(S["gates_stored"], GATES)
                    if has_ahead:
                        scores_step_tensor(pe, S, "lor", k)
                    if has_behind and k == -3:
                        for n, kind in enumerate(("src", "tgt")):
                            mha_turn_tensor(pe, S, n, kind)
                        context_sum_tensor(pe, S)
                    if has_behind and k == -1:
                        for j in range(GATES):
                            gate_tensor(pe, S, j)
                    if has_ahead:
                        values_step_tensor(pe, S, "lor", k)
                if has_ahead:
                    pe.wait_ge(S["lor_normed"], n_l)
                    for t in range(GT):
                        tr = nc.tensor.transpose(bank(7)[:, t * P:(t + 1) * P], o_tm["lor"][:, t, :], ident[:, :])
                    tr.then_inc(S["lor_o_turned"], 1)
                    pe.wait_ge(S["lor_oT"], 1)
                    for t in range(GT):
                        mm = nc.tensor.matmul(bank(6)[:, t * P:(t + 1) * P], oT["src"][:, t * P:(t + 1) * P],
                                              w_o["lor"][:, :], start=True, stop=True)
                    mm.then_inc(S["lor_y"], 1)
                    for b in range(GB):
                        mm = nc.tensor.matmul(pair[2][:, b * C:(b + 1) * C], ctxT[:, b, :, :], w_v["src"][:, :],
                                              start=True, stop=True)
                    mm.then_inc(S["src_v"], 1)
                    nc.tensor.matmul(bank(1), w_head["srck"][:, :], ctxT[:, :, 0, :], start=True, stop=True)\
                        .then_inc(S["proj"], 1)
                    transpose_tiles(pe, S, "ln_unit", lambda t: GT * LN_TURN["ln2"] + t + 1, x_norm, bank(7), "ln2_turned")
                    pe.wait_ge(S["ln2_T"], 1)
                    for n, k in ((0, "srcq"), (2, "tgtq"), (3, "tgtk")):
                        nc.tensor.matmul(bank(n), w_head[k][:, :], xT[:, :, 0, :], start=True, stop=True)\
                            .then_inc(S["proj"], 1)
                    pe.wait_ge(S["src_V"], 1)
                    for b in range(GB):
                        mm = nc.tensor.matmul(pair[2][:, b * C:(b + 1) * C], xT[:, b, :, :], w_v["tgt"][:, :],
                                              start=True, stop=True)
                    mm.then_inc(S["tgt_v"], 1)

            @block.scalar
            def _(act):
                nc.scalar.preload_act_table_set(LN_AND_EXP)
                for k in steps("mha"):
                    if has_ahead and k == -2:
                        ln_scalar(act, S, "ln1")
                    if has_behind:
                        step_scalar(act, S, "mha", k)
                    if has_ahead and k == -1:
                        ln1_turned_scalar(act, S)
                    if has_ahead and k == 3:
                        context_scalar(act, S)
                    if has_ahead and k == 4:
                        map_exps_scalar(act, S)
                    if has_ahead and k == 5:
                        mapped_q_scalar(act, S)
                    if has_ahead and k == 6:
                        mapped_k_scalar(act, S)
                for k in steps("lor"):
                    if has_behind and k == -3:
                        for n, kind in enumerate(("src", "tgt")):
                            mha_turned_scalar(act, S, n, kind)
                    if has_ahead:
                        step_scalar(act, S, "lor", k)
                    if has_behind and k == -3:
                        context_sum_scalar(act, S)
                    if has_behind and k == -1:
                        for j in range(GATES):
                            gate_scalar(act, S, j, behind)
                if has_ahead:
                    act.wait_ge(S["lor_o_turned"], 1)
                    nc.scalar.activation(oT["src"][:, :], bank(7), ACT.Copy).then_inc(S["lor_oT"], 1)
                    act.wait_ge(S["proj"], 1)
                    for hg in range(HG):
                        nc.scalar.activation(heads["src"][1][:, :, hg, :], by_seq(bank(1)), ACT.Identity,
                                             bias=b_k_masked["src"][:, hg:hg + 1], scale=head_mask[:, hg:hg + 1])
                    ln_scalar(act, S, "ln2")
                    act.wait_ge(S["ln2_turned"], GT)
                    twice_scalar(xT[:, :, :, :], 7).then_inc(S["ln2_T"], 1)
                    for n, (b, k) in enumerate(((0, "src"), (2, "tgt"))):
                        act.wait_ge(S["proj"], n + 2)
                        nc.scalar.activation(heads[k][0][:, :], bank(b), ACT.Identity, bias=b_head[k + "q"][:, 0:1],
                                             scale=INV_SQRT_D)

            @block.vector
            def _(dve):
                for k in steps("mha"):
                    if has_behind:
                        scores_step_vector(dve, S, "mha", k)
                    if has_ahead and k in (0, 1):
                        qk_vector(dve, S, 2 * k)
                    if has_ahead and k == 2:
                        lor_values_vector(dve, S, 0)
                    if has_behind:
                        values_step_vector(dve, S, "mha", k)
                    if has_ahead and k == -2:
                        nc.vector.tensor_copy(x_cur[:, :, :], x_all[:, bass.ds(ahead * GT, GT), :])\
                            .then_inc(S["x_cur"], 1)
                        dve.wait_ge(S["x_cur"], 1)
                        ln_vector(dve, S, "ln1", x_cur, x_norm)
                    if has_ahead and k in (0, 1):
                        qk_vector(dve, S, 2 * k + 1)
                    if has_ahead and k == 2:
                        lor_values_vector(dve, S, 1)
                    if has_ahead and k == 3:
                        map_norm_vector(dve, S)
                        map_series_vector(dve, S)
                    if has_ahead and k == 4:
                        map_scale_vector(dve, S)
                        mapped_vector(dve, S)
                for k in steps("lor"):
                    if has_ahead:
                        scores_step_vector(dve, S, "lor", k)
                        values_step_vector(dve, S, "lor", k)
                if has_ahead:
                    dve.wait_ge(S["lor_y"], 1)
                    x_flat = x_cur[:, :, :].rearrange("q t c -> q (t c)")
                    nc.vector.tensor_tensor(x_flat, x_flat, bank(6), ALU.add).then_inc(S["lor_added"], 1)
                    dve.wait_ge(S["lor_added"], 1)
                    nc.vector.tensor_tensor(x_cur[:, :, :], x_cur[:, :, :], bcast(b_o_lor[:, :], 1, GT), ALU.add)\
                        .then_inc(S["lor_added"], 1)
                    dve.wait_ge(S["lor_added"], 2)
                    ln_vector(dve, S, "ln2", x_cur, x_norm)
                    nc.vector.tensor_copy(x_all[:, bass.ds(ahead * GT, GT), :], x_cur[:, :, :])
                    dve.wait_ge(S["src_v"], 1)
                    fill_V_vector("src", pair[2], 0, GB).then_inc(S["src_V"], 1)
                    dve.wait_ge(S["proj"], 4)
                    for hg in range(HG):
                        nc.vector.tensor_scalar(heads["tgt"][1][:, :, hg, :], by_seq(bank(3)), head_mask[:, hg:hg + 1],
                                                b_k_masked["tgt"][:, hg:hg + 1], ALU.mult, ALU.add)
                    dve.wait_ge(S["tgt_v"], 1)
                    fill_V_vector("tgt", pair[2], 0, GB)

            @block.gpsimd
            def _(pool):
                for k in steps("mha"):
                    if has_behind:
                        step_gpsimd(pool, S, "mha", k)
                    if has_ahead and k == 2:
                        pool.wait_ge(S["lor_qk_sb"], GT)
                        nc.gpsimd.tensor_tensor(sq, qk[:, :, 0:2 * C], qk[:, :, 0:2 * C], ALU.mult)\
                            .then_inc(S["sq"], 1)
                for k in steps("lor"):
                    if has_ahead:
                        step_gpsimd(pool, S, "lor", k)
        finish_phase(nc, S)

    with ExitStack() as sems:
        S = Signals(nc, sems)
        first_stage(S, 0, None)
        with nc.Fori(0, GROUPS - 1) as g:
            first_stage(S, g + 1, g)
        first_stage(S, None, GROUPS - 1)


LSTM_UNROLL = 16


def phase_b(m, stack):
    nc, I, bank, gate0, gates123, lstm_wh = m.nc, m.I, m.bank, m.gate0, m.gates123, m.lstm_wh

    def sb(name, shape, where=None):
        return m.sb(name, shape, where or stack)

    w = {}
    loads = []

    def load(name, shape, *parts):
        w[name] = sb(name, shape)
        for index, src in parts:
            loads.append((w[name][index], src))

    all2, all3 = np.s_[:, :], np.s_[:, :, :]
    for tag, w1, b1, w2, b2 in (("hid0", "L0_xattn_ffn_w1", "L0_xattn_ffn_b1", "L0_xattn_ffn_w2", "L0_xattn_ffn_b2"),
                                ("hid1", "L1_xattn_w1", "L1_xattn_b1", "L1_xattn_w2", "L1_xattn_b2")):
        load(tag + "_w1", [P, HID], (all2, I[w1]))
        load(tag + "_b1", [P, HC], (all2, I[b1].rearrange("(c p) -> p c", p=P)))
        load(tag + "_w2", [P, HC, C], (all3, I[w2].rearrange("(c p) n -> p c n", p=P)))
        load(tag + "_b2", [P, 1], (all2, I[b2].unsqueeze(1)))
    for tag, name in (("moe0", "L0_ffn"), ("moe1", "L1_ffn")):
        load(tag + "_w1", [P, E, EH], (all3, I[name + "_W1"].rearrange("e c h -> c e h")))
        load(tag + "_b1", [P, E, EC], (all3, I[name + "_b1"].rearrange("e (k p) -> p e k", p=P)))
        load(tag + "_w2", [P, E * EC, C], (all3, I[name + "_W2"].rearrange("e (k p) c -> p (e k) c", p=P)))
        load(tag + "_b2", [PART_ROWS, C], *[(np.s_[32 * k:32 * k + E, :], I[name + "_b2"]) for k in range(PARTS)])
    load("w_red", [P, RED], (all2, I["L0_ffn_w_red"]))
    load("wg", [E, RED], (all2, I["L0_ffn_wg"]))
    load("gate_w", [P, E], (all2, I["L1_ffn_gate_W"]))
    load("fw_q", [P, TW], (all2, I["L1_attn_wq"]))
    load("fw_k", [P, TW], (all2, I["L1_attn_wk"]))
    load("fw_t", [P, TW], (all2, I["L1_attn_wv"]))
    load("fw_o", [P, PAIRS, C], (all3, I["L1_attn_wo"].rearrange("(p r) c -> r p c", r=P)))
    load("fw_theta", [P, PAIRS], (all2, I["L1_attn_theta"].rearrange("(p two) c one -> (two c) (p one)", two=2)))
    load("fw_theta_b", [P, H], (all2, row(I["L1_attn_theta_bias"])))
    load("fw_b", [P, TW], (all2, row(I["L1_attn_b1"])))
    load("fw_g2", [P, TW], (all2, row(I["L1_attn_gamma"])))
    load("fw_gbe", [P, TW], (all2, row(I["L1_attn_beta"])))
    load("fw_g_col", [P, PAIRS], (all2, I["L1_attn_gamma"].rearrange("(p two) one d -> (two d) (p one)", two=2)))
    load("fw_be_col", [P, PAIRS], (all2, I["L1_attn_beta"].rearrange("(p two) one d -> (two d) (p one)", two=2)))
    load("fw_alpha", [P, 1], *[(np.s_[half * TD:half * TD + TD, :], I["L1_attn_alpha"].unsqueeze(1))
                               for half in range(2)])
    for n in (1, 2, 3):
        load(f"ln_g{n}", [P, C], (all2, row(I[f"L1_xattn_g{n}"])))
        load(f"ln_b{n}", [P, C], (all2, row(I[f"L1_xattn_beta{n}"])))
    w["fw_w1"] = m.x_norm[:, :, :].rearrange("q t c -> q (t c)").rearrange("q (p d) -> q p d", p=PAIRS)
    loads.append((w["fw_w1"], I["L1_attn_W1"].rearrange("(p two) c d -> (two c) p d", two=2)))

    with ExitStack() as mem:
        h = sb("lstm_h", [P, BATCH], mem)
        c = sb("lstm_c", [P, BATCH], mem)
        cand = sb("lstm_cand", [P, BATCH], mem)
        sig = sb("lstm_sig", [P, GATES - 1, BATCH], mem)
        kept = sb("lstm_kept", [P, BATCH], mem)
        new = sb("lstm_new", [P, BATCH], mem)
        c_tanh = sb("lstm_c_tanh", [P, BATCH], mem)
        arriving = Signals(nc, mem)
        with ExitStack() as sems:
            S = Signals(nc, sems)
            with nc.Block() as block:
                @block.vector
                def _(dve):
                    for tag in ("moe0", "moe1"):
                        nc.vector.memset(w[tag + "_b2"][:, :], 0.0).then_inc(S["cleared"], 1)
                    nc.vector.memset(h[:, :], 0.0).then_inc(S["cleared"], 1)
                    nc.vector.memset(c[:, :], 0.0).then_inc(S["cleared"], 1)
            finish_phase(nc, S)

        at0 = gate0[:, :].rearrange("c (b s) -> c b s", s=SEQ)
        at123 = gates123.rearrange("c j (b s) -> c j b s", s=SEQ)
        part_bank = lambda part, k: bank(2 * part + k % 2)
        parts = ((0, 1), (1, 2), (3, 1))
        def lstm_steps(S, first, with_loads):
            with nc.Block() as block:
                @block.tensor
                def _(pe):
                    def input_parts(k):
                        step = first + k
                        for part, (n, count) in enumerate(parts):
                            if n == 0:
                                at = at0[:, :, bass.ds(step, 1)].rearrange("c b s -> c (b s)")
                            else:
                                at = at123[:, n - 1:n - 1 + count, :, bass.ds(step, 1)].rearrange(
                                    "c j b s -> c j (b s)")
                            nc.tensor.matmul(part_bank(part, k)[:, 0:count * BATCH], m.ident[:, :], at,
                                             start=True, stop=False, skip_group_check=True)

                    input_parts(0)
                    for k in range(LSTM_UNROLL):
                        if k >= 1:
                            pe.wait_ge(S["h"], k)
                        for part, (n, count) in enumerate(parts):
                            for n1 in range(n, n + count):
                                j = GATE_ORDER[n1]
                                mm = nc.tensor.matmul(
                                    part_bank(part, k)[:, (n1 - n) * BATCH:(n1 - n + 1) * BATCH],
                                    lstm_wh[:, j * C:(j + 1) * C], h[:, :], start=False,
                                    stop=(n1 == n + count - 1), skip_group_check=True)
                            mm.then_inc(S["gates"], 1)
                        if k + 1 < LSTM_UNROLL:
                            if k >= 1:
                                pe.wait_ge(S["sig_out"], k)
                            input_parts(k + 1)

                @block.vector
                def _(dve):
                    for k in range(LSTM_UNROLL):
                        dve.wait_ge(S["sig"], k + 1)
                        nc.vector.tensor_tensor(kept[:, :], sig[:, 1, :], c[:, :], ALU.mult)\
                            .then_inc(S["kept"], 1)
                        dve.wait_ge(S["cand"], k + 1)
                        nc.vector.tensor_tensor(new[:, :], sig[:, 0, :], cand[:, :], ALU.mult)\
                            .then_inc(S["new"], 1)
                        dve.wait_ge(S["kept"], k + 1)
                        dve.wait_ge(S["new"], k + 1)
                        nc.vector.tensor_tensor(c[:, :], kept[:, :], new[:, :], ALU.add).then_inc(S["c"], 1)
                        dve.wait_ge(S["c_tanh"], k + 1)
                        dve.wait_ge(S["sig_out"], k + 1)
                        if k >= 1:
                            dve.wait_ge(S["h_stored"], k)
                        nc.vector.tensor_tensor(h[:, :], sig[:, 2, :], c_tanh[:, :], ALU.mult)\
                            .then_inc(S["h"], 1)

                @block.scalar
                def _(act):
                    nc.scalar.preload_act_table(ACT.Sigmoid)
                    for k in range(LSTM_UNROLL):
                        act.wait_ge(S["gates"], 3 * k + 1)
                        nc.scalar.activation(cand[:, :], part_bank(0, k)[:, 0:BATCH], ACT.Tanh)\
                            .then_inc(S["cand"], 1)
                        act.wait_ge(S["gates"], 3 * k + 2)
                        nc.scalar.activation(sig[:, 0:2, :], part_bank(1, k)[:, 0:2 * BATCH].rearrange(
                            "c (j b) -> c j b", j=2), ACT.Sigmoid).then_inc(S["sig"], 1)
                        act.wait_ge(S["gates"], 3 * k + 3)
                        nc.scalar.activation(sig[:, 2, :], part_bank(2, k)[:, 0:BATCH], ACT.Sigmoid)\
                            .then_inc(S["sig_out"], 1)
                        act.wait_ge(S["c"], k + 1)
                        nc.scalar.activation(c_tanh[:, :], c[:, :], ACT.Tanh).then_inc(S["c_tanh"], 1)

                @block.gpsimd
                def _(pool):
                    for k in range(LSTM_UNROLL):
                        step = first + k
                        pool.wait_ge(S["h"], k + 1)
                        nc.gpsimd.tensor_copy(at0[:, :, bass.ds(step, 1)].rearrange("c b s -> c (b s)"), h[:, :])\
                            .then_inc(S["h_stored"], 1)
                if with_loads:
                    @block.sync
                    def _(sp):
                        for dst, src in loads:
                            sp.dma_start(dst, src).then_inc(arriving["weights_loaded"], 16)
            finish_phase(nc, S)

        with ExitStack() as sems:
            S = Signals(nc, sems)
            lstm_steps(S, 0, True)
            with nc.Fori(1, SEQ // LSTM_UNROLL) as i:
                lstm_steps(S, i * LSTM_UNROLL, False)
        with nc.Block() as block:
            @block.sync
            def _(sp):
                sp.wait_ge(arriving["weights_loaded"], 16 * len(loads))
        finish_phase(nc, arriving)

    for name, shape in (("wg_nT", [RED, E]), ("rank", [P, E]), ("block_mask", [P, P]),
                        ("causal_mask", [P, P]), ("fw_z", [P, TW]), ("fw_zq", [P, TW]), ("fw_go", [P, PAIRS, C]),
                        ("fw_qo", [P, C]), ("fw_beo", [P, C]), ("fw_lr", [P, H]), ("token_eta", [P, 1]),
                        ):
        w[name] = sb(name, shape)
    for name, shape in (("ones", [PART_ROWS, P]), ("ident_bf16", [P, P]), ("cw_parts", [P, GT, PARTS, 32]),
                        ("sel", [PART_ROWS, E, P]), ("fw_b_rows", [PART_ROWS, TW]), ("fw_gbe_rows", [PART_ROWS, TW])):
        w[name] = m.sb(name, shape, stack, BF16)
    return w


def prepare_c(m, w):
    nc, pair, bank, ident = m.nc, m.pair, m.bank, m.ident
    with ExitStack() as mem, ExitStack() as sems:
        S = Signals(nc, sems)

        def sb(name, shape, dtype=F32):
            return m.sb(name, shape, mem, dtype)

        arena = m.arena
        wkT = arena[:, 0:1024].rearrange("r (p c) -> r p c", p=PAIRS)
        wqT = arena[:, 1024:2048].rearrange("r (p c) -> r p c", p=PAIRS)
        be_mat = arena[:, 2048:3072].rearrange("r (p q) -> r p q", p=PAIRS)
        mean = arena[:, 3072:3120].rearrange("q (n h) -> q n h", n=3)
        wg_sq = arena[0:E, 3200:3216]
        wg_v = arena[0:E, 3216:3224]
        rest = arena[:, 4096:4096 + 2 * TW].rearrange("q (n d) -> q n d", n=2)
        part = sb("bf16_part", [P, 2, TW], BF16)
        sel = arena[0:PART_ROWS, 8192:8192 + E * P].rearrange("r (e q) -> r e q", e=E)
        by_bank = lambda ap: ap.rearrange("q (two p d) -> q p two d", two=2, p=PAIRS)
        pos_i = sb("pos_i", [P, 1])
        pos = sb("pos", [P, 1])
        by_head = lambda ap: ap.rearrange("q (h d) -> q h d", h=H)

        with nc.Block() as block:
            @block.tensor
            def _(pe):
                for p in range(PAIRS):
                    tr = nc.tensor.transpose(pair[0][:, p * P:(p + 1) * P], w["fw_k"][:, p * P:(p + 1) * P], ident[:, :])
                tr.then_inc(S["wk_turned"], 1)
                for p in range(PAIRS):
                    tr = nc.tensor.transpose(pair[1][:, p * P:(p + 1) * P], w["fw_q"][:, p * P:(p + 1) * P], ident[:, :])
                tr.then_inc(S["wq_turned"], 1)
                pe.wait_ge(S["wkT"], 1)
                pe.wait_ge(S["wqT"], 1)
                for dst, src, done in ((2, wkT, "wk_w1"), (3, wqT, "wq_w1")):
                    for h in range(H):
                        rows = slice(TD * (h % 2), TD * (h % 2) + TD)
                        mm = nc.tensor.matmul(bank(2 * dst + h % 2)[:, (h // 2) * TD:(h // 2 + 1) * TD], src[rows, h // 2, :],
                                              w["fw_w1"][rows, h // 2, :], start=True, stop=True)
                    mm.then_inc(S[done], 1)
                for h in range(H):
                    rows = slice(TD * (h % 2), TD * (h % 2) + TD)
                    mm = nc.tensor.matmul(bank(h % 2)[:, h // 2:h // 2 + 1], wkT[rows, h // 2, :],
                                          w["fw_theta"][rows, h // 2:h // 2 + 1], start=True, stop=True)
                mm.then_inc(S["wk_theta"], 1)
                for p in range(PAIRS):
                    mm = nc.tensor.matmul(bank(2)[:, 0:C], wqT[:, p, :], w["fw_o"][:, p, :],
                                          start=(p == 0), stop=(p == PAIRS - 1))
                mm.then_inc(S["wq_wo"], 1)
                pe.wait_ge(S["be_mat"], 1)
                for p in range(PAIRS):
                    mm = nc.tensor.matmul(bank(3)[:, 0:C], be_mat[:, p, :], w["fw_o"][:, p, :],
                                          start=(p == 0), stop=(p == PAIRS - 1))
                mm.then_inc(S["be_wo"], 1)
                pe.wait_ge(S["wg_n"], 1)
                pe.wait_ge(S["wk_theta_sb"], 1)
                nc.tensor.transpose(bank(0)[0:RED, 128:128 + E], w["wg"][:, :], ident[0:E, 0:E])\
                    .then_inc(S["wg_turned"], 1)

            @block.scalar
            def _(act):
                act.wait_ge(S["wk_turned"], 1)
                nc.scalar.activation(wkT, pair[0].rearrange("r (p c) -> r p c", p=PAIRS), ACT.Copy)\
                    .then_inc(S["wkT"], 1)
                act.wait_ge(S["wq_turned"], 1)
                nc.scalar.activation(wqT, pair[1].rearrange("r (p c) -> r p c", p=PAIRS), ACT.Copy)\
                    .then_inc(S["wqT"], 1)
                act.wait_ge(S["wg_norm2"], 1)
                nc.scalar.activation(wg_v[:, 1:2], wg_v[:, 0:1], ACT.Ln).then_inc(S["wg_log"], 1)
                act.wait_ge(S["wg_log"], 1)
                nc.scalar.activation(wg_v[:, 2:3], wg_v[:, 1:2], ACT.Exp, scale=0.5).then_inc(S["wg_norm"], 1)
                act.wait_ge(S["wk_theta"], 1)
                nc.scalar.activation(w["fw_lr"][:, :].rearrange("q (p two) -> q two p", two=2),
                                     m.four_banks[:, 0:2, 0:PAIRS], ACT.Copy).then_inc(S["wk_theta_sb"], 1)
                act.wait_ge(S["wq_wo"], 1)
                nc.scalar.activation(w["fw_qo"][:, :], bank(2)[:, 0:C], ACT.Copy)
                act.wait_ge(S["be_wo"], 1)
                nc.scalar.activation(w["fw_beo"][:, :], bank(3)[:, 0:C], ACT.Copy)
                act.wait_ge(S["wg_turned"], 1)
                nc.scalar.activation(w["wg_nT"][:, :], bank(0)[0:RED, 128:128 + E], ACT.Copy)

            @block.vector
            def _(dve):
                nc.vector.tensor_copy(be_mat, bcast(w["fw_be_col"][:, :], 2, P)).then_inc(S["be_mat"], 1)
                nc.vector.memset(w["cw_parts"][:, :, :, :], 0.0)
                for name in ("fw_b_rows", "fw_gbe_rows"):
                    nc.vector.memset(w[name][:, :], 0.0).then_inc(S["rows_cleared"], 1)
                nc.vector.tensor_tensor(wg_sq, w["wg"][:, :], w["wg"][:, :], ALU.mult).then_inc(S["wg_v"], 1)
                dve.wait_ge(S["wg_v"], 1)
                nc.vector.tensor_reduce(wg_v[:, 3:4], wg_sq, AX_X, ALU.add).then_inc(S["wg_v"], 1)
                dve.wait_ge(S["wg_v"], 2)
                nc.vector.tensor_scalar(wg_v[:, 0:1], wg_v[:, 3:4], 1e-18, None, ALU.max).then_inc(S["wg_norm2"], 1)
                dve.wait_ge(S["wg_norm"], 1)
                nc.vector.tensor_scalar(wg_v[:, 4:5], wg_v[:, 2:3], 1e-4, None, ALU.max).then_inc(S["wg_v"], 1)
                dve.wait_ge(S["wg_v"], 3)
                nc.vector.reciprocal(wg_v[:, 5:6], wg_v[:, 4:5]).then_inc(S["wg_v"], 1)
                dve.wait_ge(S["wg_v"], 4)
                nc.vector.tensor_scalar(w["wg"][:, :], w["wg"][:, :], wg_v[:, 5:6], None, ALU.mult)\
                    .then_inc(S["wg_n"], 1)
                nc.vector.tensor_tensor(w["fw_t"][:, :], w["fw_k"][:, :], w["fw_t"][:, :], ALU.subtract)\
                    .then_inc(S["fold"], 1)
                nc.vector.tensor_tensor(w["fw_gbe"][:, :], w["fw_gbe"][:, :], w["fw_g2"][:, :], ALU.mult)\
                    .then_inc(S["gbe"], 1)
                dve.wait_ge(S["fold"], 1)
                nc.vector.tensor_tensor(w["fw_t"][:, :], w["fw_t"][:, :], w["fw_g2"][:, :], ALU.mult)\
                    .then_inc(S["fold"], 1)
                dve.wait_ge(S["fold"], 2)
                nc.vector.tensor_tensor(w["fw_g2"][:, :], w["fw_g2"][:, :], w["fw_g2"][:, :], ALU.mult)
                nc.vector.tensor_tensor(w["fw_go"][:, :, :], w["fw_o"][:, :, :], bcast(w["fw_g_col"][:, :], 2, C), ALU.mult)
                nc.vector.tensor_reduce(mean[:, 0, :], by_head(w["fw_b"][:, :]), AX_X, ALU.add).then_inc(S["mean"], 1)
                dve.wait_ge(S["wk_w1"], 1)
                nc.vector.tensor_reduce(mean[:, 1, :].rearrange("q (p two) -> q p two", two=2), by_bank(pair[2]), AX_X,
                                        ALU.add).then_inc(S["mean"], 1)
                dve.wait_ge(S["wq_w1"], 1)
                nc.vector.tensor_reduce(mean[:, 2, :].rearrange("q (p two) -> q p two", two=2), by_bank(pair[3]), AX_X,
                                        ALU.add).then_inc(S["mean"], 1)
                dve.wait_ge(S["mean"], 3)
                nc.vector.tensor_scalar(mean, mean, 1.0 / TD, None, ALU.mult).then_inc(S["mean"], 1)
                dve.wait_ge(S["mean"], 4)
                nc.vector.tensor_tensor(by_head(w["fw_b"][:, :]), by_head(w["fw_b"][:, :]), bcast(mean[:, 0, :], 2, TD),
                                        ALU.subtract).then_inc(S["b_less"], 1)
                for n, (name, ready) in enumerate((("fw_b", "b_less"), ("fw_gbe", "gbe"))):
                    dve.wait_ge(S["rows_cleared"], 2)
                    dve.wait_ge(S[ready], 1)
                    left = w[name][:, :]
                    for k in range(PARTS):
                        nc.vector.tensor_copy(part[:, n, :], left).then_inc(S[f"{name}_parts"], 1)
                        dve.wait_ge(S[f"{name}_parts"], 2 * k + 1)
                        nc.vector.tensor_copy(w[name + "_rows"][32 * k:32 * k + 1, :], part[32 * k:32 * k + 1, n, :])
                        if k < PARTS - 1:
                            nc.vector.tensor_tensor(rest[:, n, :], left, part[:, n, :], ALU.subtract)\
                                .then_inc(S[f"{name}_parts"], 1)
                            dve.wait_ge(S[f"{name}_parts"], 2 * k + 2)
                            left = rest[:, n, :]
                for n, (dst, src) in enumerate(((w["fw_z"], pair[2]), (w["fw_zq"], pair[3])), start=1):
                    in_pairs = lambda ap: ap.rearrange("q (p two) d -> q p two d", two=2)
                    nc.vector.tensor_tensor(in_pairs(by_head(dst[:, :])), by_bank(src),
                                            in_pairs(bcast(mean[:, n, :], 2, TD)), ALU.subtract)
                dve.wait_ge(S["pos"], 2)
                nc.vector.tensor_copy(pos[:, :], pos_i[:, :].bitcast(mybir.dt.int32)).then_inc(S["pos_v"], 1)
                dve.wait_ge(S["pos_v"], 1)
                nc.vector.reciprocal(pos[:, :], pos[:, :]).then_inc(S["pos_v"], 1)
                dve.wait_ge(S["pos_v"], 2)
                nc.vector.tensor_scalar(w["token_eta"][:, :], pos[:, :], w["fw_alpha"][:, 0:1], 0.0, ALU.add, ALU.max)\
                    .then_inc(S["pos_v"], 1)
                dve.wait_ge(S["pos_v"], 3)
                nc.vector.tensor_scalar(w["token_eta"][:, :], w["token_eta"][:, :], -1.0 / TD, None, ALU.mult)

            @block.gpsimd
            def _(pool):
                for half in range(2):
                    if half == 1:
                        pool.wait_ge(S["pos"], 1)
                    nc.gpsimd.iota(pos_i[half * SEQ:(half + 1) * SEQ, :].bitcast(mybir.dt.int32), pattern=[[0, 1]],
                                   base=1, channel_multiplier=1).then_inc(S["pos"], 1)
                pool.wait_ge(S["pos"], 2)
                nc.gpsimd.memset(w["ones"][:, :], 1.0)
                for e in range(E):
                    nc.gpsimd.memset(w["rank"][:, e:e + 1], float(E - e))
                nc.gpsimd.memset(sel[:, :, :], 0.0).then_inc(S["cleared"], 1)
                nc.gpsimd.memset(w["block_mask"][:, :], NEG).then_inc(S["cleared"], 1)
                pool.wait_ge(S["cleared"], 2)
                for k in range(PARTS):
                    if k >= 1:
                        pool.wait_ge(S["sel_made"], k)
                    nc.gpsimd.affine_select(out=sel[:, :, :], in_=sel[:, :, :], compare_op=ALU.not_equal, fill=1.0,
                                            base=-32 * k, pattern=[[-1, E], [0, P]], channel_multiplier=1)\
                        .then_inc(S["sel_made"], 1)
                pool.wait_ge(S["sel_made"], PARTS)
                nc.gpsimd.tensor_copy(w["sel"][:, :, :], sel[:, :, :])
                nc.gpsimd.tensor_copy(w["ident_bf16"][:, :], ident[:, :])
                for half in range(2):
                    if half == 1:
                        pool.wait_ge(S["cleared"], 3)
                    rows = slice(half * SEQ, (half + 1) * SEQ)
                    nc.gpsimd.memset(w["block_mask"][rows, rows], 0.0).then_inc(S["cleared"], 1)
                pool.wait_ge(S["cleared"], 4)
                nc.gpsimd.affine_select(out=w["causal_mask"][:, :], in_=w["block_mask"][:, :], compare_op=ALU.is_ge,
                                        fill=NEG, base=0, pattern=[[-1, P]], channel_multiplier=1)
        finish_phase(nc, S)


def phase_c(m, w):
    nc, I, tiles, pair, bank, ident, arena = m.nc, m.I, m.tiles, m.pair, m.bank, m.ident, m.arena
    x_all, gate0, x_cur, ctx_cur, x_norm = m.x_all, m.gate0, m.x_cur, m.ctx_cur, m.x_norm
    ln_vector, ln_scalar, transpose_tiles = m.ln_vector, m.ln_scalar, m.transpose_tiles
    x_flat = x_cur[:, :, :].rearrange("q t c -> q (t c)")

    def part(at, n):
        return arena[:, at:at + n]

    hid = part(10240, HC * GN).rearrange("k (c n) -> k c n", c=HC)
    yT = part(2048, GN)
    exp_hid = part(0, 2 * EC * GN).rearrange("k (u c n) -> k u c n", u=2, c=EC)
    cwT = part(2560, GN)[0:PART_ROWS]
    cw_rest = m.sb("cw_rest", [P, 2, GT, E], m.stack_c)
    cw_parts = w["cw_parts"]
    cwT_parts = m.sb("cwT_parts", [PART_ROWS, GN], m.stack_c, BF16)
    moe0_xT = part(4096, GN)
    redT = part(4096 + GN, GN)
    cw = m.sb("choice", [P, 10, GT, E], m.stack_c)
    cw_s = m.sb("choice_small", [P, 10, GT], m.stack_c)
    x_next = ctx_cur
    fw_qT = part(0, PAIRS * GN).rearrange("r (p n) -> r p n", p=PAIRS)
    fw_kT = part(4096, PAIRS * GN).rearrange("r (p n) -> r p n", p=PAIRS)
    z_sq, sqr, unit, grad = (part(8192 + 1024 * n, 1024) for n in range(4))
    done_T = z_sq[:, 0:(GT - 1) * P]
    xT = m.sb("c_xT", [P, GN], m.stack_c)
    h_cur = m.sb("h_cur", [P, GN], m.stack_c)
    SA = m.sb("fw_A", [P, H, SEQ], m.stack_c)
    zq = m.sb("fw_zq_sb", [P, TW], m.stack_c)
    sqq = m.sb("fw_sqq", [P, TW], m.stack_c)
    small = m.sb("fw_small", [P, 12, H], m.stack_c)
    eta = m.sb("fw_eta", [P, GT, H], m.stack_c)
    in_tiles = lambda ap: ap.rearrange("q (t c) -> q t c", t=GT)
    y = in_tiles(part(4096, GN))
    att = in_tiles(part(4608, GN))
    attT = part(5120, GN)
    ctxT = part(5632, GN)
    yT2 = part(6144, GN)
    att_s = part(6656, 4 * GT).rearrange("q (k t) -> q k t", k=4)
    xhid = part(7168, HC * GN).rearrange("k (c n) -> k c n", c=HC)
    x_front = in_tiles(part(9216, GN))
    att_out = in_tiles(part(9728, GN))
    frontT = part(10240, GN)
    result = in_tiles(part(10752, GN))
    by_head = lambda ap: ap.rearrange("q (h d) -> q h d", h=H)

    def lnT_scalar(act, S, tag, dst=None, b=7):
        act.wait_ge(S[f"{tag}_turned"], GT)
        nc.scalar.activation(xT[:, :] if dst is None else dst, bank(b), ACT.Copy).then_inc(S[f"{tag}_T"], 1)

    def hidden_tensor(pe, S, tag, src, chunks, banks):
        for c in chunks:
            if c >= len(banks):
                pe.wait_ge(S[f"{tag}_hid"], c - len(banks) + 1)
            nc.tensor.matmul(bank(banks[c % len(banks)]), w[tag + "_w1"][:, c * P:(c + 1) * P], src,
                             start=True, stop=True).then_inc(S[f"{tag}_pre"], 1)

    def dense_out_tensor(pe, S, tag, out_bank):
        for c in range(HC):
            pe.wait_ge(S[f"{tag}_hid"], c + 1)
            mm = nc.tensor.matmul(bank(out_bank), w[tag + "_w2"][:, c, :], hid_of[tag][:, c, :],
                                  start=(c == 0), stop=(c == HC - 1))
        mm.then_inc(S[f"{tag}_y"], 1)

    def dense_hidden_scalar(act, S, tag, c, banks):
        act.wait_ge(S[f"{tag}_pre"], c + 1)
        nc.scalar.activation(hid_of[tag][:, c, :], bank(banks[c % len(banks)]), ACT.Relu,
                             bias=w[tag + "_b1"][:, c:c + 1]).then_inc(S[f"{tag}_hid"], 1)

    def dense_sum_scalar(act, S, tag, out_bank):
        act.wait_ge(S[f"{tag}_y"], 1)
        nc.scalar.activation(yT_of[tag], bank(out_bank), ACT.Identity, bias=w[tag + "_b2"][:, 0:1])\
            .then_inc(S[f"{tag}_yT"], 1)

    def back_tensor(pe, S, tag, src, b):
        pe.wait_ge(S[f"{tag}_yT"], 1)
        for t in range(GT):
            tr = nc.tensor.transpose(bank(b)[:, t * P:(t + 1) * P], src[:, t * P:(t + 1) * P], ident[:, :])
        tr.then_inc(S[f"{tag}_back"], 1)

    hid_of = {"hid0": hid, "hid1": xhid}
    yT_of = {"hid0": h_cur[:, :], "hid1": yT2}
    experts_xT = {"moe0": moe0_xT, "moe1": xT[:, :]}

    def weights_feature_major(S, tag):
        for t in range(GT):
            mm = nc.tensor.matmul(bank(4)[0:PART_ROWS, t * P:(t + 1) * P], cw_parts[:, t, :, :], w["ident_bf16"][:, :],
                                  start=True, stop=True)
        mm.then_inc(S[f"{tag}_cw_turned"], 1)

    def expert_biases_tensor(pe, S, tag):
        pe.wait_ge(S[f"{tag}_cwT"], 2)
        nc.tensor.matmul(bank(4), w[tag + "_b2"][:, :], cwT, start=True, stop=False)

    def expert_in_tensor(pe, S, tag, e):
        if e >= 2:
            pe.wait_ge(S[f"{tag}_scaled"], EC * (e - 1))
        nc.tensor.matmul(bank(2 + e % 2), w["sel"][:, e, :], cwT_parts[:, :], start=True, stop=True)\
            .then_inc(S[f"{tag}_cw_rows"], 1)
        for c in range(EC):
            i = EC * e + c
            if e >= 1:
                pe.wait_ge(S[f"{tag}_act"], i - 1)
            nc.tensor.matmul(bank(i % 2), w[tag + "_w1"][:, e, c * P:(c + 1) * P], experts_xT[tag],
                             start=True, stop=True).then_inc(S[f"{tag}_pre"], 1)

    def expert_out_tensor(pe, S, tag, e):
        for c in range(EC):
            i = EC * e + c
            pe.wait_ge(S[f"{tag}_scaled"], i + 1)
            nc.tensor.matmul(bank(4), w[tag + "_w2"][:, i, :], exp_hid[:, e % 2, c, :],
                             start=False, stop=(i == E * EC - 1)).then_inc(S[f"{tag}_used"], 1)

    def weights_scalar(act, S, tag):
        act.wait_ge(S[f"{tag}_cw_turned"], 1)
        nc.scalar.activation(cwT_parts[:, :], bank(4)[0:PART_ROWS, :], ACT.Copy).then_inc(S[f"{tag}_cwT"], 1)
        nc.scalar.activation(cwT, bank(4)[0:PART_ROWS, :], ACT.Copy).then_inc(S[f"{tag}_cwT"], 1)

    def expert_scalar(act, S, tag, e, func):
        for c in range(EC):
            i = EC * e + c
            act.wait_ge(S[f"{tag}_pre"], i + 1)
            if e >= 2:
                act.wait_ge(S[f"{tag}_used"], i - 3)
            nc.scalar.activation(exp_hid[:, e % 2, c, :], bank(i % 2), func, bias=w[tag + "_b1"][:, e, c:c + 1])\
                .then_inc(S[f"{tag}_act"], 1)

    def experts_sum_scalar(act, S, tag):
        act.wait_ge(S[f"{tag}_used"], E * EC)
        nc.scalar.activation(yT, bank(4), ACT.Copy).then_inc(S[f"{tag}_yT"], 1)

    def expert_vector(dve, S, tag, e):
        dve.wait_ge(S[f"{tag}_cw_rows"], e + 1)
        for c in range(EC):
            dve.wait_ge(S[f"{tag}_act"], EC * e + c + 1)
            nc.vector.tensor_tensor(exp_hid[:, e % 2, c, :], exp_hid[:, e % 2, c, :], bank(2 + e % 2), ALU.mult)\
                .then_inc(S[f"{tag}_scaled"], 1)

    def split_weights_vector(dve, S, tag):
        left = cw[:, 0]
        for k in range(PARTS):
            nc.vector.tensor_copy(cw_parts[:, :, k, 0:E], left).then_inc(S[f"{tag}_cw"], 1)
            if k < PARTS - 1:
                dve.wait_ge(S[f"{tag}_cw"], k + 1)
                nc.vector.tensor_tensor(cw_rest[:, k], left, cw_parts[:, :, k, 0:E], ALU.subtract)\
                    .then_inc(S[f"{tag}_cw_rest"], 1)
                dve.wait_ge(S[f"{tag}_cw_rest"], k + 1)
                left = cw_rest[:, k]

    def first_of_max(dve, S, tag, values, top, tmp, key, hot, n0):
        nc.vector.tensor_reduce(top, values, AX_X, ALU.max).then_inc(S[f"{tag}_sel"], 1)
        dve.wait_ge(S[f"{tag}_sel"], n0 + 1)
        nc.vector.tensor_tensor(tmp, values, bcast(top, 2, E), ALU.is_equal).then_inc(S[f"{tag}_sel"], 1)
        dve.wait_ge(S[f"{tag}_sel"], n0 + 2)
        nc.vector.tensor_tensor(tmp, tmp, bcast(w["rank"][:, :], 1, GT), ALU.mult).then_inc(S[f"{tag}_sel"], 1)
        dve.wait_ge(S[f"{tag}_sel"], n0 + 3)
        nc.vector.tensor_reduce(key, tmp, AX_X, ALU.max).then_inc(S[f"{tag}_sel"], 1)
        dve.wait_ge(S[f"{tag}_sel"], n0 + 4)
        nc.vector.tensor_tensor(hot, tmp, bcast(key, 2, E), ALU.is_equal).then_inc(S[f"{tag}_sel"], 1)
        dve.wait_ge(S[f"{tag}_sel"], n0 + 5)

    def two_choices_vector(dve, S):
        gate_exps_vector(dve, S, "moe1", 6)
        nc.vector.scalar_tensor_tensor(out=cw[:, 6], in0=cw[:, 3], scalar=NEG, in1=cw[:, 1],
                                       op0=ALU.mult, op1=ALU.add).then_inc(S["without_first"], 1)
        dve.wait_ge(S["without_first"], 1)
        first_of_max(dve, S, "moe1", cw[:, 6], cw_s[:, 4], cw[:, 2], cw_s[:, 5], cw[:, 7], 5)
        nc.vector.tensor_tensor(cw[:, 8], cw[:, 3], cw[:, 7], ALU.add).then_inc(S["choose"], 1)
        dve.wait_ge(S["choose"], 1)
        nc.vector.tensor_tensor(cw[:, 8], cw[:, 8], cw[:, 5], ALU.mult).then_inc(S["choose"], 1)
        dve.wait_ge(S["choose"], 2)
        nc.vector.tensor_tensor(cw[:, 8], cw[:, 8], bcast(cw_s[:, 3], 2, E), ALU.mult)\
            .then_inc(S["choose"], 1)
        dve.wait_ge(S["choose"], 3)
        nc.vector.tensor_reduce(cw_s[:, 6], cw[:, 8], AX_X, ALU.add).then_inc(S["choose"], 1)
        dve.wait_ge(S["choose"], 4)
        nc.vector.tensor_scalar(cw_s[:, 7], cw_s[:, 6], 1e-8, None, ALU.add).then_inc(S["choose"], 1)
        dve.wait_ge(S["choose"], 5)
        nc.vector.reciprocal(cw_s[:, 8], cw_s[:, 7]).then_inc(S["choose"], 1)
        dve.wait_ge(S["choose"], 6)
        nc.vector.tensor_tensor(cw[:, 0], cw[:, 8], bcast(cw_s[:, 8], 2, E), ALU.mult)\
            .then_inc(S["moe1_choice"], 1)
        dve.wait_ge(S["moe1_choice"], 1)
        split_weights_vector(dve, S, "moe1")

    def gate_exps_vector(dve, S, tag, b):
        dve.wait_ge(S[f"{tag}_logits"], 1)
        nc.vector.tensor_copy(cw[:, 1], bank(b)[:, 0:GT * E].rearrange("q (t e) -> q t e", t=GT))\
            .then_inc(S[f"{tag}_logits_sb"], 1)
        dve.wait_ge(S[f"{tag}_logits_sb"], 1)
        first_of_max(dve, S, tag, cw[:, 1], cw_s[:, 0], cw[:, 2], cw_s[:, 1], cw[:, 3], 0)
        nc.vector.tensor_tensor(cw[:, 4], cw[:, 1], bcast(cw_s[:, 0], 2, E), ALU.subtract)\
            .then_inc(S[f"{tag}_less_max"], 1)
        dve.wait_ge(S[f"{tag}_exp"], 1)
        nc.vector.tensor_reduce(cw_s[:, 2], cw[:, 5], AX_X, ALU.add).then_inc(S[f"{tag}_gate"], 1)
        dve.wait_ge(S[f"{tag}_gate"], 1)
        nc.vector.reciprocal(cw_s[:, 3], cw_s[:, 2]).then_inc(S[f"{tag}_gate"], 1)
        dve.wait_ge(S[f"{tag}_gate"], 2)

    def gate_exps_scalar(act, S, tag):
        act.wait_ge(S[f"{tag}_less_max"], 1)
        nc.scalar.activation(cw[:, 5], cw[:, 4], ACT.Exp).then_inc(S[f"{tag}_exp"], 1)

    def turn_choice_tensor(pe, S, tag):
        transpose_tiles(pe, S, "ln_unit", lambda t: GT * LN_TURN[tag] + t + 1, x_norm, bank(3), f"{tag}_turned")

    def reduce_tensor(pe, S, tag):
        pe.wait_ge(S[f"{tag}_T"], 1)
        nc.tensor.matmul(bank(0)[0:RED, :], w["w_red"][:, :], moe0_xT, start=True, stop=True).then_inc(S["red"], 1)

    def logits_tensor(pe, S):
        pe.wait_ge(S["redT"], 1)
        for t in range(GT):
            mm = nc.tensor.matmul(bank(6)[:, t * E:(t + 1) * E], redT[0:RED, t * P:(t + 1) * P], w["wg_nT"][:, :],
                                  start=True, stop=True)
        mm.then_inc(S["moe0_logits"], 1)

    def reduced_scalar(act, S):
        act.wait_ge(S["red"], 1)
        nc.scalar.activation(redT[0:RED, :], bank(0)[0:RED, :], ACT.Copy).then_inc(S["redT"], 1)

    def stream_vector(dve, S, tag):
        dve.wait_ge(S["x_next"], 1)
        dve.wait_ge(S["hid0_back"], 1)
        nc.vector.tensor_tensor(x_next[:, :, :], x_next[:, :, :], in_tiles(bank(0)), ALU.add).then_inc(S["dense_added"], 1)
        dve.wait_ge(S["dense_added"], 1)
        ln_vector(dve, S, tag, x_next, x_norm)

    def choice_vector(dve, S):
        gate_exps_vector(dve, S, "moe0", 6)
        nc.vector.tensor_tensor(cw[:, 0], cw[:, 3], bcast(cw_s[:, 3], 2, E), ALU.mult).then_inc(S["moe0_choice"], 1)
        dve.wait_ge(S["moe0_choice"], 1)
        split_weights_vector(dve, S, "moe0")

    def attend_scores_tensor(S, tag, kT, b):
        for t in range(GT):
            mm = nc.tensor.matmul(bank(b)[:, t * P:(t + 1) * P], frontT[:, t * P:(t + 1) * P], kT[:, t * P:(t + 1) * P],
                                  start=True, stop=True)
        mm.then_inc(S[f"{tag}_score"], 1)

    def attend_turn_tensor(pe, S, tag, b):
        pe.wait_ge(S[f"{tag}_prob"], 1)
        for t in range(GT):
            tr = nc.tensor.transpose(bank(b)[:, t * P:(t + 1) * P], att[:, t, :], ident[:, :])
        tr.then_inc(S[f"{tag}_turned"], 1)

    def attend_values_tensor(pe, S, tag, values, b):
        pe.wait_ge(S[f"{tag}_probT"], 1)
        for t in range(GT):
            mm = nc.tensor.matmul(bank(b)[:, t * P:(t + 1) * P], attT[:, t * P:(t + 1) * P], values[:, t, :],
                                  start=True, stop=True)
        mm.then_inc(S[f"{tag}_pv"], 1)

    def attend_exp_scalar(act, S, tag):
        act.wait_ge(S[f"{tag}_less_max"], 1)
        nc.scalar.activation(att, att, ACT.Exp).then_inc(S[f"{tag}_prob"], 1)

    def attend_turned_scalar(act, S, tag, b):
        act.wait_ge(S[f"{tag}_turned"], 1)
        nc.scalar.activation(attT, bank(b), ACT.Copy).then_inc(S[f"{tag}_probT"], 1)

    def attend_shift_vector(dve, S, tag, mask, b):
        dve.wait_ge(S[f"{tag}_score"], 1)
        nc.vector.scalar_tensor_tensor(out=att, in0=in_tiles(bank(b)), scalar=INV_SQRT_C,
                                       in1=bcast(w[mask][:, :], 1, GT), op0=ALU.mult, op1=ALU.add)\
            .then_inc(S[f"{tag}_masked"], 1)
        dve.wait_ge(S[f"{tag}_masked"], 1)
        nc.vector.tensor_reduce(att_s[:, 0], att, AX_X, ALU.max).then_inc(S[f"{tag}_max"], 1)
        dve.wait_ge(S[f"{tag}_max"], 1)
        nc.vector.tensor_tensor(att, att, bcast(att_s[:, 0], 2, P), ALU.subtract).then_inc(S[f"{tag}_less_max"], 1)

    def attend_sum_vector(dve, S, tag):
        dve.wait_ge(S[f"{tag}_prob"], 1)
        nc.vector.tensor_reduce(att_s[:, 1], att, AX_X, ALU.add).then_inc(S[f"{tag}_sum"], 1)
        dve.wait_ge(S[f"{tag}_sum"], 1)
        nc.vector.reciprocal(att_s[:, 2], att_s[:, 1]).then_inc(S[f"{tag}_rec"], 1)

    def attend_out_vector(dve, S, tag, b):
        dve.wait_ge(S[f"{tag}_rec"], 1)
        dve.wait_ge(S[f"{tag}_pv"], 1)
        nc.vector.tensor_tensor(att_out, in_tiles(bank(b)), bcast(att_s[:, 2], 2, C), ALU.mult)\
            .then_inc(S[f"{tag}_out"], 1)
        dve.wait_ge(S[f"{tag}_out"], 1)
        nc.vector.tensor_tensor(y, y, att_out, ALU.add).then_inc(S[f"{tag}_added"], 1)
        dve.wait_ge(S[f"{tag}_added"], 1)

    def fast_tensor(pe, S, beside):
        pe.wait_ge(S["ln4_T"], 1)
        for t in range(GT):
            mm = nc.tensor.matmul(bank(7)[:, t * H:(t + 1) * H], xT[:, t * P:(t + 1) * P], w["fw_lr"][:, :],
                                  start=True, stop=True)
        mm.then_inc(S["fw_lr"], 1)

        def head_pairs():
            for j in range(2 * PAIRS):
                p, side = divmod(j, 2)
                if j == 2 and beside:
                    pe.wait_ge(S["hid0_yT"], 1)
                if j == 3:
                    pe.wait_ge(S["fw_lr_in"], 1)
                if j >= 4:
                    pe.wait_ge(S["fw_heads_act" if side == 0 else "fw_heads_dve"], j // 2 - 1)
                nc.tensor.matmul(bank(4 + j % 4), w["fw_q" if side == 0 else "fw_k"][:, p * P:(p + 1) * P], xT[:, :],
                                 start=True, stop=True).then_inc(S["fw_heads"], 1)
            pe.wait_ge(S["fw_heads_act"], PAIRS)
            pe.wait_ge(S["fw_heads_dve"], PAIRS)

        def with_row(dst, x_tile, weights, rows, last):
            for half in range(2):
                cols = slice(half * 512, half * 512 + 512)
                nc.tensor.matmul(dst[:, cols], x_tile, weights[:, cols], start=True, stop=False, skip_group_check=True)
                mm = nc.tensor.matmul(dst[:, cols], w["ones"][:, :], rows[:, cols], start=False, stop=last,
                                      skip_group_check=True)
            return mm

        for t in range(-1, GT + 1):
            new, old = t + 1, t - 1
            if new < GT:
                x_tile = xT[:, new * P:(new + 1) * P]
                if new >= 1:
                    pe.wait_ge(S["fw_unit"], new)
                with_row(pair[0], x_tile, w["fw_z"], w["fw_b_rows"], True).then_inc(S["fw_z"], 1)
                if new >= 1:
                    pe.wait_ge(S["fw_gxh"], new)
                with_row(pair[1], x_tile, w["fw_t"], w["fw_gbe_rows"], True).then_inc(S["fw_t"], 1)
            if old >= 0:
                pe.wait_ge(S["fw_unit2"], old + 1)
                pe.wait_ge(S["fw_A"], min(t + 1, GT))
                for p in range(PAIRS):
                    tr = nc.tensor.transpose(pair[2][:, p * P:(p + 1) * P], zq[:, p * P:(p + 1) * P], ident[:, :])
                tr.then_inc(S["fw_turned"], 1)
            if t == GT and beside:
                turn_choice_tensor(pe, S, "ln3")
            if t == -1:
                head_pairs()
            if 0 <= t < GT:
                with_row(pair[3], xT[:, t * P:(t + 1) * P], w["fw_zq"], w["fw_b_rows"], False)
            if t == GT:
                pe.wait_ge(S["fw_yT"], 1)
                pe.wait_ge(S["fw_unit"], GT)
                for n in range(GT - 1):
                    tr = nc.tensor.transpose(bank(1)[:, n * P:(n + 1) * P], done_T[:, n * P:(n + 1) * P], ident[:, :])
                tr.then_inc(S["fw_back"], 1)
                if beside:
                    reduce_tensor(pe, S, "ln3")
                    logits_tensor(pe, S)
                pe.wait_ge(S["fw_turned_act"], GT)
                last = slice(old * P, GT * P)
                nc.tensor.matmul(bank(4)[:, 0:C], xT[:, last], w["fw_qo"][:, :], start=True, stop=False)
                for p in range(PAIRS):
                    mm = nc.tensor.matmul(bank(4)[:, 0:C], fw_qT[:, p, last], w["fw_go"][:, p, :], start=False,
                                          stop=(p == PAIRS - 1))
                mm.then_inc(S["fw_y"], 1)
            if 0 <= t < GT:
                pe.wait_ge(S["fw_A"], t + 1)
                pe.wait_ge(S["fw_step"], t + 1)
                for b in range(2):
                    rows = slice(b * SEQ, (b + 1) * SEQ)
                    for h in range(H):
                        mm = nc.tensor.matmul(pair[3][rows, h * TD:(h + 1) * TD], SA[rows, h, :],
                                              grad[rows, h * TD:(h + 1) * TD], start=False,
                                              stop=(b == 1 and h in (H // 2 - 1, H - 1)), skip_group_check=True)
                mm.then_inc(S["fw_zq"], 1)
            if t == GT - 1:
                pe.wait_ge(S["fw_unit"], GT)
                if beside:
                    back_tensor(pe, S, "hid0", h_cur, 0)
                pe.wait_ge(S["fw_gxh"], GT)
                pe.wait_ge(S["fw_turned_act"], t)
                done = slice(0, t * P)
                nc.tensor.matmul(bank(2)[:, done], w["fw_qo"][:, :], xT[:, done], start=True, stop=False)
                for p in range(PAIRS):
                    mm = nc.tensor.matmul(bank(2)[:, done], w["fw_go"][:, p, :], fw_qT[:, p, done], start=False,
                                          stop=(p == PAIRS - 1))
                mm.then_inc(S["fw_y_before"], 1)
            if new < GT:
                if old >= 0:
                    pe.wait_ge(S["fw_turned_act"], old + 1)
                elif new >= 1:
                    pe.wait_ge(S["fw_A"], new)
                for b in range(2):
                    for h in range(H):
                        rows, cols = slice(TD * (h % 2), TD * (h % 2) + TD), slice((2 * new + b) * SEQ, (2 * new + b + 1) * SEQ)
                        mm = nc.tensor.matmul(bank(4 + h % 2)[b * SEQ:(b + 1) * SEQ, (h // 2) * SEQ:(h // 2 + 1) * SEQ],
                                              fw_kT[rows, h // 2, cols], fw_qT[rows, h // 2, cols],
                                              start=True, stop=True)
                mm.then_inc(S["fw_kq"], 1)

    def fast_scalar(act, S, beside):
        def rstd(src, log, dst, ready, count, tag):
            act.wait_ge(S[ready], count)
            nc.scalar.activation(log, src, ACT.Ln, bias=m.eps6[:, 0:1], scale=1.0 / TD).then_inc(S[f"{tag}_log"], 1)
            act.wait_ge(S[f"{tag}_log"], count)
            nc.scalar.activation(dst, log, ACT.Exp, scale=-0.5).then_inc(S[f"{tag}_rstd"], 1)

        for t in range(-1, GT + 1):
            new, old = t + 1, t - 1
            if old >= 0:
                act.wait_ge(S["fw_zq"], old + 1)
                if old >= 1:
                    act.wait_ge(S["fw_var2"], old)
                nc.scalar.activation(sqq[:, :], pair[3][:, :], ACT.Square).then_inc(S["fw_sqq"], 1)
            if 0 <= t < GT:
                act.wait_ge(S["fw_kq"], t + 1)
                if t >= 1:
                    act.wait_ge(S["fw_zq"], t)
                nc.scalar.activation(SA[:, :, :].rearrange("k (p two) q -> k two p q", two=2),
                                     pair[2].rearrange("k (two p q) -> k two p q", two=2, p=PAIRS), ACT.Identity,
                                     bias=m.one[:, 0:1]).then_inc(S["fw_A"], 1)
            if old >= 0:
                rstd(small[:, 3, :], small[:, 4, :], small[:, 5, :], "fw_var2", old + 1, "fw2")
            if t == GT and beside:
                ln_scalar(act, S, "ln3")
            if new < GT:
                act.wait_ge(S["fw_z"], new + 1)
                if new >= 1:
                    act.wait_ge(S["fw_var"], new)
                nc.scalar.activation(z_sq, pair[0][:, :], ACT.Square).then_inc(S["fw_sqr"], 1)
            if t == -1:
                act.wait_ge(S["fw_lr_in"], 1)
                nc.scalar.activation(eta[:, :, :], eta[:, :, :], ACT.Exp, scale=-1.0).then_inc(S["fw_lr_e"], 1)
            if old >= 0:
                if t == GT:
                    act.wait_ge(S["fw_y_before"], 1)
                    act.wait_ge(S["fw_var"], GT)
                    nc.scalar.activation(done_T, bank(2)[:, 0:old * P], ACT.Copy).then_inc(S["fw_yT"], 1)
                    if beside:
                        lnT_scalar(act, S, "ln3", moe0_xT, 3)
                act.wait_ge(S["fw_turned"], old + 1)
                nc.scalar.activation(fw_qT[:, :, old * P:(old + 1) * P], pair[2].rearrange("r (p q) -> r p q", p=PAIRS),
                                     ACT.Copy).then_inc(S["fw_turned_act"], 1)
                if t == GT and beside:
                    reduced_scalar(act, S)
                    gate_exps_scalar(act, S, "moe0")
            if new < GT:
                rstd(small[:, 0, :], small[:, 1, :], small[:, 2, :], "fw_var", new + 1, "fw1")
            if t == -1:
                for p in range(PAIRS):
                    act.wait_ge(S["fw_heads"], 2 * p + 1)
                    nc.scalar.activation(fw_qT[:, p, :], bank(4 + (2 * p) % 4), ACT.Copy).then_inc(S["fw_heads_act"], 1)

    def fast_vector(dve, S, beside):
        def keys(*pairs):
            for p in pairs:
                dve.wait_ge(S["fw_heads"], 2 * p + 2)
                nc.vector.tensor_copy(fw_kT[:, p, :], bank(4 + (2 * p + 1) % 4)).then_inc(S["fw_heads_dve"], 1)

        dve.wait_ge(S["fw_lr"], 1)
        nc.vector.tensor_tensor(eta[:, :, :], bank(7)[:, 0:GT * H].rearrange("q (t h) -> q t h", t=GT),
                                bcast(w["fw_theta_b"][:, :], 1, GT), ALU.add).then_inc(S["fw_lr_in"], 1)
        dve.wait_ge(S["fw_lr_e"], 1)
        nc.vector.tensor_scalar(eta[:, :, :], eta[:, :, :], 1.0, None, ALU.add).then_inc(S["fw_eta"], 1)
        dve.wait_ge(S["fw_eta"], 1)
        nc.vector.reciprocal(eta[:, :, :], eta[:, :, :]).then_inc(S["fw_eta"], 1)
        dve.wait_ge(S["fw_eta"], 2)
        nc.vector.tensor_scalar(eta[:, :, :], eta[:, :, :], w["token_eta"][:, 0:1], None, ALU.mult)\
            .then_inc(S["fw_eta"], 1)
        dve.wait_ge(S["fw_eta"], 3)
        for t in range(-1, GT + 1):
            new, old = t + 1, t - 1
            if 0 <= t < GT:
                dve.wait_ge(S["fw_t"], t + 1)
                dve.wait_ge(S["fw_gx"], t + 1)
                if t >= 1:
                    dve.wait_ge(S["fw_zq"], t)
                nc.vector.tensor_tensor(grad, sqr, pair[1][:, :], ALU.add).then_inc(S["fw_gxh"], 1)
                if t == 0:
                    keys(2)
            if old >= 0:
                dve.wait_ge(S["fw_sqq"], old + 1)
                nc.vector.tensor_reduce(small[:, 3, :], by_head(sqq[:, :]), AX_X, ALU.add).then_inc(S["fw_var2"], 1)
            if 0 <= t < GT:
                dve.wait_ge(S["fw_gxh"], t + 1)
                nc.vector.tensor_reduce(small[:, 6, :], by_head(grad), AX_X, ALU.add).then_inc(S["fw_s1"], 1)
                if t == 0:
                    keys(3)
            if old >= 0:
                dve.wait_ge(S["fw2_rstd"], old + 1)
                if old >= 1:
                    dve.wait_ge(S["fw_turned"], old)
                nc.vector.tensor_tensor(by_head(zq[:, :]), by_head(pair[3]), bcast(small[:, 5, :], 2, TD), ALU.mult)\
                    .then_inc(S["fw_unit2"], 1)
            if t == GT and beside:
                stream_vector(dve, S, "ln3")
            if 0 <= t < GT:
                dve.wait_ge(S["fw_p"], t + 1)
                nc.vector.tensor_reduce(small[:, 7, :], by_head(sqr), AX_X, ALU.add).then_inc(S["fw_s2"], 1)
                nc.vector.tensor_tensor(small[:, 8, :], eta[:, t, :], small[:, 2, :], ALU.mult).then_inc(S["fw_coef"], 1)
                dve.wait_ge(S["fw_s1"], t + 1)
                dve.wait_ge(S["fw_s2"], t + 1)
                nc.vector.tensor_scalar(small[:, 6:8, :], small[:, 6:8, :], 1.0 / TD, None, ALU.mult)\
                    .then_inc(S["fw_means"], 1)
                if t == 0:
                    keys(4)
                dve.wait_ge(S["fw_means"], t + 1)
                nc.vector.tensor_tensor(by_head(grad), by_head(grad), bcast(small[:, 6, :], 2, TD), ALU.subtract)\
                    .then_inc(S["fw_less"], 1)
                if t == 0:
                    keys(5)
                dve.wait_ge(S["fw_less"], 2 * t + 1)
                dve.wait_ge(S["fw_u"], t + 1)
                nc.vector.tensor_tensor(grad, grad, sqr, ALU.subtract).then_inc(S["fw_less"], 1)
                if t == 0:
                    keys(6)
                dve.wait_ge(S["fw_less"], 2 * t + 2)
                dve.wait_ge(S["fw_coef"], t + 1)
                nc.vector.tensor_tensor(by_head(grad), by_head(grad), bcast(small[:, 8, :], 2, TD), ALU.mult)\
                    .then_inc(S["fw_step"], 1)
                if t == 0:
                    keys(7)
            if new < GT:
                dve.wait_ge(S["fw_sqr"], new + 1)
                nc.vector.tensor_reduce(small[:, 0, :], by_head(z_sq), AX_X, ALU.add).then_inc(S["fw_var"], 1)
            if new < GT:
                dve.wait_ge(S["fw1_rstd"], new + 1)
                nc.vector.tensor_tensor(by_head(unit), by_head(pair[0]), bcast(small[:, 2, :], 2, TD), ALU.mult)\
                    .then_inc(S["fw_unit"], 1)
            if t == -1:
                keys(0, 1)
        dve.wait_ge(S["fw_back"], 1)
        before = slice(0, GT - 1)
        nc.vector.tensor_tensor(x_cur[:, before, :], x_cur[:, before, :],
                                bank(1)[:, 0:(GT - 1) * P].rearrange("q (t c) -> q t c", c=C), ALU.add)\
            .then_inc(S["fw_x"], 1)
        if beside:
            choice_vector(dve, S)
        dve.wait_ge(S["fw_y"], 1)
        nc.vector.tensor_tensor(x_cur[:, GT - 1, :], x_cur[:, GT - 1, :], bank(4)[:, 0:C], ALU.add)\
            .then_inc(S["fw_x"], 1)
        dve.wait_ge(S["fw_x"], 2)
        nc.vector.tensor_tensor(x_cur[:, :, :], x_cur[:, :, :], bcast(w["fw_beo"][:, :], 1, GT), ALU.add)\
            .then_inc(S["fw_added"], 1)
        dve.wait_ge(S["fw_added"], 1)

    def fast_gpsimd(pool, S):
        for t in range(GT):
            pool.wait_ge(S["fw_unit"], t + 1)
            if t >= 1:
                pool.wait_ge(S["fw_less"], 2 * t)
            nc.gpsimd.tensor_tensor(sqr, unit, w["fw_g2"][:, :], ALU.mult).then_inc(S["fw_gx"], 1)
            pool.wait_ge(S["fw_gxh"], t + 1)
            nc.gpsimd.tensor_tensor(sqr, grad, unit, ALU.mult).then_inc(S["fw_p"], 1)
            pool.wait_ge(S["fw_means"], t + 1)
            nc.gpsimd.tensor_tensor(by_head(sqr), by_head(unit), bcast(small[:, 7, :], 2, TD), ALU.mult)\
                .then_inc(S["fw_u"], 1)

    def middle_stage(S, group, following):
        with nc.Block() as block:
            @block.tensor
            def _(pe):
                weights_feature_major(S, "moe0")
                expert_biases_tensor(pe, S, "moe0")
                for e in range(E + 1):
                    if e < E:
                        expert_in_tensor(pe, S, "moe0", e)
                    if e >= 1:
                        expert_out_tensor(pe, S, "moe0", e - 1)
                back_tensor(pe, S, "moe0", yT, 5)
                if following is not None:
                    pe.wait_ge(S["h_cur"], 1)
                    hidden_tensor(pe, S, "hid0", h_cur[:, :], range(HC), (0, 1))
                transpose_tiles(pe, S, "ln_unit", lambda t: GT * LN_TURN["ln4"] + t + 1, x_norm, bank(7), "ln4_turned")
                if following is not None:
                    dense_out_tensor(pe, S, "hid0", 6)
                fast_tensor(pe, S, following is not None)

            @block.scalar
            def _(act):
                weights_scalar(act, S, "moe0")
                for e in range(E):
                    expert_scalar(act, S, "moe0", e, ACT.Gelu)
                experts_sum_scalar(act, S, "moe0")
                nc.scalar.preload_act_table_set(LN_AND_EXP)
                if following is not None:
                    for c in range(2):
                        dense_hidden_scalar(act, S, "hid0", c, (0, 1))
                ln_scalar(act, S, "ln4")
                if following is not None:
                    for c in range(2, HC):
                        dense_hidden_scalar(act, S, "hid0", c, (0, 1))
                lnT_scalar(act, S, "ln4")
                if following is not None:
                    dense_sum_scalar(act, S, "hid0", 6)
                fast_scalar(act, S, following is not None)

            @block.vector
            def _(dve):
                nc.vector.tensor_copy(x_cur[:, :, :], x_next[:, :, :]).then_inc(S["x_cur"], 1)
                for e in range(E):
                    expert_vector(dve, S, "moe0", e)
                dve.wait_ge(S["x_cur"], 1)
                dve.wait_ge(S["moe0_back"], 1)
                nc.vector.tensor_tensor(x_flat, x_flat, bank(5), ALU.add).then_inc(S["moe0_added"], 1)
                dve.wait_ge(S["moe0_added"], 1)
                ln_vector(dve, S, "ln4", x_cur, x_norm)
                fast_vector(dve, S, following is not None)
                nc.vector.tensor_copy(x_all[:, bass.ds(group * GT, GT), :], x_cur[:, :, :])

            @block.gpsimd
            def _(pool):
                if following is not None:
                    nc.gpsimd.tensor_copy(h_cur[:, :], gate0[:, bass.ds(following * GN, GN)]).then_inc(S["h_cur"], 1)
                    pool.wait_ge(S["x_cur"], 1)
                    nc.gpsimd.tensor_copy(x_next[:, :, :], x_all[:, bass.ds(following * GT, GT), :])\
                        .then_inc(S["x_next"], 1)
                fast_gpsimd(pool, S)
        finish_phase(nc, S)

    with ExitStack() as sems:
        S = Signals(nc, sems)
        with nc.Block() as block:
            @block.tensor
            def _(pe):
                pe.wait_ge(S["h_cur"], 1)
                hidden_tensor(pe, S, "hid0", h_cur[:, :], range(HC), (1, 2, 3, 4))
                dense_out_tensor(pe, S, "hid0", 5)
                back_tensor(pe, S, "hid0", h_cur, 0)
                turn_choice_tensor(pe, S, "ln3_first")
                reduce_tensor(pe, S, "ln3_first")
                logits_tensor(pe, S)

            @block.scalar
            def _(act):
                nc.scalar.preload_act_table_set(LN_AND_EXP)
                for c in range(HC):
                    dense_hidden_scalar(act, S, "hid0", c, (1, 2, 3, 4))
                dense_sum_scalar(act, S, "hid0", 5)
                ln_scalar(act, S, "ln3_first")
                lnT_scalar(act, S, "ln3_first", moe0_xT, 3)
                reduced_scalar(act, S)
                gate_exps_scalar(act, S, "moe0")

            @block.vector
            def _(dve):
                nc.vector.tensor_copy(x_next[:, :, :], x_all[:, 0:GT, :]).then_inc(S["x_next"], 1)
                stream_vector(dve, S, "ln3_first")
                choice_vector(dve, S)

            @block.gpsimd
            def _(pool):
                nc.gpsimd.tensor_copy(h_cur[:, :], gate0[:, 0:GN]).then_inc(S["h_cur"], 1)
        finish_phase(nc, S)
        with nc.Fori(0, GROUPS - 1) as g:
            middle_stage(S, g, g + 1)
        middle_stage(S, GROUPS - 1, None)

    def second_stage(S, front, back):
        with nc.Block() as block:
            @block.sync
            def _(sp):
                if front is not None:
                    sp.dma_start(ctx_cur[:, :, :], tiles(I["ctx_1024"])[:, bass.ds(front * GT, GT), :])\
                        .then_inc(S["ctx_loaded"], 16)
                if back is not None:
                    sp.wait_ge(S["result"], 1)
                    sp.dma_start(tiles(m.out)[:, bass.ds(back * GT, GT), :], result).then_inc(S["stored"], 16)
                    sp.wait_ge(S["stored"], 16)
                if front is not None:
                    sp.wait_ge(S["ctx_loaded"], 16)

            @block.tensor
            def _(pe):
                def expert_in(e):
                    if back is not None:
                        expert_in_tensor(pe, S, "moe1", e)

                def expert_out(e):
                    if back is not None:
                        expert_out_tensor(pe, S, "moe1", e)

                ahead = front is not None
                if back is not None:
                    weights_feature_major(S, "moe1")
                if ahead:
                    transpose_tiles(pe, S, "ln_unit", lambda t: GT * LN_TURN["ln5"] + t + 1, y, bank(7), "ln5_turned")
                    pe.wait_ge(S["ctx_loaded"], 16)
                    for t in range(GT):
                        tr = nc.tensor.transpose(bank(6)[:, t * P:(t + 1) * P], ctx_cur[:, t, :], ident[:, :])
                    tr.then_inc(S["ctx_turned"], 1)
                if back is not None:
                    expert_biases_tensor(pe, S, "moe1")
                expert_in(0)
                if ahead:
                    pe.wait_ge(S["ln5_T"], 1)
                    attend_scores_tensor(S, "self", frontT, 5)
                expert_in(1)
                expert_out(0)
                if ahead:
                    pe.wait_ge(S["ctx_T"], 1)
                    attend_turn_tensor(pe, S, "self", 6)
                expert_in(2)
                if ahead:
                    attend_values_tensor(pe, S, "self", y, 7)
                expert_out(1)
                expert_in(3)
                expert_out(2)
                if ahead:
                    transpose_tiles(pe, S, "g1_done", lambda t: 1, y, bank(5), "g1_turned")
                expert_in(4)
                if ahead:
                    pe.wait_ge(S["g1_T"], 1)
                    attend_scores_tensor(S, "cross", ctxT, 6)
                expert_out(3)
                expert_in(5)
                if ahead:
                    attend_turn_tensor(pe, S, "cross", 7)
                expert_out(4)
                if ahead:
                    attend_values_tensor(pe, S, "cross", ctx_cur, 5)
                expert_in(6)
                expert_out(5)
                expert_in(7)
                if ahead:
                    transpose_tiles(pe, S, "g2_done", lambda t: 1, y, bank(6), "g2_turned")
                expert_out(6)
                if ahead:
                    pe.wait_ge(S["g2_T"], 1)
                    hidden_tensor(pe, S, "hid1", frontT, range(HC), (5, 7))
                    dense_out_tensor(pe, S, "hid1", 6)
                if ahead:
                    back_tensor(pe, S, "hid1", yT2, 7)
                expert_out(7)
                if back is not None:
                    back_tensor(pe, S, "moe1", yT, 2)
                if ahead:
                    transpose_tiles(pe, S, "ln_unit", lambda t: GT * LN_TURN["ln6"] + t + 1, x_norm, bank(5), "ln6_turned")
                    pe.wait_ge(S["ln6_T"], 1)
                    for t in range(GT):
                        mm = nc.tensor.matmul(bank(6)[:, t * E:(t + 1) * E], xT[:, t * P:(t + 1) * P],
                                              w["gate_w"][:, :], start=True, stop=True)
                    mm.then_inc(S["moe1_logits"], 1)

            @block.scalar
            def _(act):
                def expert(e):
                    if back is not None:
                        expert_scalar(act, S, "moe1", e, ACT.Relu)

                ahead = front is not None
                nc.scalar.preload_act_table_set(LN_AND_EXP)
                if back is not None:
                    weights_scalar(act, S, "moe1")
                if ahead:
                    ln_scalar(act, S, "ln5")
                    lnT_scalar(act, S, "ln5", frontT)
                    act.wait_ge(S["ctx_turned"], 1)
                    nc.scalar.activation(ctxT, bank(6), ACT.Copy).then_inc(S["ctx_T"], 1)
                expert(0)
                if ahead:
                    attend_exp_scalar(act, S, "self")
                expert(1)
                if ahead:
                    attend_turned_scalar(act, S, "self", 6)
                expert(2)
                expert(3)
                if ahead:
                    ln_scalar(act, S, "g1")
                    lnT_scalar(act, S, "g1", frontT, 5)
                expert(4)
                if ahead:
                    attend_exp_scalar(act, S, "cross")
                expert(5)
                if ahead:
                    attend_turned_scalar(act, S, "cross", 7)
                expert(6)
                if ahead:
                    ln_scalar(act, S, "g2")
                expert(7)
                if ahead:
                    lnT_scalar(act, S, "g2", frontT, 6)
                if ahead:
                    for c in range(HC):
                        dense_hidden_scalar(act, S, "hid1", c, (5, 7))
                    dense_sum_scalar(act, S, "hid1", 6)
                    ln_scalar(act, S, "g3")
                if back is not None:
                    experts_sum_scalar(act, S, "moe1")
                if ahead:
                    ln_scalar(act, S, "ln6")
                    lnT_scalar(act, S, "ln6", None, 5)
                    gate_exps_scalar(act, S, "moe1")

            @block.vector
            def _(dve):
                def expert(e):
                    if back is not None:
                        expert_vector(dve, S, "moe1", e)

                ahead = front is not None
                if ahead:
                    nc.vector.tensor_copy(x_front, x_all[:, bass.ds(front * GT, GT), :]).then_inc(S["x_front"], 1)
                    dve.wait_ge(S["x_front"], 1)
                    ln_vector(dve, S, "ln5", x_front, y)
                    dve.wait_ge(S["ln_unit"], GT * (LN_TURN["ln5"] + 1))
                if back is not None:
                    nc.vector.tensor_tensor(result, x_cur[:, :, :], x_norm[:, :, :], ALU.add).then_inc(S["unit_added"], 1)
                expert(0)
                if ahead:
                    attend_shift_vector(dve, S, "self", "causal_mask", 5)
                expert(1)
                if ahead:
                    attend_sum_vector(dve, S, "self")
                expert(2)
                if ahead:
                    attend_out_vector(dve, S, "self", 7)
                    ln_vector(dve, S, "g1", y, y, (w["ln_g1"][:, :], w["ln_b1"][:, :]))
                    dve.wait_ge(S["g1_done"], 1)
                expert(3)
                expert(4)
                if ahead:
                    attend_shift_vector(dve, S, "cross", "block_mask", 6)
                expert(5)
                if ahead:
                    attend_sum_vector(dve, S, "cross")
                    attend_out_vector(dve, S, "cross", 5)
                expert(6)
                if ahead:
                    ln_vector(dve, S, "g2", y, y, (w["ln_g2"][:, :], w["ln_b2"][:, :]))
                    dve.wait_ge(S["g2_done"], 1)
                expert(7)
                if ahead:
                    dve.wait_ge(S["hid1_back"], 1)
                    dve.wait_ge(S["g2_turned"], GT)
                    nc.vector.tensor_tensor(y, y, in_tiles(bank(7)), ALU.add).then_inc(S["hid1_added"], 1)
                    dve.wait_ge(S["hid1_added"], 1)
                    ln_vector(dve, S, "g3", y, y, (w["ln_g3"][:, :], w["ln_b3"][:, :]))
                    dve.wait_ge(S["g3_done"], 1)
                    nc.vector.tensor_tensor(x_cur[:, :, :], x_front, y, ALU.add).then_inc(S["x5"], 1)
                    dve.wait_ge(S["x5"], 1)
                    ln_vector(dve, S, "ln6", x_cur, x_norm)
                if back is not None:
                    dve.wait_ge(S["unit_added"], 1)
                    dve.wait_ge(S["moe1_back"], 1)
                    nc.vector.tensor_tensor(result, result, in_tiles(bank(2)), ALU.add).then_inc(S["result"], 1)
                if ahead:
                    two_choices_vector(dve, S)
        finish_phase(nc, S)

    with ExitStack() as sems:
        S = Signals(nc, sems)
        second_stage(S, 0, None)
        with nc.Fori(0, GROUPS - 1) as g:
            second_stage(S, g + 1, g)
        second_stage(S, None, GROUPS - 1)


_OUTS = [((BATCH, SEQ, C), "float32")]


def kernel(**inputs):
    import numpy as _np
    import concourse.bacc as _bacc
    from concourse import mybir as _mybir
    from concourse.bass_utils import run_bass_kernel_spmd as _run

    nc = _bacc.Bacc("TRN2", target_bir_lowering=False, num_devices=1)
    arrays, args = {}, {}
    for name in inputs:
        a = _np.ascontiguousarray(inputs[name])
        if a.ndim == 0:
            a = a.reshape(1)
        if name == "L0_xattn_tgt_bias":
            a = a.reshape(SEQ, SEQ)
        arrays[f"in_{name}_dram"] = a
        args[name] = nc.dram_tensor(f"in_{name}_dram", a.shape, _mybir.dt.from_np(a.dtype), kind="ExternalInput").ap()
    outs = [nc.dram_tensor(f"out_{i}_dram", shape, _mybir.dt.from_np(_np.dtype(dtype)), kind="ExternalOutput").ap()
            for i, (shape, dtype) in enumerate(_OUTS)]
    build(nc, args, outs[0])
    r = _run(nc, [arrays], core_ids=[0])
    return r.results[0]["out_0_dram"]
```
